# Optimizing a Trainium2 kernel written in Bass

```python
import numpy as np
import jax
import jax.numpy as jnp

def _softmax(x, axis=-1):
    return jax.nn.softmax(x, axis=axis)

def _gelu(x):
    return jax.nn.gelu(x, approximate=True)

def _silu(x):
    return jax.nn.silu(x)

def _sigmoid(x):
    return jax.nn.sigmoid(x)

def _layernorm(x, axis=-1, eps=1e-05):
    m = jnp.mean(x, axis=axis, keepdims=True)
    v = jnp.var(x, axis=axis, keepdims=True)
    return (x - m) / jnp.sqrt(v + eps)

def _scatter_add(tgt, idx, src, axis=0):
    return tgt.at[idx].add(src)

def _segment_sum(src, seg, n):
    return jax.ops.segment_sum(src, seg, n)
kernel_name = 'mk_seq_preln_d2_jaxref_r8_312876'

def setup_inputs(seed: int=0):
    np.random.seed(seed)
    _w = jnp.asarray

    def _L0_attn_setup():
        import jax, jax.numpy as jnp
        import numpy as np
        B, S, D = (4, 256, 128)

        def _gaussian_mask(seq_len, dtype):
            pos = jnp.arange(seq_len, dtype=dtype)
            center = seq_len / 2
            sigma = seq_len / 4
            m = jnp.exp(-0.5 * ((pos - center) / sigma) ** 2)
            return m[None, None, :]
        key = jax.random.key(seed)
        ks = jax.random.split(key, 9)
        sc = 1.0 / np.sqrt(D)
        return {'x': jax.random.normal(ks[0], (B, S, D), dtype=jnp.float32), 'Wq': jax.random.normal(ks[1], (D, D), dtype=jnp.float32) * sc, 'bq': jnp.zeros((D,), dtype=jnp.float32), 'Wk': jax.random.normal(ks[2], (D, D), dtype=jnp.float32) * sc, 'bk': jnp.zeros((D,), dtype=jnp.float32), 'Wv': jax.random.normal(ks[3], (D, D), dtype=jnp.float32) * sc, 'bv': jnp.zeros((D,), dtype=jnp.float32), 'Wo': jax.random.normal(ks[4], (D, D), dtype=jnp.float32) * sc, 'bo': jnp.zeros((D,), dtype=jnp.float32)}
    _L0_attn_in = _L0_attn_setup()

    def _L0_ffn_setup():
        import jax, jax.numpy as jnp
        import numpy as np
        B, S, D, H, E = (8, 256, 128, 512, 16)
        key = jax.random.key(seed)
        ks = jax.random.split(key, 4)
        sd = 1.0 / np.sqrt(D).astype(np.float32)
        sh = 1.0 / np.sqrt(H).astype(np.float32)
        return {'x': jax.random.normal(ks[0], (B, S, D), jnp.float32), 'Wg': jax.random.normal(ks[1], (D, E), jnp.float32) * sd, 'bg': jnp.zeros((E,), jnp.float32), 'W1': jax.random.normal(ks[2], (E, D, H), jnp.float32) * sd, 'b1': jnp.zeros((E, H), jnp.float32), 'W2': jax.random.normal(ks[3], (E, H, D), jnp.float32) * sh, 'b2': jnp.zeros((E, D), jnp.float32)}
    _L0_ffn_in = _L0_ffn_setup()

    def _L1_attn_setup():
        import jax, jax.numpy as jnp
        import numpy as np
        DIM = 128
        key = jax.random.key(seed)
        kx, kw = jax.random.split(key)
        x = jax.random.normal(kx, (4, 256, DIM), dtype=jnp.float32)
        W_qkv = jax.random.normal(kw, (3 * DIM, DIM), dtype=jnp.float32) * DIM ** (-0.5)
        return {'x': x, 'W_qkv': W_qkv}
    _L1_attn_in = _L1_attn_setup()

    def _L1_ffn_setup():
        import jax, jax.numpy as jnp
        import numpy as np
        D_MODEL = 128
        N_HEAD = 16
        HEAD_DIM = D_MODEL // N_HEAD
        D_FF = 512
        N_EXPERTS = 4
        EPS = 1e-05

        def _layer_norm(x, gamma, beta):
            mu = jnp.mean(x, axis=-1, keepdims=True)
            var = jnp.mean((x - mu) ** 2, axis=-1, keepdims=True)
            return (x - mu) / jnp.sqrt(var + EPS) * gamma + beta
        key = jax.random.key(seed)
        ks = jax.random.split(key, 20)
        f32 = jnp.float32
        sc = 1.0 / np.sqrt(D_MODEL)
        scf = 1.0 / np.sqrt(D_FF)
        return {'src': jax.random.normal(ks[0], (4, 64, D_MODEL), f32), 'Wq': jax.random.normal(ks[1], (D_MODEL, D_MODEL), f32) * sc, 'bq': jnp.zeros((D_MODEL,), f32), 'Wk': jax.random.normal(ks[2], (D_MODEL, D_MODEL), f32) * sc, 'bk': jnp.zeros((D_MODEL,), f32), 'Wv': jax.random.normal(ks[3], (D_MODEL, D_MODEL), f32) * sc, 'bv': jnp.zeros((D_MODEL,), f32), 'Wo': jax.random.normal(ks[4], (D_MODEL, D_MODEL), f32) * sc, 'bo': jnp.zeros((D_MODEL,), f32), 'router_w': jax.random.normal(ks[5], (D_MODEL, 1), f32) * 0.05, 'router_b': jnp.zeros((1,), f32), 'W1': jax.random.normal(ks[6], (N_EXPERTS, D_MODEL, D_FF), f32) * sc, 'b1': jnp.zeros((N_EXPERTS, D_FF), f32), 'W2': jax.random.normal(ks[7], (N_EXPERTS, D_FF, D_MODEL), f32) * scf, 'b2': jnp.zeros((N_EXPERTS, D_MODEL), f32), 'ln1_g': jnp.ones((D_MODEL,), f32), 'ln1_b': jnp.zeros((D_MODEL,), f32), 'ln2_g': jnp.ones((D_MODEL,), f32), 'ln2_b': jnp.zeros((D_MODEL,), f32)}
    _L1_ffn_in = _L1_ffn_setup()
    _d = {'L0_attn_x': _L0_attn_in['x'], 'L0_attn_Wq': _L0_attn_in['Wq'], 'L0_attn_bq': _L0_attn_in['bq'], 'L0_attn_Wk': _L0_attn_in['Wk'], 'L0_attn_bk': _L0_attn_in['bk'], 'L0_attn_Wv': _L0_attn_in['Wv'], 'L0_attn_bv': _L0_attn_in['bv'], 'L0_attn_Wo': _L0_attn_in['Wo'], 'L0_attn_bo': _L0_attn_in['bo'], 'L0_ffn_Wg': _L0_ffn_in['Wg'], 'L0_ffn_bg': _L0_ffn_in['bg'], 'L0_ffn_W1': _L0_ffn_in['W1'], 'L0_ffn_b1': _L0_ffn_in['b1'], 'L0_ffn_W2': _L0_ffn_in['W2'], 'L0_ffn_b2': _L0_ffn_in['b2'], 'L1_attn_W_qkv': _L1_attn_in['W_qkv'], 'L1_ffn_Wq': _L1_ffn_in['Wq'], 'L1_ffn_bq': _L1_ffn_in['bq'], 'L1_ffn_Wk': _L1_ffn_in['Wk'], 'L1_ffn_bk': _L1_ffn_in['bk'], 'L1_ffn_Wv': _L1_ffn_in['Wv'], 'L1_ffn_bv': _L1_ffn_in['bv'], 'L1_ffn_Wo': _L1_ffn_in['Wo'], 'L1_ffn_bo': _L1_ffn_in['bo'], 'L1_ffn_router_w': _L1_ffn_in['router_w'], 'L1_ffn_router_b': _L1_ffn_in['router_b'], 'L1_ffn_W1': _L1_ffn_in['W1'], 'L1_ffn_b1': _L1_ffn_in['b1'], 'L1_ffn_W2': _L1_ffn_in['W2'], 'L1_ffn_b2': _L1_ffn_in['b2'], 'L1_ffn_ln1_g': _L1_ffn_in['ln1_g'], 'L1_ffn_ln1_b': _L1_ffn_in['ln1_b'], 'L1_ffn_ln2_g': _L1_ffn_in['ln2_g'], 'L1_ffn_ln2_b': _L1_ffn_in['ln2_b']}
    _x0 = _d['L0_attn_x']
    _d['L0_attn_x'] = jax.random.normal(jax.random.fold_in(jax.random.key(seed), 1), (8, 512, 128), dtype=_x0.dtype)
    del _x0
    return _d

def reference(L0_attn_x, L0_attn_Wq, L0_attn_bq, L0_attn_Wk, L0_attn_bk, L0_attn_Wv, L0_attn_bv, L0_attn_Wo, L0_attn_bo, L0_ffn_Wg, L0_ffn_bg, L0_ffn_W1, L0_ffn_b1, L0_ffn_W2, L0_ffn_b2, L1_attn_W_qkv, L1_ffn_Wq, L1_ffn_bq, L1_ffn_Wk, L1_ffn_bk, L1_ffn_Wv, L1_ffn_bv, L1_ffn_Wo, L1_ffn_bo, L1_ffn_router_w, L1_ffn_router_b, L1_ffn_W1, L1_ffn_b1, L1_ffn_W2, L1_ffn_b2, L1_ffn_ln1_g, L1_ffn_ln1_b, L1_ffn_ln2_g, L1_ffn_ln2_b):

    def _L0_attn_ref(x, Wq, bq, Wk, bk, Wv, bv, Wo, bo):
        import jax, jax.numpy as jnp
        import numpy as np
        B, S, D = (4, 256, 128)

        def _gaussian_mask(seq_len, dtype):
            pos = jnp.arange(seq_len, dtype=dtype)
            center = seq_len / 2
            sigma = seq_len / 4
            m = jnp.exp(-0.5 * ((pos - center) / sigma) ** 2)
            return m[None, None, :]
        d = x.shape[-1]
        Q = x @ Wq.T + bq
        K = x @ Wk.T + bk
        V = x @ Wv.T + bv
        scores = jnp.einsum('bqd,bkd->bqk', Q, K) / jnp.sqrt(jnp.asarray(d, x.dtype))
        scores = scores * _gaussian_mask(x.shape[1], x.dtype)
        attn = jax.nn.softmax(scores, axis=-1)
        out = jnp.einsum('bqk,bkd->bqd', attn, V)
        return out @ Wo.T + bo

    def _L0_ffn_ref(x, Wg, bg, W1, b1, W2, b2):
        import jax, jax.numpy as jnp
        import numpy as np
        B, S, D, H, E = (8, 256, 128, 512, 16)
        d = x.shape[-1]
        xf = x.reshape(-1, d)
        n_tok = xf.shape[0]
        n_exp = Wg.shape[1]
        cap = -(-n_tok // n_exp)
        score = jax.nn.softmax(xf @ Wg + bg, axis=-1)
        gate = jnp.max(score, axis=-1)
        idx = jnp.argmax(score, axis=-1)
        onehot = jax.nn.one_hot(idx, n_exp, dtype=jnp.int32)
        pos = jnp.sum((jnp.cumsum(onehot, axis=0) - 1) * onehot, axis=-1)
        keep = pos < cap
        safe_pos = jnp.where(keep, pos, cap - 1)
        buf = jnp.zeros((n_exp, cap, d), x.dtype).at[idx, safe_pos].add(jnp.where(keep[:, None], xf, 0.0))
        h = jax.nn.relu(jnp.einsum('ecd,edh->ech', buf, W1) + b1[:, None, :])
        y = jnp.einsum('ech,ehd->ecd', h, W2) + b2[:, None, :]
        out = y[idx, safe_pos] * gate[:, None]
        out = jnp.where(keep[:, None], out, 0.0)
        return out.reshape(x.shape)

    def _L1_attn_ref(x, W_qkv):
        import jax, jax.numpy as jnp
        import numpy as np
        DIM = 128
        qkv = jnp.einsum('bnd,ed->bne', x, W_qkv)
        B, N, _ = qkv.shape
        qkv = qkv.reshape(B, N, 3, DIM).transpose(2, 0, 1, 3)
        q, k, v = (qkv[0], qkv[1], qkv[2])
        scale = DIM ** (-0.5)
        attn = jnp.einsum('bnd,bmd->bnm', q * scale, k)
        attn = jax.nn.softmax(attn, axis=-1)
        out = jnp.einsum('bnm,bmd->bnd', attn, v)
        return out

    def _L1_ffn_ref(src, Wq, bq, Wk, bk, Wv, bv, Wo, bo, router_w, router_b, W1, b1, W2, b2, ln1_g, ln1_b, ln2_g, ln2_b):
        import jax, jax.numpy as jnp
        import numpy as np
        D_MODEL = 128
        N_HEAD = 16
        HEAD_DIM = D_MODEL // N_HEAD
        D_FF = 512
        N_EXPERTS = 4
        EPS = 1e-05

        def _layer_norm(x, gamma, beta):
            mu = jnp.mean(x, axis=-1, keepdims=True)
            var = jnp.mean((x - mu) ** 2, axis=-1, keepdims=True)
            return (x - mu) / jnp.sqrt(var + EPS) * gamma + beta
        B, T, _ = src.shape
        q = (src @ Wq + bq).reshape(B, T, N_HEAD, HEAD_DIM)
        k = (src @ Wk + bk).reshape(B, T, N_HEAD, HEAD_DIM)
        v = (src @ Wv + bv).reshape(B, T, N_HEAD, HEAD_DIM)
        scale = HEAD_DIM ** (-0.5)
        scores = jnp.einsum('bqhd,bkhd->bhqk', q, k) * scale
        probs = jax.nn.softmax(scores, axis=-1)
        attn = jnp.einsum('bhqk,bkhd->bqhd', probs, v).reshape(B, T, D_MODEL)
        attn = attn @ Wo + bo
        x = _layer_norm(src + attn, ln1_g, ln1_b)
        keys = (x @ router_w + router_b)[..., 0]
        expert_idx = jnp.remainder(jnp.floor(keys).astype(jnp.int32), N_EXPERTS)
        ff_out = jnp.zeros_like(x)
        for e in range(N_EXPERTS):
            h = jax.nn.relu(x @ W1[e] + b1[e])
            y = h @ W2[e] + b2[e]
            ff_out = ff_out + jnp.where((expert_idx == e)[..., None], y, 0.0)
        return _layer_norm(x + ff_out, ln2_g, ln2_b)
    x = L0_attn_x
    x = x + _L0_attn_ref(_layernorm(x, axis=-1), L0_attn_Wq, L0_attn_bq, L0_attn_Wk, L0_attn_bk, L0_attn_Wv, L0_attn_bv, L0_attn_Wo, L0_attn_bo)
    x = x + _L0_ffn_ref(_layernorm(x, axis=-1), L0_ffn_Wg, L0_ffn_bg, L0_ffn_W1, L0_ffn_b1, L0_ffn_W2, L0_ffn_b2)
    x = x + _L1_attn_ref(_layernorm(x, axis=-1), L1_attn_W_qkv)
    x = x + _L1_ffn_ref(_layernorm(x, axis=-1), L1_ffn_Wq, L1_ffn_bq, L1_ffn_Wk, L1_ffn_bk, L1_ffn_Wv, L1_ffn_bv, L1_ffn_Wo, L1_ffn_bo, L1_ffn_router_w, L1_ffn_router_b, L1_ffn_W1, L1_ffn_b1, L1_ffn_W2, L1_ffn_b2, L1_ffn_ln1_g, L1_ffn_ln1_b, L1_ffn_ln2_g, L1_ffn_ln2_b)
    return x

_drawn_inputs = setup_inputs


def setup_inputs(seed=0):
    import zlib

    import numpy as np

    out = dict(_drawn_inputs(seed))
    spreads = {'L0_attn_bq': (0.0, 0.1),
     'L0_attn_bk': (0.0, 0.696),
     'L0_attn_bv': (0.0, 0.1),
     'L0_attn_bo': (0.0, 0.1),
     'L0_ffn_bg': (0.0, 0.1),
     'L0_ffn_b1': (0.0, 0.1),
     'L0_ffn_b2': (0.0, 0.1),
     'L1_ffn_bq': (0.0, 0.394),
     'L1_ffn_bk': (0.0, 0.8),
     'L1_ffn_bv': (0.0, 0.1),
     'L1_ffn_bo': (0.0, 0.1),
     'L1_ffn_b1': (0.0, 0.1),
     'L1_ffn_b2': (0.0, 0.1),
     'L1_ffn_ln1_g': (1.0, 0.2),
     'L1_ffn_ln1_b': (0.0, 0.1),
     'L1_ffn_ln2_g': (1.0, 0.2),
     'L1_ffn_ln2_b': (0.0, 0.1)}
    factors = {}
    for name, (base, spread) in spreads.items():
        noise = np.random.default_rng([zlib.crc32(name.encode()), seed]).standard_normal(out[name].shape)
        drawn = base * np.exp(spread * noise) if base else spread * noise
        out[name] = jnp.asarray(drawn.astype(out[name].dtype))
    for name, factor in factors.items():
        out[name] = (out[name] * factor).astype(out[name].dtype)
    return out
```

```python
from contextlib import ExitStack

import concourse.bass as bass
from concourse import mybir

ALU = mybir.AluOpType
ACT = mybir.ActivationFunctionType
AX = mybir.AxisListType.X
F32 = mybir.dt.float32
F16 = mybir.dt.float16
I32 = mybir.dt.int32
ds = bass.ds

P = 128
B = 8
S = 512
D = 128
N = B * S
T = S // P
NT = N // P
H = 512
HC = H // P
E0 = 16
CAP = N // E0
E1 = 4
PAIR = 2 * P
U0 = N // PAIR
U1 = 20
PAD = 8192
NH = 16
DH = D // NH
G = 4
EPS = 1e-5
SCALE_H = float(DH) ** -0.5
ROW = 2 * D
WP = H + HC * D + HC + D

WCOL = {}
at = 0
for name, width in (("q0", D), ("k0", D), ("v0", D), ("o0", D), ("g0", E0), ("q1", D), ("k1", D), ("v1", D),
                    ("qh", D), ("kh", D), ("vh", D), ("oh", D), ("ident", D), ("gauss", S), ("bq0", 1), ("bk0", 1),
                    ("bqh", 1), ("bkh", 1), ("one24", 1)):
    WCOL[name] = (at, at + width)
    at += width
WTOT = at
RCOL = {}
at = 0
for name, width in (("bv0", D), ("bo0", D), ("bg0", T * E0), ("rev0", E0), ("bvh", D), ("boh", D), ("g1", D), ("b1", D),
                    ("g2", D), ("b2", D), ("rw", D), ("rb", 1), ("iota", P), ("tile", NT), ("place", 1)):
    RCOL[name] = (at, at + width)
    at += width
RTOT = at
CCOL = {"ident": 0, "tri": D, "ones": 2 * D, "qA": 3 * D, "qB": 7 * D, "kA": 11 * D, "kB": 15 * D}
CTOT = 19 * D + 4


def build(nc, x_in, w_in, r_in, c_in, pack0_in, pack1_in, out):
    table0 = nc.dram_tensor("table0", (N, ROW), F32).ap()
    x2d = nc.dram_tensor("x_after_experts0", (N, D), F32).ap()
    table1 = nc.dram_tensor("table1", (N, ROW), F32).ap()

    ctx = ExitStack()
    with ctx:
        def sb(name, shape, dt=F32):
            return ctx.enter_context(nc.sbuf_tensor(name, shape, dt))

        def sem(name):
            return ctx.enter_context(nc.semaphore(name))

        psum = ctx.enter_context(nc.psum_tensor("psum", [P, 8 * 512], F32))
        bank = [psum[:, i * 512:(i + 1) * 512] for i in range(8)]

        w_all = sb("w_all", [P, WTOT])
        r_all = sb("r_all", [P, RTOT])
        c_all = sb("c_all", [P, CTOT], F16)
        x_all = sb("x_all", [P, NT * D])
        s_all = sb("s_all", [P, NT * D])
        stats3 = sb("stats3", [P, NT, 6])
        mv_all = sb("mv_all", [P, NT, 2])
        var_all = sb("var_all", [P, NT])
        rstd_all = sb("rstd_all", [P, NT])
        neg_half = sb("neg_half", [P, NT])
        eps = sb("eps", [P, NT])

        def W(name):
            return w_all[:, WCOL[name][0]:WCOL[name][1]]

        def R(name):
            return r_all[:, RCOL[name][0]:RCOL[name][1]]

        def C(name, n=0):
            return c_all[:, CCOL[name] + n * D:CCOL[name] + (n + 1) * D]

        def xt(i, of=x_all):
            return of[:, ds(i * D, D)]

        def x4(i, of=x_all):
            return of[:, ds(i * T * D, T * D)].rearrange("p (t d) -> p t d", t=T)

        def bank3(i, a, b):
            return bank[i][:, 0:a * b].rearrange("p (a b) -> p a b", a=a)

        def bcast(ap, n):
            return ap.unsqueeze(2).broadcast_to([P, ap.shape[1], n])

        stats = sb("stats", [P, T, 6])
        stats2 = sb("stats2", [P, T, 6])
        mv = sb("mv", [P, T, 2])
        mv2 = sb("mv2", [P, T, 2])
        var_eps = sb("var_eps", [P, T])
        rstd = sb("rstd", [P, T])
        xn = sb("xn", [P, T, D])
        xnT = sb("xnT", [P, S])
        qT = sb("qT", [P, S])
        kT = sb("kT", [P, S])
        vv = sb("vv", [P, T, D])
        pr = sb("pr", [P, 2, S])
        prT = sb("prT", [P, 2, S])
        oT = sb("oT", [P, 2, D])
        nmax = sb("nmax", [P, T])
        rsum = sb("rsum", [P, T])
        rinv = sb("rinv", [P, T])
        xg = sb("xg", [P, 2, T, D])
        xgT = sb("xgT", [P, 2, S])
        lg = sb("lg", [P, NT, E0])
        wide = [sb(f"wide{i}", [P, NT, E0]) for i in range(4)]
        oh = sb("oh", [P, NT, E0], F16)
        one = {n: sb("r_" + n, [P, NT]) for n in
               ("lmax", "lsum", "gate", "rest", "rest2", "best", "pos", "late", "p16", "col", "key", "keyf", "gt", "floor",
                "ef", "base", "jf", "pf")}
        oni = {n: sb("ri_" + n, [P, NT], I32) for n in ("key", "floor", "e", "pos", "p", "j")}
        gpiece = sb("gpiece", [P, 3, NT], F16)
        ptm_mem = sb("ptm", [P, 4 * 2 * S])
        otm_mem = sb("otm", [P, G * S])
        ptm = ptm_mem[:, :].rearrange("p (r n) -> p r n", r=4)
        otm = otm_mem[:, :].rearrange("p (g n) -> p g n", g=G)
        at_place = otm_mem[:, :].bitcast(F16).rearrange("p (t n) -> p t n", t=NT)
        at_col = ptm_mem[:, 0:NT * 5 * U1].bitcast(F16).rearrange("p (t k n) -> p t k n", t=NT, k=5)
        vals = sb("vals", [P, 5, 2 * U1])
        padm = sb("padm", [P, 2 * U1])
        idf = sb("idf", [P, 2 * U1])
        gslot = sb("gslot", [P, 2 * U1])
        gsum = sb("gsum", [P, 2 * U1])
        tot = sb("tot", [P, E1])
        toti = sb("toti", [P, E1], I32)
        pairs = sb("pairs", [P, E1])
        ends = sb("ends", [P, E1])
        starts = sb("starts", [P, E1])
        which = sb("which", [P, 3, U1])
        esum = sb("esum", [P, U1])
        e_of = sb("e_of", [P, U1], I32)
        ids_all = sb("ids_all", [P, 2 * U1], I32)
        raw = sb("raw", [P, 2, 2, 2], I32)
        zero_i = sb("zero_i", [P, 2, 2], I32)
        ids = sb("ids", [P, 2, 2, 2], I32)
        wx = sb("wx", [P, 2, WP])
        rg = sb("rg", [P, 2, 2, ROW])
        exT = sb("exT", [P, 2, PAIR])
        hT = sb("hT", [P, 2, HC, PAIR])
        yb = sb("yb", [P, 2, 2, D])
        yo = sb("yo", [P, 2, 2, D])
        yr = sb("yr", [P, 2, 2, D])
        yn = sb("yn", [P, 2, 2, D])
        bx = sb("bx", [P, 2, 2, D])
        st1 = sb("st1", [P, 2, 6])
        mv1 = sb("mv1", [P, 2, 2])
        ve1 = sb("ve1", [P, 2])
        rs1 = sb("rs1", [P, 2])
        qhi = sb("qhi", [P, S], F16)
        qlo = sb("qlo", [P, S], F16)
        khi = sb("khi", [P, S], F16)
        klo = sb("klo", [P, S], F16)
        kst = sb("kst", [P, S], F16)
        kpad = sb("kpad", [P, G, 4, S], F16)
        qs1 = sb("qs1", [P, G, S], F16)
        qs2 = sb("qs2", [P, G, S], F16)
        mrow = sb("mrow", [P, 2, T, P], F16)
        vh = sb("vh", [P, T, NH, 32])
        rch = sb("rch", [P, NH])
        ath = sb("ath", [P, T, D])
        atT = sb("atT", [P, D])

        class Signals(dict):
            def __init__(self, phase):
                self.phase = phase

            def __missing__(self, name):
                self[name] = sem(f"{self.phase}_{name}")
                return self[name]

        READY = 8
        consts = sem("consts_loaded")
        ready = sem("constants_set")
        outs = sem("outs_stored")

        def apart(eng, value):
            value = value if isinstance(value, int) else eng.snap(value)
            eng.wait_ge(ready, READY)
            return value

        def steps(eng, n, body):
            with eng.Fori(0, n - 1) as i:
                body(i, False)
            body(n - 1, True)

        def steps3(eng, n, body):
            body(0, True, False)
            with eng.Fori(1, n - 1) as i:
                body(i, False, False)
            body(n - 1, False, True)

        A = Signals("attn0")
        C1 = Signals("attn1")

        def ln_stats(v, s, it):
            for t in range(T):
                ins = nc.vector.bn_stats(stats[:, t, :], xt(it * T + t))
            ins.then_inc(s["bn"], 1)
            v.wait_ge(s["bn"], apart(v, it + 1))
            for t in range(T):
                ins = nc.vector.bn_aggr(mv[:, t, :], stats[:, t, :])
            ins.then_inc(s["stats"], 1)

        def ln_rstd(p, s, it):
            p.wait_ge(s["stats"], it + 1)
            nc.gpsimd.tensor_tensor(var_eps[:, :], mv[:, :, 1], eps[:, 0:T], ALU.add).then_inc(s["eps"], 1)
            p.wait_ge(s["eps"], it + 1)
            nc.gpsimd.tensor_tensor(rstd[:, :], var_eps[:, :], neg_half[:, 0:T], ALU.pow).then_inc(s["rstd"], 1)

        def rstd_of_all(p, s):
            p.wait_ge(s["mv_all"], B)
            nc.gpsimd.tensor_tensor(var_all[:, :], mv_all[:, :, 1], eps[:, :], ALU.add).then_inc(s["eps"], 1)
            p.wait_ge(s["eps"], B + 1)
            nc.gpsimd.tensor_tensor(rstd_all[:, :], var_all[:, :], neg_half[:, :], ALU.pow).then_inc(s["rstd"], 1)

        def apply_all(i, t, dst):
            return nc.vector.tensor_scalar(dst, xt(i * T + t),
                                           mv_all[:, ds(i * T + t, 1), 0:1].rearrange("p o c -> p (o c)"),
                                           rstd_all[:, ds(i * T + t, 1)], ALU.subtract, ALU.mult)

        def ln_apply(v, s, it, dst):
            v.wait_ge(s["rstd"], it + 1)
            for t in range(T):
                ins = nc.vector.tensor_scalar(dst(t), xt(it * T + t), mv[:, t, 0:1], rstd[:, t:t + 1],
                                              ALU.subtract, ALU.mult)
            ins.then_inc(s["xn"], 1)

        def attn_pe(pe, s, wq, wk, wv, wo):
            def transposes(it):
                pe.wait_ge(s["xn"], it + 1)
                for t in range(T):
                    ins = nc.tensor.transpose(bank[0][:, t * P:(t + 1) * P], xn[:, t, :], W("ident"))
                ins.then_inc(s["xT_ps"], 1)

            def qk(it):
                pe.wait_ge(s["xT"], it + 1)
                nc.tensor.matmul(bank[1][:, :], wq, xnT[:, :], start=True, stop=True).then_inc(s["q_ps"], 1)
                if wo is not None:
                    pe.wait_ge(s["ot"], it * T)
                nc.tensor.matmul(bank[2][:, :], wk, xnT[:, :], start=True, stop=True).then_inc(s["k_ps"], 1)

            def values(it):
                for t in range(T):
                    ins = nc.tensor.matmul(bank[3][:, t * D:(t + 1) * D], xnT[:, t * P:(t + 1) * P], wv,
                                           start=True, stop=True)
                ins.then_inc(s["v_ps"], 1)

            def scores(it, t):
                if t == 0:
                    pe.wait_ge(s["q"], it + 1)
                    pe.wait_ge(s["k"], it + 1)
                if t >= 2:
                    pe.wait_ge(s["p"], it * T + t - 1)
                nc.tensor.matmul(bank[4 + t % 2][:, :], qT[:, t * P:(t + 1) * P], kT[:, :],
                                 start=True, stop=True).then_inc(s["s_ps"], 1)

            def turn(it, t):
                pe.wait_ge(s["p"], it * T + t + 1)
                if t >= 2:
                    pe.wait_ge(s["pt"], it * T + t - 1)
                for c in range(T):
                    ins = nc.tensor.transpose(bank[6 + t % 2][:, c * P:(c + 1) * P],
                                              pr[:, t % 2, c * P:(c + 1) * P], W("ident"))
                ins.then_inc(s["pt_ps"], 1)

            def mix(it, t):
                pe.wait_ge(s["pt"], it * T + t + 1)
                if t == 0:
                    pe.wait_ge(s["v"], it + 1)
                if t >= 2:
                    pe.wait_ge(s["ot"], it * T + t - 1)
                for c in range(T):
                    ins = nc.tensor.matmul(bank[1 + t % 2][:, 0:P], vv[:, c, :], prT[:, t % 2, c * P:(c + 1) * P],
                                           start=(c == 0), stop=(c == T - 1))
                ins.then_inc(s["ot_ps"], 1)

            def z_bank(it, t):
                if t == 1:
                    pe.wait_ge(s["x_out"], it * T + 1)
                if t == 3:
                    pe.wait_ge(s["x_out"], it * T + 2)
                if t == 2:
                    pe.wait_ge(s["x_out"], it * T + 1)
                return bank[0 if t % 2 else 3][:, 0:D]

            def project(it, t):
                pe.wait_ge(s["ot"], it * T + t + 1)
                nc.tensor.matmul(z_bank(it, t), oT[:, t % 2, :], wo, start=True, stop=True).then_inc(s["z_ps"], 1)

            def mix_rows(it, t):
                pe.wait_ge(s["pt"], it * T + t + 1)
                if t == 0:
                    pe.wait_ge(s["v"], it + 1)
                z = z_bank(it, t)
                for c in range(T):
                    ins = nc.tensor.matmul(z, prT[:, t % 2, c * P:(c + 1) * P], vv[:, c, :],
                                           start=(c == 0), stop=(c == T - 1))
                ins.then_inc(s["z_ps"], 1)

            lag = 3 if wo is not None else 2

            def body(it, last):
                for k in range(T + 3):
                    if k < T:
                        scores(it, k)
                    if 0 <= k - 1 < T:
                        turn(it, k - 1)
                    if 0 <= k - 2 < T:
                        if wo is not None:
                            mix(it, k - 2)
                        else:
                            if k - 2 == 3 and not last:
                                pe.wait_ge(s["xT"], it + 2)
                            mix_rows(it, k - 2)
                    if wo is not None and 0 <= k - 3 < T:
                        if k - 3 == 3 and not last:
                            pe.wait_ge(s["xT"], it + 2)
                        project(it, k - 3)
                    if k == T and not last:
                        pe.wait_ge(s["x_out"], it * T + 2)
                        transposes(it + 1)
                    if k == T + 1 and not last:
                        if wo is not None:
                            pe.wait_ge(s["ot"], it * T + 3)
                        qk(it + 1)
                if not last:
                    pe.wait_ge(s["x_out"], it * T + 3)
                    values(it + 1)

            pe.wait_ge(consts, 48)
            transposes(0)
            pe.wait_ge(s["xT"], 1)
            nc.tensor.matmul(bank[1][:, :], wq, xnT[:, :], start=True, stop=True).then_inc(s["q_ps"], 1)
            nc.tensor.matmul(bank[2][:, :], wk, xnT[:, :], start=True, stop=True).then_inc(s["k_ps"], 1)
            values(0)
            steps(pe, B, body)

        def attn_act(act, s, bq, o):
            def x_copy(it, first=False):
                act.wait_ge(s["xT_ps"], it + 1)
                if not first:
                    act.wait_ge(s["v_ps"], it)
                nc.scalar.copy(xnT[:, :], bank[0][:, :]).then_inc(s["xT"], 1)

            def q_copy(it):
                act.wait_ge(s["q_ps"], it + 1)
                nc.scalar.activation(qT[:, :], bank[1][:, :], ACT.Identity, bias=bq if bq is not None else 0.0
                                     ).then_inc(s["q"], 1)

            def body(it, last):
                for k in range(T + 3):
                    if k < T:
                        act.wait_ge(s["nmax"], it * T + k + 1)
                        if k >= 2:
                            act.wait_ge(s["pt_ps"], it * T + k - 1)
                        nc.scalar.activation(pr[:, k % 2, :], bank[4 + k % 2][:, :], ACT.Exp, bias=nmax[:, k:k + 1],
                                             accum_out=rsum[:, k:k + 1]).then_inc(s["p"], 1)
                    if 0 <= k - 1 < T:
                        t = k - 1
                        act.wait_ge(s["pt_ps"], it * T + t + 1)
                        if t >= 2:
                            act.wait_ge(s["ot_ps" if o else "z_ps"], it * T + t - 1)
                        nc.scalar.copy(prT[:, t % 2, :], bank[6 + t % 2][:, :]).then_inc(s["pt"], 1)
                    if o and 0 <= k - 2 < T:
                        t = k - 2
                        act.wait_ge(s["ot_ps"], it * T + t + 1)
                        if t >= 2:
                            act.wait_ge(s["z_ps"], it * T + t - 1)
                        nc.scalar.copy(oT[:, t % 2, :], bank[1 + t % 2][:, 0:P]).then_inc(s["ot"], 1)
                    if k == T and not last:
                        x_copy(it + 1)
                    if k == T + 1 and not last:
                        q_copy(it + 1)

            act.wait_ge(consts, 48)
            x_copy(0, True)
            q_copy(0)
            steps(act, B, body)

        def attn_dve(v, s, bk, bv, mask, o):
            def k_copy(it):
                v.wait_ge(s["k_ps"], it + 1)
                if mask is not None:
                    nc.vector.scalar_tensor_tensor(out=kT[:, :], in0=bank[2][:, :], scalar=bk, in1=mask,
                                                   op0=ALU.add, op1=ALU.mult).then_inc(s["k"], 1)
                else:
                    nc.vector.tensor_scalar(kT[:, :], bank[2][:, :], float(D) ** -0.5, None,
                                            ALU.mult).then_inc(s["k"], 1)

            def v_copy(it):
                v.wait_ge(s["v_ps"], it + 1)
                if bv is not None:
                    nc.vector.tensor_tensor(vv[:, :, :], bank3(3, T, D), bv.unsqueeze(1).broadcast_to([P, T, D]),
                                            ALU.add).then_inc(s["v"], 1)
                else:
                    nc.vector.tensor_copy(vv[:, :, :], bank3(3, T, D)).then_inc(s["v"], 1)

            def final(it, t):
                if t == 0:
                    if o:
                        v.wait_ge(s["xb"], it + 1)
                    v.wait_ge(s["p"], (it + 1) * T)
                    nc.vector.reciprocal(rinv[:, :], rsum[:, :]).then_inc(s["rinv"], 1)
                    v.wait_ge(s["rinv"], it + 1)
                v.wait_ge(s["z_ps"], it * T + t + 1)
                nc.vector.scalar_tensor_tensor(out=xt(it * T + t), in0=bank[0 if t % 2 else 3][:, 0:D],
                                               scalar=rinv[:, t:t + 1], in1=xt(it * T + t),
                                               op0=ALU.mult, op1=ALU.add).then_inc(s["x_out"], 1)

            def body(it, last):
                for k in range(T + 3):
                    if k < T:
                        v.wait_ge(s["s_ps"], it * T + k + 1)
                        nc.vector.tensor_reduce(nmax[:, k:k + 1], bank[4 + k % 2][:, :], AX, ALU.max,
                                                negate=True).then_inc(s["nmax"], 1)
                    if k == 1 and not last:
                        v.wait_ge(s["x_loaded"], apart(v, 16 * (it + 2)))
                        ln_stats(v, s, it + 1)
                    if k == T - 1 and not last:
                        v.wait_ge(s["xT_ps"], it + 1)
                        ln_apply(v, s, it + 1, lambda t: xn[:, t, :])
                    first = 3 if o else 2
                    if k - first in range(T) and k >= T - 1 or (not o and k == T - 1):
                        if not o and k == T - 1:
                            final(it, 0)
                            final(it, 1)
                        else:
                            final(it, k - first)
                    if k == T + 1 and not last:
                        k_copy(it + 1)
                v.wait_ge(s["x_out"], apart(v, (it + 1) * T))
                for t in range(T):
                    ins = nc.vector.bn_stats(stats2[:, t, :], xt(it * T + t))
                ins.then_inc(s["bn2"], 1)
                v.wait_ge(s["bn2"], apart(v, it + 1))
                for t in range(T):
                    ins = nc.vector.bn_aggr(mv2[:, t, :], stats2[:, t, :])
                ins.then_inc(s["mv2"], 1)
                v.wait_ge(s["mv2"], it + 1)
                nc.vector.tensor_copy(mv_all[:, ds(it * T, T), :], mv2[:, :, :]).then_inc(s["mv_all"], 1)
                if not last:
                    if o:
                        v.wait_ge(s["ot_ps"], (it + 1) * T)
                    v_copy(it + 1)

            v.wait_ge(s["x_loaded"], 16)
            ln_stats(v, s, 0)
            ln_apply(v, s, 0, lambda t: xn[:, t, :])
            v.wait_ge(consts, 48)
            k_copy(0)
            v_copy(0)
            steps(v, B, body)

        def attn_pool(p, s, bo):
            def body(it, last):
                ln_rstd(p, s, it)
                if bo is not None:
                    p.wait_ge(s["xn"], it + 1)
                    nc.gpsimd.tensor_tensor(x4(it), x4(it), bo.unsqueeze(1).broadcast_to([P, T, D]), ALU.add
                                            ).then_inc(s["xb"], 1)
            steps(p, B, body)

        def attn_sp(sp, s, src):
            def body(it, first, last):
                if not first:
                    sp.wait_ge(s["x_loaded"], 16 * it)
                sp.dma_start(x4(it), src[ds(it * S, S), :].rearrange("(t p) d -> p t d", p=P)
                             ).then_inc(s["x_loaded"], 16)
            steps3(sp, B, body)

        GL = Signals("gate0")

        def gate_dve(v, s):
            v.wait_ge(A["rstd"], B + 1)

            def body(i, first, last):
                for slot in range(2):
                    u = 2 * i + slot
                    if not first:
                        v.wait_ge(s[f"rows{slot}"], 16 * i)
                        v.wait_ge(s["xT_ps"], u - 1)
                    for t in range(T):
                        ins = apply_all(u, t, xg[:, slot, t, :])
                    ins.then_inc(s["xn"], 1)
                for slot in range(2):
                    u = 2 * i + slot
                    v.wait_ge(s["lg_ps"], u + 1)
                    nc.vector.tensor_tensor(lg[:, ds(u * T, T), :], bank3(4 * slot + 1, T, E0),
                                            R("bg0").rearrange("p (t e) -> p t e", t=T), ALU.add).then_inc(s["lg"], 1)
            steps3(v, B // 2, body)

        def gate_pe(pe, s):
            def body(i, first, last):
                for slot in range(2):
                    u = 2 * i + slot
                    pe.wait_ge(s["xn"], u + 1)
                    if not first:
                        pe.wait_ge(s["xT"], u - 1)
                    for t in range(T):
                        ins = nc.tensor.transpose(bank[4 * slot][:, t * P:(t + 1) * P], xg[:, slot, t, :], W("ident"))
                    ins.then_inc(s["xT_ps"], 1)
                for slot in range(2):
                    u = 2 * i + slot
                    pe.wait_ge(s["xT"], u + 1)
                    if not first:
                        pe.wait_ge(s["lg"], u - 1)
                    for t in range(T):
                        ins = nc.tensor.matmul(bank[4 * slot + 1][:, t * E0:(t + 1) * E0], xgT[:, slot, t * P:(t + 1) * P],
                                               W("g0"), start=True, stop=True)
                    ins.then_inc(s["lg_ps"], 1)
            steps3(pe, B // 2, body)

        def gate_act(act, s):
            def body(i, first, last):
                for slot in range(2):
                    u = 2 * i + slot
                    act.wait_ge(s["xT_ps"], u + 1)
                    if not first:
                        act.wait_ge(s["lg_ps"], u - 1)
                    nc.scalar.copy(xgT[:, slot, :], bank[4 * slot][:, :]).then_inc(s["xT"], 1)
            steps3(act, B // 2, body)

        def gate_sp(sp, s):
            def body(it, last):
                sp.wait_ge(A["x_out"], T * (it + 1))
                sp.dma_start(x2d[ds(it * S, S), :].rearrange("(t p) d -> p t d", p=P), x4(it)).then_inc(s["x2"], 16)
                sp.dma_start(table0[ds(it * S, S), D:2 * D].rearrange("(t p) d -> p t d", p=P), x4(it)
                             ).then_inc(s["x2"], 16)
            steps(sp, B, body)

            def rows(i, last):
                for slot in range(2):
                    u = 2 * i + slot
                    sp.wait_ge(s["xn"], u + 1)
                    sp.dma_start(table0[ds(u * S, S), 0:D].rearrange("(t p) d -> p t d", p=P), xg[:, slot, :, :]
                                 ).then_inc(s[f"rows{slot}"], 16)
            steps(sp, B // 2, rows)

        class Line:
            def __init__(self, eng, s):
                self.eng, self.s, self.n = eng, s, 0

            def __call__(self, ins):
                self.n += 1
                ins.then_inc(self.s, 1)
                self.eng.wait_ge(self.s, self.n)

        RT0 = Signals("route0")
        RT1 = Signals("route1")

        def places(v, s, then, e, pos_out):
            v.wait_ge(s["cnt_ps"], 1)
            a, b = wide[0][:, :, 0:e], wide[1][:, :, 0:e]
            then(nc.vector.tensor_copy(a, bank3(1, NT, e)))
            step = 1
            while step < NT:
                nc.vector.tensor_copy(b[:, 0:step, :], a[:, 0:step, :])
                then(nc.vector.tensor_tensor(b[:, step:, :], a[:, step:, :], a[:, 0:NT - step, :], ALU.add))
                a, b = b, a
                step *= 2
            c, d = wide[2][:, :, 0:e], wide[3][:, :, 0:e]
            nc.vector.tensor_copy(c[:, 0:1, :], bank3(0, NT, e)[:, 0:1, :])
            then(nc.vector.tensor_tensor(c[:, 1:, :], bank3(0, NT, e)[:, 1:, :], a[:, 0:NT - 1, :], ALU.add))
            then(nc.vector.tensor_tensor(d, c, oh[:, :, 0:e], ALU.mult))
            then(nc.vector.tensor_reduce(pos_out, d, AX, ALU.add))
            return a

        def slots(v, s, then, cols, n_vals):
            iota = R("iota")
            for c in range(4):
                part = slice(c * NT // 4, (c + 1) * NT // 4)
                nc.vector.tensor_tensor(at_place[:, part, :], iota.unsqueeze(1).broadcast_to([P, NT // 4, P]),
                                        bcast(one["p16"][:, part], P), ALU.is_equal).then_inc(s["a"], 1)
            w = at_place[:, 0, :]
            first = at_col[:, :, 0, 0:cols]
            hot = at_col[:, :, 1, 0:cols]
            then(nc.vector.tensor_tensor(hot, iota[:, 0:cols].unsqueeze(1).broadcast_to([P, NT, cols]),
                                         bcast(one["col"][:, :], cols), ALU.is_equal))
            nc.vector.tensor_tensor(first, hot, bcast(R("tile"), cols), ALU.mult)
            for k in range(3 if n_vals == 5 else 0):
                nc.vector.tensor_tensor(at_col[:, :, 2 + k, 0:cols], hot, bcast(gpiece[:, k, :], cols), ALU.mult)
            nc.vector.tensor_scalar(hot, hot, R("place"), None, ALU.mult).then_inc(s["b"], 1)

        def slots_pe(pe, s, cols, n_vals):
            pe.wait_ge(s["b"], 1)
            dst = bank[2][:, 0:n_vals * cols].rearrange("p (n c) -> p n c", n=n_vals)
            for t in range(NT):
                if t % (NT // 4) == 0:
                    pe.wait_ge(s["a"], t // (NT // 4) + 1)
                ins = nc.tensor.matmul(dst, at_place[:, t, :], at_col[:, t, 0:n_vals, 0:cols],
                                       start=(t == 0), stop=(t == NT - 1))
            ins.then_inc(s["ids_ps"], 1)

        def counts_pe(pe, s, e):
            pe.wait_ge(s["oh"], 1)
            nc.tensor.matmul(bank3(0, NT, e), C("tri"), oh[:, :, 0:e], start=True, stop=True)
            nc.tensor.matmul(bank3(1, NT, e), C("ones"), oh[:, :, 0:e], start=True, stop=True).then_inc(s["cnt_ps"], 1)

        def ids_out(v, s, then, cols, n_vals):
            v.wait_ge(s["ids_ps"], 1)
            src = bank[2][:, 0:n_vals * cols].rearrange("p (n c) -> p n c", n=n_vals)
            then(nc.vector.tensor_copy(vals[:, 0:n_vals, 0:cols], src))
            nc.vector.tensor_scalar(padm[:, 0:cols], vals[:, 1, 0:cols], 0.0, float(PAD), ALU.is_equal, ALU.mult)
            if n_vals == 5:
                then(nc.vector.scalar_tensor_tensor(out=gsum[:, 0:cols], in0=vals[:, 4, 0:cols], scalar=2.0 ** -12,
                                                    in1=vals[:, 3, 0:cols], op0=ALU.mult, op1=ALU.add))
                then(nc.vector.scalar_tensor_tensor(out=gslot[:, 0:cols], in0=gsum[:, 0:cols], scalar=2.0 ** -12,
                                                    in1=vals[:, 2, 0:cols], op0=ALU.mult, op1=ALU.add))
            then(nc.vector.scalar_tensor_tensor(out=idf[:, 0:cols], in0=vals[:, 0, 0:cols], scalar=float(P),
                                                in1=vals[:, 1, 0:cols], op0=ALU.mult, op1=ALU.add))
            nc.vector.scalar_tensor_tensor(out=ids_all[:, 0:cols], in0=idf[:, 0:cols], scalar=-1.0, in1=padm[:, 0:cols],
                                           op0=ALU.add, op1=ALU.add).then_inc(s["ids"], 1)

        def route0_dve(v, s):
            then = Line(v, s["line"])
            rev = R("rev0").unsqueeze(1).broadcast_to([P, NT, E0])
            v.wait_ge(GL["lg"], B)
            then(nc.vector.tensor_reduce(one["lmax"][:, :], lg[:, :, :], AX, ALU.max))
            nc.vector.tensor_tensor(wide[3][:, :, :], lg[:, :, :], bcast(one["lmax"][:, :], E0), ALU.subtract
                                    ).then_inc(s["lsh"], 1)
            then(nc.vector.tensor_tensor(wide[0][:, :, :], lg[:, :, :], bcast(one["lmax"][:, :], E0), ALU.is_equal))
            then(nc.vector.tensor_tensor(wide[1][:, :, :], wide[0][:, :, :], rev, ALU.mult))
            then(nc.vector.tensor_reduce(one["best"][:, :], wide[1][:, :, :], AX, ALU.max))
            nc.vector.tensor_tensor(oh[:, :, :], rev, bcast(one["best"][:, :], E0), ALU.is_equal).then_inc(s["oh"], 1)
            v.wait_ge(s["ex"], 1)
            then(nc.vector.tensor_reduce(one["lsum"][:, :], wide[2][:, :, :], AX, ALU.add))
            then(nc.vector.reciprocal(one["gate"][:, :], one["lsum"][:, :]))
            then(nc.vector.tensor_copy(gpiece[:, 0, :], one["gate"][:, :]))
            then(nc.vector.tensor_tensor(one["rest"][:, :], one["gate"][:, :], gpiece[:, 0, :], ALU.subtract))
            then(nc.vector.tensor_scalar(gpiece[:, 1, :], one["rest"][:, :], 4096.0, None, ALU.mult))
            then(nc.vector.scalar_tensor_tensor(out=one["rest2"][:, :], in0=one["rest"][:, :], scalar=4096.0,
                                                in1=gpiece[:, 1, :], op0=ALU.mult, op1=ALU.subtract))
            then(nc.vector.tensor_scalar(gpiece[:, 2, :], one["rest2"][:, :], 4096.0, None, ALU.mult))
            places(v, s, then, E0, one["pos"][:, :])
            then(nc.vector.tensor_scalar(one["late"][:, :], one["pos"][:, :], float(P), None, ALU.is_ge))
            then(nc.vector.scalar_tensor_tensor(out=one["p16"][:, :], in0=one["late"][:, :], scalar=-float(P),
                                                in1=one["pos"][:, :], op0=ALU.mult, op1=ALU.add))
            then(nc.vector.scalar_tensor_tensor(out=one["ef"][:, :], in0=one["best"][:, :], scalar=-2.0,
                                                in1=one["late"][:, :], op0=ALU.mult, op1=ALU.add))
            then(nc.vector.tensor_scalar(one["col"][:, :], one["ef"][:, :], 2.0 * E0, None, ALU.add))
            slots(v, s, then, 2 * E0, 5)
            ids_out(v, s, then, 2 * E0, 5)

        def route0_act(act, s):
            act.wait_ge(s["lsh"], 1)
            nc.scalar.activation(wide[2][:, :, :], wide[3][:, :, :], ACT.Exp).then_inc(s["ex"], 1)

        X0 = Signals("exp0")

        def expert_pool(p, s, table, dest, before, n, extra=None):
            def gather(at, slot):
                for t in range(2):
                    nc.gpsimd.indirect_dma_start(
                        out=rg[:, slot, t, :], out_offset=None, in_=table,
                        in_offset=bass.IndirectOffsetOnAxis(ap=at[:, t:t + 1], axis=0),
                        bounds_check=N - 1, oob_is_err=False).then_inc(s[f"g{slot}"], 16)

            def ids_of(u, i, slot, first, last):
                if not first:
                    p.wait_ge(s[f"s{slot}"], apart(p, 32 * i))
                if last:
                    nc.gpsimd.tensor_copy(raw[:, slot, 0, :], ids_all[:, ds(u * 2, 2)]).then_inc(s["raw"], 1)
                else:
                    nc.gpsimd.tensor_copy(raw[:, slot, :, :], ids_all[:, ds(u * 2, 6)].rearrange(
                        "p (k c) -> p k c", c=2)[:, 0:3:2, :]).then_inc(s["raw"], 1)
                done = u + 1
                if extra is not None:
                    extra(p, s, u, slot, i)
                p.wait_ge(s["yo"], done)
                p.wait_ge(s["raw"], done)
                nc.gpsimd.tensor_tensor(ids[:, slot, :, :], raw[:, slot, :, :], zero_i[:, :, :], ALU.add
                                        ).then_inc(s["ids"], 1)
                p.wait_ge(ready, READY)
                p.wait_ge(s["ids"], done)

            def body(i, first, last):
                for slot in range(2):
                    u = 2 * i + slot
                    ids_of(u, i, slot, first, last)
                    for t in range(2):
                        nc.gpsimd.indirect_dma_start(
                            out=dest, out_offset=bass.IndirectOffsetOnAxis(ap=ids[:, slot, 0, t:t + 1], axis=0),
                            in_=yo[:, slot, t, :], in_offset=None,
                            bounds_check=N - 1, oob_is_err=False).then_inc(s[f"s{slot}"], 16)
                    if not last:
                        gather(ids[:, slot, 1, :], slot)

            before(p)
            gather(ids_all[:, 0:2], 0)
            gather(ids_all[:, 2:4], 1)
            steps3(p, n // 2, body)

        def expert_sp(sp, s, pack, which, n, before):
            before(sp)

            def load(u, slot):
                sp.dma_start(wx[:, slot, :], pack[ds(which(sp, u), 1), :, :].rearrange("o p w -> (o p) w")
                             ).then_inc(s[f"w{slot}"], 16)

            def body(i, last):
                for slot in range(2):
                    u = 2 * i + slot
                    if not last:
                        sp.wait_ge(s["yb"], apart(sp, u + 1))
                        load(u + 2, slot)
            load(0, 0)
            load(1, 1)
            steps(sp, n // 2, body)

        def expert_pe(pe, s, n):
            def turn(u, i, slot):
                pe.wait_ge(s[f"g{slot}"], 32 * (i + 1))
                for t in range(2):
                    ins = nc.tensor.transpose(bank[4 * slot][:, t * P:(t + 1) * P], rg[:, slot, t, 0:D], W("ident"))
                ins.then_inc(s["xT_ps"], 1)

            def hidden(u, i, slot):
                pe.wait_ge(s["xT"], u + 1)
                pe.wait_ge(s[f"w{slot}"], 16 * (i + 1))
                for c in range(HC):
                    ins = nc.tensor.matmul(bank[4 * slot + 1 + c // 2][:, (c % 2) * PAIR:(c % 2 + 1) * PAIR],
                                           wx[:, slot, c * P:(c + 1) * P], exT[:, slot, :], start=True, stop=True)
                    if c % 2:
                        ins.then_inc(s["hb_ps" if c > 1 else "ha_ps"], 1)

            def outer(u, slot):
                for t in range(2):
                    for c in range(HC):
                        if t == 0 and c % 2 == 0:
                            pe.wait_ge(s["hb" if c else "ha"], u + 1)
                        ins = nc.tensor.matmul(bank[4 * slot + 3][:, t * D:(t + 1) * D], hT[:, slot, c, t * P:(t + 1) * P],
                                               wx[:, slot, H + c * D:H + (c + 1) * D], start=(c == 0), stop=(c == HC - 1))
                ins.then_inc(s["y_ps"], 1)

            def body(i, last):
                for slot in range(2):
                    u = 2 * i + slot
                    hidden(u, i, slot)
                    if not (last and slot):
                        turn(u + 1, i + slot, 1 - slot)
                    outer(u, slot)
            turn(0, 0, 0)
            steps(pe, n // 2, body)

        def expert_act(act, s, n):
            def body(i, last):
                for slot in range(2):
                    u = 2 * i + slot
                    if True:
                        act.wait_ge(s["xT_ps"], u + 1)
                        nc.scalar.copy(exT[:, slot, :], bank[4 * slot][:, 0:PAIR]).then_inc(s["xT"], 1)
                    act.wait_ge(s["ha_ps"], u + 1)
                    for c in range(2):
                        ins = nc.scalar.activation(hT[:, slot, c, :], bank[4 * slot + 1][:, c * PAIR:(c + 1) * PAIR],
                                                   ACT.Relu, bias=wx[:, slot, H + HC * D + c:H + HC * D + c + 1])
                    ins.then_inc(s["ha"], 1)
            steps(act, n // 2, body)

        def expert_dve0(v, s, n):
            def body(i, first, last):
                for slot in range(2):
                    u = 2 * i + slot
                    v.wait_ge(s["hb_ps"], u + 1)
                    for c in range(2, HC):
                        ins = nc.vector.tensor_scalar(hT[:, slot, c, :], bank[4 * slot + 2][:, (c - 2) * PAIR:(c - 1) * PAIR],
                                                      wx[:, slot, H + HC * D + c:H + HC * D + c + 1], 0.0, ALU.add, ALU.max)
                    ins.then_inc(s["hb"], 1)
                    v.wait_ge(s["y_ps"], u + 1)
                    nc.vector.tensor_tensor(yb[:, slot, :, :], bank3(4 * slot + 3, 2, D),
                                            wx[:, slot, WP - D:WP].unsqueeze(1).broadcast_to([P, 2, D]), ALU.add
                                            ).then_inc(s["yb"], 1)
                    v.wait_ge(s["yb"], u + 1)
                    if not first:
                        v.wait_ge(s[f"s{slot}"], 32 * i)
                    for t in range(2):
                        ins = nc.vector.scalar_tensor_tensor(out=yo[:, slot, t, :], in0=yb[:, slot, t, :],
                                                             scalar=gslot[:, ds(u * 2 + t, 1)],
                                                             in1=rg[:, slot, t, D:2 * D], op0=ALU.mult, op1=ALU.add)
                    ins.then_inc(s["yo"], 1)
            steps3(v, n // 2, body)

        def expert_dve1(v, s, n):
            def body(i, first, last):
                for slot in range(2):
                    u = 2 * i + slot
                    v.wait_ge(s["hb_ps"], u + 1)
                    for c in range(2, HC):
                        ins = nc.vector.tensor_scalar(hT[:, slot, c, :], bank[4 * slot + 2][:, (c - 2) * PAIR:(c - 1) * PAIR],
                                                      wx[:, slot, H + HC * D + c:H + HC * D + c + 1], 0.0, ALU.add, ALU.max)
                    ins.then_inc(s["hb"], 1)
                    v.wait_ge(s["y_ps"], u + 1)
                    nc.vector.tensor_tensor(yb[:, slot, :, :], bank3(4 * slot + 3, 2, D),
                                            wx[:, slot, WP - D:WP].unsqueeze(1).broadcast_to([P, 2, D]), ALU.add
                                            ).then_inc(s["yb"], 1)
                    v.wait_ge(s["yb"], u + 1)
                    nc.vector.tensor_tensor(yr[:, slot, :, :], yb[:, slot, :, :], rg[:, slot, :, 0:D], ALU.add
                                            ).then_inc(s["yb2"], 1)
                    v.wait_ge(s["yb2"], u + 1)
                    for t in range(2):
                        ins = nc.vector.bn_stats(st1[:, t, :], yr[:, slot, t, :])
                    ins.then_inc(s["bn"], 1)
                    v.wait_ge(s["bn"], apart(v, u + 1))
                    for t in range(2):
                        ins = nc.vector.bn_aggr(mv1[:, t, :], st1[:, t, :])
                    ins.then_inc(s["st"], 1)
                    v.wait_ge(s["rs"], u + 1)
                    for t in range(2):
                        ins = nc.vector.tensor_scalar(yn[:, slot, t, :], yr[:, slot, t, :], mv1[:, t, 0:1],
                                                      rs1[:, t:t + 1], ALU.subtract, ALU.mult)
                    ins.then_inc(s["yn"], 1)
                    v.wait_ge(s["yn"], u + 1)
                    nc.vector.tensor_tensor(yr[:, slot, :, :], yn[:, slot, :, :],
                                            R("g2").unsqueeze(1).broadcast_to([P, 2, D]), ALU.mult).then_inc(s["ys"], 1)
                    v.wait_ge(s["ys"], u + 1)
                    v.wait_ge(s["bx"], u + 1)
                    if not first:
                        v.wait_ge(s[f"s{slot}"], 32 * i)
                    nc.vector.tensor_tensor(yo[:, slot, :, :], yr[:, slot, :, :], bx[:, slot, :, :], ALU.add
                                            ).then_inc(s["yo"], 1)
            steps3(v, n // 2, body)

        M = Signals("heads")

        def plan(first, last):
            at = [[(0, "ks", 0, 2), (2, "qs", 0, 2), (3, "V", 0, 0)],
                  [(0, "ks", 0, 3), (2, "qs", 0, 3)], [], []]
            if not first:
                at[0] += [(6, "BT", -1, 0), (8, "BT", -1, 1), (10, "BT", -1, 2), (12, "BT", -1, 3)]
                at[1] += [(10, "AT", -1, 0), (12, "WO", -1, 0)]
                at[2] += [(4, "AT", -1, 1), (6, "WO", -1, 1), (8, "AT", -1, 2), (10, "WO", -1, 2)]
                at[3] += [(5, "AT", -1, 3), (8, "WO", -1, 3)]
            if not last:
                at[1] += [(4, "T", 1, 0), (6, "Q", 1, 0), (8, "K", 1, 0)]
                at[2] += [(0, "ks", 1, 0), (2, "qs", 1, 0)]
                at[3] += [(0, "ks", 1, 1), (2, "qs", 1, 1)]
            for g in range(G - 1 if last else G):
                at[g].append((15, "q2", (g + 1) // G, (g + 1) % G))
            return [sorted(a, key=lambda z: z[0]) for a in at]

        PROLOGUE = [("T", 0, 0), ("Q", 0, 0), ("K", 0, 0), ("ks", 0, 0), ("qs", 0, 0), ("ks", 0, 1), ("qs", 0, 1)]
        EPILOGUE = [("BT", -1, t) for t in range(T)] + [(k, -1, t) for t in range(T) for k in ("AT", "WO")]
        FIRST = sum(len(a) for a in plan(True, False))
        MIDDLE = sum(len(a) for a in plan(False, False))
        START = len(PROLOGUE) + 1

        def misc_base(it, first, last):
            return START if first else it * MIDDLE + (START + FIRST - MIDDLE)

        class Misc:
            def __init__(self, do):
                self.do = do

            def sequence(self, it, first, last, step):
                base, n = misc_base(it, first, last), 0
                for slot, units in enumerate(plan(first, last)):
                    start = n
                    units = list(units)
                    for i in range(16):
                        while units and units[0][0] == i:
                            _, kind, db, k = units.pop(0)
                            self.do(kind, it + db, k, base + n)
                            n += 1
                        step(it, slot, i, base + start, first, last)

        def heads_pe(pe):
            s = M

            def do(kind, b, k, m):
                if m is None or not (type(m) is int and m == 0):
                    pe.wait_ge(s["misc_empty"], m)
                x = bank[7]
                if kind == "T":
                    pe.wait_ge(s["xn"], b + 1)
                    for t in range(T):
                        ins = nc.tensor.transpose(x[:, t * P:(t + 1) * P], xn[:, t, :], W("ident"))
                elif kind in "QK":
                    ins = nc.tensor.matmul(x, W("qh" if kind == "Q" else "kh"), xnT[:, :], start=True, stop=True)
                elif kind == "V":
                    for t in range(T):
                        ins = nc.tensor.matmul(x[:, t * D:(t + 1) * D], xnT[:, t * P:(t + 1) * P], W("vh"),
                                               start=True, stop=True)
                elif kind in ("ks", "qs"):
                    hi, lo = (khi, klo) if kind == "ks" else (qhi, qlo)
                    nc.tensor.matmul(x, C(kind[0] + "A", k), hi[:, :], start=True, stop=False)
                    ins = nc.tensor.matmul(x, C(kind[0] + "B", k), lo[:, :], start=False, stop=True)
                elif kind == "q2":
                    pe.wait_ge(s["nmax"], (b * G + k + 1) * 16)
                    for t in range(T):
                        nc.tensor.matmul(x[:, t * P:(t + 1) * P], mrow[:, k % 2, t, :], C("ident"),
                                         start=(t == 0), stop=False)
                    ins = nc.tensor.matmul(x, C("ident"), qs1[:, k, :], start=False, stop=True)
                elif kind == "BT":
                    pe.wait_ge(s["otm"], (b + 1) * G)
                    for g in range(G):
                        ins = nc.tensor.transpose(x[:, g * P:(g + 1) * P], otm[:, g, k * P:(k + 1) * P], W("ident"))
                elif kind == "AT":
                    ins = nc.tensor.transpose(x[:, 0:P], ath[:, k, :], W("ident"))
                elif kind == "WO":
                    ins = nc.tensor.matmul(x[:, 0:P], atT[:, :], W("oh"), start=True, stop=True)
                ins.then_inc(s["misc_full"], 1)

            def score(n, g, i, start=False):
                if i == 0:
                    pe.wait_ge(s["kpad"], n + 1)
                if not (start and i < 2):
                    pe.wait_ge(s["nmax"], n * 16 + i - 1)
                j, t = i // 4, i % 4
                nc.tensor.matmul(bank[i % 2], qs1[:, g, t * P:(t + 1) * P], kpad[:, g, j, :],
                                 start=True, stop=True).then_inc(s["s_ps"], 1)

            def turned(n, g, i, early):
                c, j = i // 4, i % 4
                if i % 2 == 0 and not (early and i < 4):
                    pe.wait_ge(s["exp"], n * 8 + i // 2 - 1)
                ins = nc.tensor.matmul(bank[2 + i % 4], kpad[:, g, j, c * P:(c + 1) * P], qs2[:, g, :],
                                       start=True, stop=True)
                if i % 2:
                    ins.then_inc(s["st_ps"], 1)

            def mix(n, g, c, early):
                pe.wait_ge(s["exp"], n * 8 + 2 * c + 2)
                if c == 0 and not early:
                    pe.wait_ge(s["otm"], n)
                for j in range(4):
                    ins = nc.tensor.matmul(bank[6][32 * j:32 * j + 32, :], vh[:, c, 4 * g + j, :],
                                           ptm[:, (2 * c + j // 2) % 4, (j % 2) * S:(j % 2 + 1) * S],
                                           start=(c == 0), stop=(c == T - 1))
                ins.then_inc(s["pv"], 1)

            def step(it, g, i, m0, first, last):
                n = it * G + g
                if not (last and g == G - 1):
                    for k in ((0, 1), (2,), (3,), (4,), (5, 6), (7,), (8,), (9,), (10, 11), (12,), (13,), (14,), (15,))[i] \
                            if i < 13 else ():
                        score(n + 1, (g + 1) % G, k)
                if i == 0:
                    pe.wait_ge(s["misc_empty"], m0)
                early = first and g == 0
                turned(n, g, i, early)
                if i == 2 and not early:
                    mix(n - 1, (g - 1) % G, 3, False)
                if i in (6, 10, 14):
                    if i == 6 and g == 0:
                        pe.wait_ge(s["misc_empty"], m0 + 3)
                    mix(n, g, (i - 6) // 4, early)

            m = 0
            for kind, b, k in PROLOGUE:
                do(kind, b, k, m)
                m += 1
            for i in range(16):
                score(0, 0, i, True)
            do("q2", 0, 0, m)
            misc = Misc(do)
            steps3(pe, B, lambda it, first, last: misc.sequence(it, first, last, step))
            mix(B * G - 1, G - 1, 3, False)
            m = misc_base(B, False, False) - MIDDLE + sum(len(a) for a in plan(False, True))
            for kind, db, k in EPILOGUE:
                do(kind, B + db, k, m)
                m += 1

        def heads_act(act):
            s = M

            def do(kind, b, k, m):
                act_kinds = {"T", "Q", "K", "ks", "qs", "q2", "AT"}
                if kind not in act_kinds:
                    return
                act.wait_ge(s["misc_full"], m + 1)
                x = bank[7]
                if kind == "T":
                    nc.scalar.copy(xnT[:, :], x).then_inc(s["misc_empty"], 1)
                elif kind == "Q":
                    nc.scalar.activation(qhi[:, :], x, ACT.Identity, bias=W("bqh")).then_inc(s["qhi"], 1)
                elif kind == "K":
                    nc.scalar.activation(khi[:, :], x, ACT.Identity, bias=W("bkh")).then_inc(s["khi"], 1)
                elif kind == "ks":
                    if not (type(b) is int and b == 0 and k == 0):
                        act.wait_ge(s["kpad"], b * G + k)
                    nc.scalar.activation(kst[:, :], x, ACT.Identity, bias=W("one24")).then_inc(s["misc_empty"], 1)
                elif kind == "qs":
                    nc.scalar.copy(qs1[:, k, :], x).then_inc(s["misc_empty"], 1)
                elif kind == "q2":
                    nc.scalar.copy(qs2[:, k, :], x).then_inc(s["misc_empty"], 1)
                elif kind == "AT":
                    nc.scalar.copy(atT[:, :], x[:, 0:P]).then_inc(s["misc_empty"], 1)

            def step(it, g, i, m0, first, last):
                n = it * G + g
                if i % 2:
                    q = i // 2
                    act.wait_ge(s["st_ps"], n * 8 + q + 1)
                    if not (first and g == 0 and q < 4):
                        act.wait_ge(s["pv"], n * 4 + q // 2 - 1)
                    nc.scalar.activation(ptm[:, q % 4, :], psum[:, (2 + 2 * (q % 2)) * S:(4 + 2 * (q % 2)) * S], ACT.Exp,
                                         scale=SCALE_H).then_inc(s["exp"], 1)
                if i == 4 and not (first and g == 0):
                    group_out(n - 1, (g - 1) % G)

            def group_out(n, g):
                act.wait_ge(s["pv"], n * 4 + 4)
                nc.scalar.copy(otm[:, g, :], bank[6]).then_inc(s["otm"], 1)

            m = 0
            for kind, b, k in PROLOGUE:
                do(kind, b, k, m)
                m += 1
            do("q2", 0, 0, m)
            misc = Misc(do)
            steps3(act, B, lambda it, first, last: misc.sequence(it, first, last, step))
            group_out(B * G - 1, G - 1)
            m = misc_base(B, False, False) - MIDDLE + sum(len(a) for a in plan(False, True))
            for kind, db, k in EPILOGUE:
                do(kind, B + db, k, m)
                m += 1

        def heads_dve(v):
            s = M

            def apply(b, first=False):
                if not first:
                    v.wait_ge(s["sres"], b)
                for t in range(T):
                    ins = apply_all(b, t, xn[:, t, :])
                ins.then_inc(s["xn"], 1)

            def do(kind, b, k, m):
                if kind not in {"Q", "K", "V", "BT", "WO"}:
                    return
                x = bank[7]
                if kind in "QK":
                    hi, lo, bias, ev = (qhi, qlo, W("bqh"), "qhi") if kind == "Q" else (khi, klo, W("bkh"), "khi")
                    v.wait_ge(s[ev], b + 1)
                    nc.vector.scalar_tensor_tensor(out=lo[:, :], in0=x, scalar=bias, in1=hi[:, :], op0=ALU.add,
                                                   op1=ALU.subtract).then_inc(s["misc_empty"], 1)
                    return
                v.wait_ge(s["misc_full"], m + 1)
                if kind == "V":
                    nc.vector.tensor_tensor(vh[:, :, :, 0:DH], x.rearrange("p (t h e) -> p t h e", t=T, h=NH),
                                            R("bvh").rearrange("p (h e) -> p h e", h=NH).unsqueeze(1)
                                            .broadcast_to([P, T, NH, DH]), ALU.add).then_inc(s["misc_empty"], 1)
                elif kind == "BT":
                    x3 = x.rearrange("p (h e) -> p h e", h=NH)
                    nc.vector.reciprocal(rch[:, :], x3[:, :, DH]).then_inc(s["rch"], 1)
                    v.wait_ge(s["rch"], b * T + k + 1)
                    nc.vector.tensor_tensor(ath[:, k, :].rearrange("p (h e) -> p h e", h=NH), x3[:, :, 0:DH],
                                            bcast(rch[:, :], DH), ALU.mult).then_inc(s["misc_empty"], 1)
                elif kind == "WO":
                    nc.vector.tensor_tensor(xt(b * T + k, s_all), x[:, 0:D], xt(b * T + k, s_all), ALU.add
                                            ).then_inc(s["misc_empty"], 1)

            def row_max(n, g, i):
                v.wait_ge(s["s_ps"], n * 16 + i + 1)
                j, t = i // 4, i % 4
                nc.vector.tensor_reduce(mrow[:, g % 2, t, 32 * j + 24:32 * j + 25], bank[i % 2], AX, ALU.max, negate=True
                                        ).then_inc(s["nmax"], 1)

            def step(it, g, i, m0, first, last):
                n = it * G + g
                if not (last and g == G - 1):
                    for k in ((0, 1), (2,), (3,), (4,), (5, 6), (7,), (8,), (9,), (10, 11), (12,), (13,), (14,), (15,))[i] \
                            if i < 13 else ():
                        row_max(n + 1, (g + 1) % G, k)
                if g == 0 and i == 2 and not last:
                    apply(it + 1)

            v.wait_ge(C1["rstd"], B + 1)
            apply(0, True)
            for kind, b, k in PROLOGUE:
                do(kind, b, k, 0)
            for i in range(16):
                row_max(0, 0, i)
            misc = Misc(do)
            steps3(v, B, lambda it, first, last: misc.sequence(it, first, last, step))
            m = misc_base(B, False, False) - MIDDLE + sum(len(a) for a in plan(False, True))
            for kind, db, k in EPILOGUE:
                do(kind, B + db, k, m)
                m += 1
            v.wait_ge(s["misc_empty"], m)

        def heads_pool(p):
            s = M

            def spread(b, g, m):
                p.wait_ge(s["misc_empty"], m + 1)
                nc.gpsimd.tensor_tensor(kpad[:, g, :, :], kst[:, :].unsqueeze(1).broadcast_to([P, 4, S]),
                                        c_all[:, CTOT - 4:CTOT].unsqueeze(2).broadcast_to([P, 4, S]), ALU.mult
                                        ).then_inc(s["kpad"], 1)

            def residual(b):
                p.wait_ge(s["xn"], b + 1)
                nc.gpsimd.tensor_tensor(x4(b, s_all), xn[:, :, :], R("boh").unsqueeze(1).broadcast_to([P, T, D]), ALU.add
                                        ).then_inc(s["sres"], 1)

            def do(kind, b, k, m):
                if kind == "ks":
                    spread(b, k, m)

            def step(it, g, i, m0, first, last):
                if g == 0 and i == 5 and not last:
                    residual(it + 1)
            residual(0)
            for m, (kind, b, k) in enumerate(PROLOGUE):
                do(kind, b, k, m)
            misc = Misc(do)
            steps3(p, B, lambda it, first, last: misc.sequence(it, first, last, step))

        F = Signals("norm1")

        def norm1_dve(v, s):
            for i in range(NT):
                ins = nc.vector.bn_stats(stats3[:, i, :], xt(i, s_all))
            ins.then_inc(s["bn"], 1)
            v.wait_ge(s["bn"], 1)
            for i in range(NT):
                ins = nc.vector.bn_aggr(mv_all[:, i, :], stats3[:, i, :])
            ins.then_inc(s["mv"], 1)
            v.wait_ge(s["rstd"], 1)
            for b in range(B):
                for t in range(T):
                    i = b * T + t
                    ins = nc.vector.tensor_scalar(xt(i, s_all), xt(i, s_all), mv_all[:, i, 0:1], rstd_all[:, i:i + 1],
                                                  ALU.subtract, ALU.mult)
                ins.then_inc(s["xn"], 1)
                v.wait_ge(s["xn"], b + 1)
                nc.vector.tensor_tensor(x4(b, s_all), x4(b, s_all), R("g1").unsqueeze(1).broadcast_to([P, T, D]), ALU.mult
                                        ).then_inc(s["scaled"], 1)
            for b in range(B):
                v.wait_ge(s["x1"], b + 1)
                nc.vector.tensor_tensor(xg[:, b % 2, :, :], x4(b, s_all), R("rw").unsqueeze(1).broadcast_to([P, T, D]),
                                        ALU.mult).then_inc(s["dot"], 1)
                v.wait_ge(s["dot"], b + 1)
                nc.vector.tensor_reduce(one["key"][:, b * T:(b + 1) * T], xg[:, b % 2, :, :], AX, ALU.add
                                        ).then_inc(s["key"], 1)
            v.wait_ge(s["key"], B)

        def norm1_pool(p, s):
            p.wait_ge(s["mv"], 1)
            nc.gpsimd.tensor_tensor(var_all[:, :], mv_all[:, :, 1], eps[:, :], ALU.add).then_inc(s["eps"], 1)
            p.wait_ge(s["eps"], 1)
            nc.gpsimd.tensor_tensor(rstd_all[:, :], var_all[:, :], neg_half[:, :], ALU.pow).then_inc(s["rstd"], 1)
            for b in range(B):
                p.wait_ge(s["scaled"], b + 1)
                nc.gpsimd.tensor_tensor(x4(b, s_all), x4(b, s_all), R("b1").unsqueeze(1).broadcast_to([P, T, D]), ALU.add
                                        ).then_inc(s["x1"], 1)

        def norm1_sp(sp, s):
            for b in range(B):
                sp.wait_ge(C1["x_out"], (b + 1) * T)
                sp.dma_start(table1[b * S:(b + 1) * S, D:2 * D].rearrange("(t p) d -> p t d", p=P), x4(b)
                             ).then_inc(s["table"], 16)
            for b in range(B):
                sp.wait_ge(s["x1"], b + 1)
                sp.dma_start(table1[b * S:(b + 1) * S, 0:D].rearrange("(t p) d -> p t d", p=P), x4(b, s_all)
                             ).then_inc(s["table"], 16)

        def route1_dve(v, s):
            then = Line(v, s["line"])
            o = {n: a[:, :] for n, a in one.items()}
            i = {n: a[:, :] for n, a in oni.items()}
            then(nc.vector.tensor_scalar(o["key"], o["key"], R("rb"), None, ALU.add))
            then(nc.vector.tensor_copy(i["key"], o["key"]))
            then(nc.vector.tensor_copy(o["keyf"], i["key"]))
            then(nc.vector.tensor_tensor(o["gt"], o["keyf"], o["key"], ALU.is_gt))
            then(nc.vector.tensor_tensor(i["floor"], o["keyf"], o["gt"], ALU.subtract))
            then(nc.vector.tensor_scalar(i["e"], i["floor"], E1 - 1, None, ALU.bitwise_and))
            then(nc.vector.tensor_copy(o["ef"], i["e"]))
            nc.vector.tensor_tensor(oh[:, :, 0:E1], R("iota")[:, 0:E1].unsqueeze(1).broadcast_to([P, NT, E1]),
                                    bcast(o["ef"], E1), ALU.is_equal).then_inc(s["oh"], 1)
            sums = places(v, s, then, E1, o["pos"])
            then(nc.vector.tensor_scalar(toti[:, :], sums[:, NT - 1, :], float(PAIR - 1), None, ALU.add))
            then(nc.vector.tensor_scalar(toti[:, :], toti[:, :], 8, None, ALU.logical_shift_right))
            then(nc.vector.tensor_copy(pairs[:, :], toti[:, :]))
            then(nc.vector.memset(starts[:, :], 0.0))
            for e in range(E1 - 1):
                then(nc.vector.tensor_tensor(starts[:, e + 1:e + 2], starts[:, e:e + 1], pairs[:, e:e + 1], ALU.add))
            for e in range(1, E1):
                ins = nc.vector.tensor_scalar(which[:, e - 1, :], R("iota")[:, 0:U1], starts[:, e:e + 1], None, ALU.is_ge)
            then(ins)
            then(nc.vector.tensor_tensor(esum[:, :], which[:, 0, :], which[:, 1, :], ALU.add))
            nc.vector.tensor_tensor(e_of[:, :], esum[:, :], which[:, 2, :], ALU.add).then_inc(s["e_of"], 1)
            then(nc.vector.tensor_copy(i["pos"], o["pos"]))
            nc.vector.tensor_scalar(i["p"], i["pos"], P - 1, None, ALU.bitwise_and)
            then(nc.vector.tensor_scalar(i["j"], i["pos"], 7, None, ALU.logical_shift_right))
            nc.vector.tensor_copy(o["p16"], i["p"])
            then(nc.vector.tensor_copy(o["jf"], i["j"]))
            then(nc.vector.tensor_tensor(wide[3][:, :, 0:E1], oh[:, :, 0:E1],
                                         starts[:, :].unsqueeze(1).broadcast_to([P, NT, E1]), ALU.mult))
            then(nc.vector.tensor_reduce(o["base"], wide[3][:, :, 0:E1], AX, ALU.add))
            then(nc.vector.scalar_tensor_tensor(out=o["col"], in0=o["base"], scalar=2.0, in1=o["jf"],
                                                op0=ALU.mult, op1=ALU.add))
            slots(v, s, then, 2 * U1, 2)
            ids_out(v, s, then, 2 * U1, 2)

        X1 = Signals("exp1")

        def expert_pool1(p, s, u, slot, i):
            p.wait_ge(s[f"g{slot}"], 32 * (i + 1))
            nc.gpsimd.tensor_tensor(bx[:, slot, :, :], rg[:, slot, :, D:2 * D], R("b2").unsqueeze(1).broadcast_to([P, 2, D]),
                                    ALU.add).then_inc(s["bx"], 1)
            p.wait_ge(s["st"], u + 1)
            nc.gpsimd.tensor_tensor(ve1[:, :], mv1[:, :, 1], eps[:, 0:2], ALU.add).then_inc(s["eps"], 1)
            p.wait_ge(s["eps"], u + 1)
            nc.gpsimd.tensor_tensor(rs1[:, :], ve1[:, :], neg_half[:, 0:2], ALU.pow).then_inc(s["rs"], 1)

        block = ctx.enter_context(nc.Block())

        @block.sync
        def _(sp):
            sp.dma_start(r_all[:, :], r_in).then_inc(consts, 16)
            sp.dma_start(c_all[:, :], c_in).then_inc(consts, 16)
            attn_sp(sp, A, x_in)
            gate_sp(sp, GL)
            expert_sp(sp, X0, pack0_in, lambda sp, u: u, U0, lambda sp: None)
            for slot in range(2):
                sp.wait_ge(X0[f"s{slot}"], 32 * (U0 // 2))
            sp.wait_ge(GL["x2"], 32 * B)
            attn_sp(sp, C1, x2d)
            norm1_sp(sp, F)

            def expert_of(sp, u):
                return sp.value_load(e_of[0:1, ds(u, 1)], min_val=0, max_val=E1 - 1)
            sp.wait_ge(RT1["e_of"], 1)
            expert_sp(sp, X1, pack1_in, expert_of, U1, lambda sp: None)
            for slot in range(2):
                sp.wait_ge(X1[f"s{slot}"], 32 * (U1 // 2))

        @block.scalar
        def _(act):
            act.dma_start(w_all[:, :], w_in).then_inc(consts, 16)
            attn_act(act, A, W("bq0"), True)
            gate_act(act, GL)
            route0_act(act, RT0)
            expert_act(act, X0, U0)
            attn_act(act, C1, None, False)
            heads_act(act)
            expert_act(act, X1, U1)

        @block.vector
        def _(v):
            nc.vector.memset(rg[:, :, :, :], 0.0).then_inc(ready, 1)
            nc.vector.memset(mrow[:, :, :, :], 0.0).then_inc(ready, 1)
            attn_dve(v, A, W("bk0"), R("bv0"), W("gauss"), True)
            gate_dve(v, GL)
            route0_dve(v, RT0)
            expert_dve0(v, X0, U0)
            attn_dve(v, C1, None, None, None, False)
            heads_dve(v)
            norm1_dve(v, F)
            route1_dve(v, RT1)
            expert_dve1(v, X1, U1)

        @block.gpsimd
        def _(p):
            nc.gpsimd.memset(neg_half[:, :], -0.5).then_inc(ready, 1)
            nc.gpsimd.memset(eps[:, :], EPS).then_inc(ready, 1)
            nc.gpsimd.memset(zero_i[:, :, :], 0).then_inc(ready, 1)
            nc.gpsimd.memset(raw[:, :, :, :], 0).then_inc(ready, 1)
            nc.gpsimd.memset(vh[:, :, :, DH + 1:], 0.0).then_inc(ready, 1)
            nc.gpsimd.memset(vh[:, :, :, DH:DH + 1], 1.0).then_inc(ready, 1)
            p.wait_ge(ready, READY)
            p.wait_ge(consts, 48)
            attn_pool(p, A, R("bo0"))
            rstd_of_all(p, A)

            def before0(p):
                p.wait_ge(RT0["ids"], 1)
                p.wait_ge(GL["x2"], 32 * B)
                for slot in range(2):
                    p.wait_ge(GL[f"rows{slot}"], 16 * (B // 2))
            expert_pool(p, X0, table0, x2d, before0, U0)
            attn_pool(p, C1, None)
            rstd_of_all(p, C1)
            heads_pool(p)
            norm1_pool(p, F)

            def before1(p):
                p.wait_ge(RT1["ids"], 1)
                p.wait_ge(F["table"], 32 * B)
            expert_pool(p, X1, table1, out, before1, U1, expert_pool1)

        @block.tensor
        def _(pe):
            attn_pe(pe, A, W("q0"), W("k0"), W("v0"), W("o0"))
            gate_pe(pe, GL)
            counts_pe(pe, RT0, E0)
            slots_pe(pe, RT0, 2 * E0, 5)
            expert_pe(pe, X0, U0)
            attn_pe(pe, C1, W("q1"), W("k1"), W("v1"), None)
            heads_pe(pe)
            counts_pe(pe, RT1, E1)
            slots_pe(pe, RT1, 2 * U1, 2)
            expert_pe(pe, X1, U1)


def lay_out(x):
    import numpy as np

    f = np.float32
    w = np.zeros((P, WTOT), f)

    def put(name, a):
        w[:, WCOL[name][0]:WCOL[name][1]] = a

    put("q0", x["L0_attn_Wq"].T)
    put("k0", x["L0_attn_Wk"].T)
    put("v0", x["L0_attn_Wv"].T)
    put("o0", x["L0_attn_Wo"].T)
    put("g0", x["L0_ffn_Wg"])
    for n, name in enumerate(("q1", "k1", "v1")):
        put(name, x["L1_attn_W_qkv"][n * D:(n + 1) * D, :].T)
    put("qh", x["L1_ffn_Wq"])
    put("kh", x["L1_ffn_Wk"])
    put("vh", x["L1_ffn_Wv"])
    put("oh", x["L1_ffn_Wo"])
    put("ident", np.eye(P, dtype=f))
    place = np.arange(S, dtype=f)
    put("gauss", np.exp(f(-0.5) * ((place - f(S / 2)) / f(S / 4)) ** 2) * f(float(D) ** -0.5))
    put("bq0", x["L0_attn_bq"][:, None])
    put("bk0", x["L0_attn_bk"][:, None])
    put("bqh", x["L1_ffn_bq"][:, None])
    put("bkh", x["L1_ffn_bk"][:, None])
    one24 = np.zeros((P, 1), f)
    one24[24::32] = 1
    put("one24", one24)

    r = np.zeros((P, RTOT), f)

    def row(name, a):
        r[:, RCOL[name][0]:RCOL[name][1]] = a

    row("bv0", x["L0_attn_bv"])
    row("bo0", x["L0_attn_bo"])
    row("bg0", np.tile(x["L0_ffn_bg"], T))
    row("rev0", np.arange(E0, 0, -1, dtype=f))
    row("bvh", x["L1_ffn_bv"])
    row("boh", x["L1_ffn_bo"])
    row("g1", x["L1_ffn_ln1_g"])
    row("b1", x["L1_ffn_ln1_b"])
    row("g2", x["L1_ffn_ln2_g"])
    row("b2", x["L1_ffn_ln2_b"])
    row("rw", x["L1_ffn_router_w"][:, 0])
    row("rb", x["L1_ffn_router_b"])
    row("iota", np.arange(P, dtype=f))
    row("tile", np.arange(NT, dtype=f))
    row("place", np.arange(1, P + 1, dtype=f)[:, None])

    c = np.zeros((P, CTOT), np.float16)
    c[:, 0:D] = np.eye(P)
    c[:, D:2 * D] = np.triu(np.ones((P, P)), 1)
    c[:, 2 * D:3 * D] = 1
    for j in range(4):
        c[32 * j:32 * j + 32, CTOT - 4 + j] = 1
    for g in range(G):
        for j in range(4):
            for d in range(DH):
                i = (4 * g + j) * DH + d
                for name, pieces in (("qA", (0, 1)), ("qB", (2,)), ("kA", (0, 2)), ("kB", (1,))):
                    for piece in pieces:
                        c[i, CCOL[name] + g * P + 32 * j + piece * DH + d] = 1

    def pack(e, w1, b1, w2, b2):
        out = np.zeros((e, P, WP), f)
        out[:, :, 0:H] = w1
        out[:, :, H:H + HC * D] = w2.reshape(e, HC, P, D).transpose(0, 2, 1, 3).reshape(e, P, HC * D)
        out[:, :, H + HC * D:H + HC * D + HC] = b1.reshape(e, HC, P).transpose(0, 2, 1)
        out[:, :, WP - D:] = b2[:, None, :]
        return out

    return {
        "x": np.ascontiguousarray(x["L0_attn_x"]).reshape(N, D),
        "weights": w, "rows": r, "constants": c,
        "experts0": pack(E0, x["L0_ffn_W1"], x["L0_ffn_b1"], x["L0_ffn_W2"], x["L0_ffn_b2"]),
        "experts1": pack(E1, x["L1_ffn_W1"], x["L1_ffn_b1"], x["L1_ffn_W2"], x["L1_ffn_b2"]),
    }


def program(nc, arrays):
    args = [nc.dram_tensor(name, a.shape, mybir.dt.from_np(a.dtype), kind="ExternalInput").ap()
            for name, a in arrays.items()]
    out = nc.dram_tensor("out", (N, D), F32, kind="ExternalOutput").ap()
    build(nc, *args, out)
    return nc


def kernel(**inputs):
    import numpy as np
    import concourse.bacc as bacc
    from concourse.bass_utils import run_bass_kernel_spmd

    arrays = lay_out({name: np.asarray(a) for name, a in inputs.items()})
    nc = program(bacc.Bacc("TRN2", target_bir_lowering=False, num_devices=1), arrays)
    got = run_bass_kernel_spmd(nc, [arrays], core_ids=[0])
    return got.results[0]["out"].reshape(B, S, D)
```

```python
from contextlib import ExitStack

import concourse.bass as bass
from concourse import mybir

ALU = mybir.AluOpType
ACT = mybir.ActivationFunctionType
AX = mybir.AxisListType.X
F32 = mybir.dt.float32
F16 = mybir.dt.float16
I32 = mybir.dt.int32
ds = bass.ds

P = 128
B = 8
S = 512
D = 128
N = B * S
T = S // P
NT = N // P
H = 512
HC = H // P
E0 = 16
CAP = N // E0
E1 = 4
PAIR = 2 * P
U0 = N // PAIR
U1 = 20
NX = 4
PAD = 8192
NH = 16
DH = D // NH
G = 4
EPS = 1e-5
SCALE_H = float(DH) ** -0.5
ROW = 2 * D
WP = H + HC * D + HC + D

WCOL = {}
at = 0
for name, width in (("q0", D), ("k0", D), ("v0", D), ("o0", D), ("g0", E0), ("q1", D), ("k1", D), ("v1", D),
                    ("qh", D), ("kh", D), ("vh", D), ("oh", D), ("ident", D), ("gauss", S), ("bq0", 1), ("bk0", 1),
                    ("bqh", 1), ("bkh", 1), ("one24", 1)):
    WCOL[name] = (at, at + width)
    at += width
WTOT = at
RCOL = {}
at = 0
for name, width in (("bv0", D), ("bo0", D), ("bg0", T * E0), ("rev0", E0), ("bvh", D), ("boh", D), ("g1", D), ("b1", D),
                    ("g2", D), ("b2", D), ("rw", D), ("rb", 1), ("iota", P), ("tile", NT), ("place", 1)):
    RCOL[name] = (at, at + width)
    at += width
RTOT = at
CCOL = {"ident": 0, "tri": D, "ones": 2 * D, "qA": 3 * D, "qB": 7 * D, "kA": 11 * D, "kB": 15 * D}
CTOT = 19 * D + 4


def build(nc, x_in, w_in, r_in, c_in, pack0_in, pack1_in, out):
    table0 = nc.dram_tensor("table0", (N, ROW), F32).ap()
    x2d = nc.dram_tensor("x_after_experts0", (N, D), F32).ap()
    table1 = nc.dram_tensor("table1", (N, ROW), F32).ap()

    ctx = ExitStack()
    with ctx:
        def sb(name, shape, dt=F32):
            return ctx.enter_context(nc.sbuf_tensor(name, shape, dt))

        def sem(name):
            return ctx.enter_context(nc.semaphore(name))

        psum = ctx.enter_context(nc.psum_tensor("psum", [P, 8 * 512], F32))
        bank = [psum[:, i * 512:(i + 1) * 512] for i in range(8)]

        w_all = sb("w_all", [P, WTOT])
        r_all = sb("r_all", [P, RTOT])
        c_all = sb("c_all", [P, CTOT], F16)
        x_all = sb("x_all", [P, NT * D])
        s_all = sb("s_all", [P, NT * D])
        stats3 = sb("stats3", [P, NT, 6])
        mv_all = sb("mv_all", [P, NT, 2])
        var_all = sb("var_all", [P, NT])
        rstd_all = sb("rstd_all", [P, NT])
        neg_half = sb("neg_half", [P, NT])
        eps = sb("eps", [P, NT])

        def W(name):
            return w_all[:, WCOL[name][0]:WCOL[name][1]]

        def R(name):
            return r_all[:, RCOL[name][0]:RCOL[name][1]]

        def C(name, n=0):
            return c_all[:, CCOL[name] + n * D:CCOL[name] + (n + 1) * D]

        def xt(i, of=x_all):
            return of[:, ds(i * D, D)]

        def x4(i, of=x_all):
            return of[:, ds(i * T * D, T * D)].rearrange("p (t d) -> p t d", t=T)

        def bank3(i, a, b):
            return bank[i][:, 0:a * b].rearrange("p (a b) -> p a b", a=a)

        def bcast(ap, n):
            return ap.unsqueeze(2).broadcast_to([P, ap.shape[1], n])

        stats = sb("stats", [P, T, 6])
        stats2 = sb("stats2", [P, T, 6])
        mv = sb("mv", [P, T, 2])
        mv2 = sb("mv2", [P, T, 2])
        var_eps = sb("var_eps", [P, T])
        rstd = sb("rstd", [P, T])
        xn = sb("xn", [P, T, D])
        xnT = sb("xnT", [P, S])
        qT = sb("qT", [P, S])
        kT = sb("kT", [P, S])
        vv = sb("vv", [P, T, D])
        pr_mem = sb("pr", [P, 4 * S])
        pr = pr_mem[:, 0:2 * S].rearrange("p (k n) -> p k n", k=2)
        prT = pr_mem[:, 2 * S:4 * S].rearrange("p (k n) -> p k n", k=2)
        oT = sb("oT", [P, 2, D])
        nmax = sb("nmax", [P, T])
        rsum = sb("rsum", [P, T])
        rinv = sb("rinv", [P, T])
        xg = sb("xg", [P, 2, T, D])
        xgT = sb("xgT", [P, 2, S])
        lg = sb("lg", [P, NT, E0])
        wide = [sb(f"wide{i}", [P, NT, E0]) for i in range(4)]
        oh = sb("oh", [P, NT, E0], F16)
        one = {n: sb("r_" + n, [P, NT]) for n in
               ("lmax", "lsum", "gate", "rest", "rest2", "best", "pos", "late", "p16", "col", "key", "keyf", "gt", "floor",
                "ef", "base", "jf", "pf")}
        oni = {n: sb("ri_" + n, [P, NT], I32) for n in ("key", "floor", "e", "pos", "p", "j")}
        gpiece = sb("gpiece", [P, 3, NT], F16)
        ptm_mem = sb("ptm", [P, 4 * 2 * S])
        otm_mem = sb("otm", [P, G * S])
        ptm = ptm_mem[:, :].rearrange("p (r n) -> p r n", r=4)
        otm = otm_mem[:, :].rearrange("p (g n) -> p g n", g=G)
        at_place = otm_mem[:, :].bitcast(F16).rearrange("p (t n) -> p t n", t=NT)
        at_col = ptm_mem[:, 0:NT * 5 * U1].bitcast(F16).rearrange("p (t k n) -> p t k n", t=NT, k=5)
        vals = sb("vals", [P, 5, 2 * U1])
        padm = sb("padm", [P, 2 * U1])
        idf = sb("idf", [P, 2 * U1])
        gslot = sb("gslot", [P, 2 * U1])
        gsum = sb("gsum", [P, 2 * U1])
        tot = sb("tot", [P, E1])
        toti = sb("toti", [P, E1], I32)
        pairs = sb("pairs", [P, E1])
        ends = sb("ends", [P, E1])
        starts = sb("starts", [P, E1])
        which = sb("which", [P, 3, U1])
        esum = sb("esum", [P, U1])
        e_of = sb("e_of", [P, U1], I32)
        ids_all = sb("ids_all", [P, 2 * U1], I32)
        raw = sb("raw", [P, NX, 2, 2], I32)
        zero_i = sb("zero_i", [P, 2, 2], I32)
        ids = sb("ids", [P, NX, 2, 2], I32)
        wx = sb("wx", [P, NX, WP])
        rg = sb("rg", [P, NX, 2, ROW])
        exT = sb("exT", [P, 2, PAIR])
        hT = pr_mem[:, :].rearrange("p (s c n) -> p s c n", s=2, c=HC)
        yb = sb("yb", [P, 2, 2, D])
        yo = sb("yo", [P, NX, 2, D])
        yr = sb("yr", [P, 2, 2, D])
        yn = sb("yn", [P, 2, 2, D])
        pre = sb("pre", [P, 2, 2, D])
        bx = sb("bx", [P, 2, 2, D])
        st1 = sb("st1", [P, 2, 6])
        mv1 = sb("mv1", [P, 2, 2, 2])
        ve1 = sb("ve1", [P, 2])
        rs1 = sb("rs1", [P, 2, 2])
        qhi = sb("qhi", [P, S], F16)
        qlo = sb("qlo", [P, S], F16)
        khi = sb("khi", [P, S], F16)
        klo = sb("klo", [P, S], F16)
        kst = sb("kst", [P, S], F16)
        kpad = sb("kpad", [P, G, 4, S], F16)
        qs1 = sb("qs1", [P, G, S], F16)
        qs2 = sb("qs2", [P, G, S], F16)
        mrow = sb("mrow", [P, 2, T, P], F16)
        vh = sb("vh", [P, T, NH, 32])
        rch = sb("rch", [P, NH])
        ath = sb("ath", [P, T, D])
        atT = sb("atT", [P, D])

        class Signals(dict):
            def __init__(self, phase):
                self.phase = phase

            def __missing__(self, name):
                self[name] = sem(f"{self.phase}_{name}")
                return self[name]

        READY = 8
        consts = sem("consts_loaded")
        ready = sem("constants_set")

        def apart(eng, value):
            value = value if isinstance(value, int) else eng.snap(value)
            eng.wait_ge(ready, READY)
            return value

        def steps(eng, n, body):
            with eng.Fori(0, n - 1) as i:
                body(i, False)
            body(n - 1, True)

        def steps3(eng, n, body):
            body(0, True, False)
            with eng.Fori(1, n - 1) as i:
                body(i, False, False)
            body(n - 1, False, True)

        A = Signals("attn0")
        C1 = Signals("attn1")

        def ln_stats(v, s, it):
            for t in range(T):
                ins = nc.vector.bn_stats(stats[:, t, :], xt(it * T + t))
            ins.then_inc(s["bn"], 1)
            v.wait_ge(s["bn"], apart(v, it + 1))
            for t in range(T):
                ins = nc.vector.bn_aggr(mv[:, t, :], stats[:, t, :])
            ins.then_inc(s["stats"], 1)

        def ln_rstd(p, s, it):
            p.wait_ge(s["stats"], it + 1)
            nc.gpsimd.tensor_tensor(var_eps[:, :], mv[:, :, 1], eps[:, 0:T], ALU.add).then_inc(s["eps"], 1)
            p.wait_ge(s["eps"], it + 1)
            nc.gpsimd.tensor_tensor(rstd[:, :], var_eps[:, :], neg_half[:, 0:T], ALU.pow).then_inc(s["rstd"], 1)

        def rstd_of_all(p, s):
            p.wait_ge(s["mv_all"], B)
            nc.gpsimd.tensor_tensor(var_all[:, :], mv_all[:, :, 1], eps[:, :], ALU.add).then_inc(s["eps"], 1)
            p.wait_ge(s["eps"], B + 1)
            nc.gpsimd.tensor_tensor(rstd_all[:, :], var_all[:, :], neg_half[:, :], ALU.pow).then_inc(s["rstd"], 1)

        def apply_all(i, t, dst):
            return nc.vector.tensor_scalar(dst, xt(i * T + t),
                                           mv_all[:, ds(i * T + t, 1), 0:1].rearrange("p o c -> p (o c)"),
                                           rstd_all[:, ds(i * T + t, 1)], ALU.subtract, ALU.mult)

        def ln_apply(v, s, it, dst):
            v.wait_ge(s["rstd"], it + 1)
            for t in range(T):
                ins = nc.vector.tensor_scalar(dst(t), xt(it * T + t), mv[:, t, 0:1], rstd[:, t:t + 1],
                                              ALU.subtract, ALU.mult)
            ins.then_inc(s["xn"], 1)

        def attn_pe(pe, s, wq, wk, wv, wo):
            def transposes(it):
                pe.wait_ge(s["xn"], it + 1)
                for t in range(T):
                    ins = nc.tensor.transpose(bank[0][:, t * P:(t + 1) * P], xn[:, t, :], W("ident"))
                ins.then_inc(s["xT_ps"], 1)

            def qk(it):
                pe.wait_ge(s["xT"], it + 1)
                nc.tensor.matmul(bank[1][:, :], wq, xnT[:, :], start=True, stop=True).then_inc(s["q_ps"], 1)
                if wo is not None:
                    pe.wait_ge(s["ot"], it * T)
                nc.tensor.matmul(bank[2][:, :], wk, xnT[:, :], start=True, stop=True).then_inc(s["k_ps"], 1)

            def values(it):
                for t in range(T):
                    ins = nc.tensor.matmul(bank[3][:, t * D:(t + 1) * D], xnT[:, t * P:(t + 1) * P], wv,
                                           start=True, stop=True)
                ins.then_inc(s["v_ps"], 1)

            def scores(it, t):
                if t == 0:
                    pe.wait_ge(s["q"], it + 1)
                    pe.wait_ge(s["k"], it + 1)
                if t >= 2:
                    pe.wait_ge(s["p"], it * T + t - 1)
                nc.tensor.matmul(bank[4 + t % 2][:, :], qT[:, t * P:(t + 1) * P], kT[:, :],
                                 start=True, stop=True).then_inc(s["s_ps"], 1)

            def turn(it, t):
                pe.wait_ge(s["p"], it * T + t + 1)
                if t >= 2:
                    pe.wait_ge(s["pt"], it * T + t - 1)
                for c in range(T):
                    ins = nc.tensor.transpose(bank[6 + t % 2][:, c * P:(c + 1) * P],
                                              pr[:, t % 2, c * P:(c + 1) * P], W("ident"))
                ins.then_inc(s["pt_ps"], 1)

            def mix(it, t):
                pe.wait_ge(s["pt"], it * T + t + 1)
                if t == 0:
                    pe.wait_ge(s["v"], it + 1)
                if t >= 2:
                    pe.wait_ge(s["ot"], it * T + t - 1)
                for c in range(T):
                    ins = nc.tensor.matmul(bank[1 + t % 2][:, 0:P], vv[:, c, :], prT[:, t % 2, c * P:(c + 1) * P],
                                           start=(c == 0), stop=(c == T - 1))
                ins.then_inc(s["ot_ps"], 1)

            def z_bank(it, t):
                if t == 1:
                    pe.wait_ge(s["x_out"], it * T + 1)
                if t == 3:
                    pe.wait_ge(s["x_out"], it * T + 2)
                if t == 2:
                    pe.wait_ge(s["x_out"], it * T + 1)
                return bank[0 if t % 2 else 3][:, 0:D]

            def project(it, t):
                pe.wait_ge(s["ot"], it * T + t + 1)
                nc.tensor.matmul(z_bank(it, t), oT[:, t % 2, :], wo, start=True, stop=True).then_inc(s["z_ps"], 1)

            def mix_rows(it, t):
                pe.wait_ge(s["pt"], it * T + t + 1)
                if t == 0:
                    pe.wait_ge(s["v"], it + 1)
                z = z_bank(it, t)
                for c in range(T):
                    ins = nc.tensor.matmul(z, prT[:, t % 2, c * P:(c + 1) * P], vv[:, c, :],
                                           start=(c == 0), stop=(c == T - 1))
                ins.then_inc(s["z_ps"], 1)

            lag = 3 if wo is not None else 2

            def body(it, last):
                for k in range(T + 3):
                    if k < T:
                        scores(it, k)
                    if 0 <= k - 1 < T:
                        turn(it, k - 1)
                    if 0 <= k - 2 < T:
                        if wo is not None:
                            mix(it, k - 2)
                        else:
                            if k - 2 == 3 and not last:
                                pe.wait_ge(s["xT"], it + 2)
                            mix_rows(it, k - 2)
                    if wo is not None and 0 <= k - 3 < T:
                        if k - 3 == 3 and not last:
                            pe.wait_ge(s["xT"], it + 2)
                        project(it, k - 3)
                    if k == T and not last:
                        pe.wait_ge(s["x_out"], it * T + 2)
                        transposes(it + 1)
                    if k == T + 1 and not last:
                        if wo is not None:
                            pe.wait_ge(s["ot"], it * T + 3)
                        qk(it + 1)
                if not last:
                    pe.wait_ge(s["x_out"], it * T + 3)
                    values(it + 1)

            pe.wait_ge(consts, 48)
            transposes(0)
            pe.wait_ge(s["xT"], 1)
            nc.tensor.matmul(bank[1][:, :], wq, xnT[:, :], start=True, stop=True).then_inc(s["q_ps"], 1)
            nc.tensor.matmul(bank[2][:, :], wk, xnT[:, :], start=True, stop=True).then_inc(s["k_ps"], 1)
            values(0)
            steps(pe, B, body)

        def attn_act(act, s, bq, o):
            def x_copy(it, first=False):
                act.wait_ge(s["xT_ps"], it + 1)
                if not first:
                    act.wait_ge(s["v_ps"], it)
                nc.scalar.copy(xnT[:, :], bank[0][:, :]).then_inc(s["xT"], 1)

            def q_copy(it):
                act.wait_ge(s["q_ps"], it + 1)
                nc.scalar.activation(qT[:, :], bank[1][:, :], ACT.Identity, bias=bq if bq is not None else 0.0
                                     ).then_inc(s["q"], 1)

            def body(it, last):
                for k in range(T + 3):
                    if k < T:
                        act.wait_ge(s["nmax"], it * T + k + 1)
                        if k >= 2:
                            act.wait_ge(s["pt_ps"], it * T + k - 1)
                        nc.scalar.activation(pr[:, k % 2, :], bank[4 + k % 2][:, :], ACT.Exp, bias=nmax[:, k:k + 1],
                                             accum_out=rsum[:, k:k + 1]).then_inc(s["p"], 1)
                    if 0 <= k - 1 < T:
                        t = k - 1
                        act.wait_ge(s["pt_ps"], it * T + t + 1)
                        if t >= 2:
                            act.wait_ge(s["ot_ps" if o else "z_ps"], it * T + t - 1)
                        nc.scalar.copy(prT[:, t % 2, :], bank[6 + t % 2][:, :]).then_inc(s["pt"], 1)
                    if o and 0 <= k - 2 < T:
                        t = k - 2
                        act.wait_ge(s["ot_ps"], it * T + t + 1)
                        if t >= 2:
                            act.wait_ge(s["z_ps"], it * T + t - 1)
                        nc.scalar.copy(oT[:, t % 2, :], bank[1 + t % 2][:, 0:P]).then_inc(s["ot"], 1)
                    if k == T and not last:
                        x_copy(it + 1)
                    if k == T + 1 and not last:
                        q_copy(it + 1)

            act.wait_ge(consts, 48)
            x_copy(0, True)
            q_copy(0)
            steps(act, B, body)

        def attn_dve(v, s, bk, bv, mask, o):
            def k_copy(it):
                v.wait_ge(s["k_ps"], it + 1)
                if mask is not None:
                    nc.vector.scalar_tensor_tensor(out=kT[:, :], in0=bank[2][:, :], scalar=bk, in1=mask,
                                                   op0=ALU.add, op1=ALU.mult).then_inc(s["k"], 1)
                else:
                    nc.vector.tensor_scalar(kT[:, :], bank[2][:, :], float(D) ** -0.5, None,
                                            ALU.mult).then_inc(s["k"], 1)

            def v_copy(it):
                v.wait_ge(s["v_ps"], it + 1)
                if bv is not None:
                    nc.vector.tensor_tensor(vv[:, :, :], bank3(3, T, D), bv.unsqueeze(1).broadcast_to([P, T, D]),
                                            ALU.add).then_inc(s["v"], 1)
                else:
                    nc.vector.tensor_copy(vv[:, :, :], bank3(3, T, D)).then_inc(s["v"], 1)

            def final(it, t):
                if t == 0:
                    if o:
                        v.wait_ge(s["xb"], it + 1)
                    v.wait_ge(s["p"], (it + 1) * T)
                    nc.vector.reciprocal(rinv[:, :], rsum[:, :]).then_inc(s["rinv"], 1)
                    v.wait_ge(s["rinv"], it + 1)
                v.wait_ge(s["z_ps"], it * T + t + 1)
                nc.vector.scalar_tensor_tensor(out=xt(it * T + t), in0=bank[0 if t % 2 else 3][:, 0:D],
                                               scalar=rinv[:, t:t + 1], in1=xt(it * T + t),
                                               op0=ALU.mult, op1=ALU.add).then_inc(s["x_out"], 1)

            def body(it, last):
                for k in range(T + 3):
                    if k < T:
                        v.wait_ge(s["s_ps"], it * T + k + 1)
                        nc.vector.tensor_reduce(nmax[:, k:k + 1], bank[4 + k % 2][:, :], AX, ALU.max,
                                                negate=True).then_inc(s["nmax"], 1)
                    if k == 1 and not last:
                        v.wait_ge(s["x_loaded"], apart(v, 16 * (it + 2)))
                        ln_stats(v, s, it + 1)
                    if k == T - 1 and not last:
                        v.wait_ge(s["xT_ps"], it + 1)
                        ln_apply(v, s, it + 1, lambda t: xn[:, t, :])
                    first = 3 if o else 2
                    if k - first in range(T) and k >= T - 1 or (not o and k == T - 1):
                        if not o and k == T - 1:
                            final(it, 0)
                            final(it, 1)
                        else:
                            final(it, k - first)
                    if k == T + 1 and not last:
                        k_copy(it + 1)
                v.wait_ge(s["x_out"], apart(v, (it + 1) * T))
                for t in range(T):
                    ins = nc.vector.bn_stats(stats2[:, t, :], xt(it * T + t))
                ins.then_inc(s["bn2"], 1)
                v.wait_ge(s["bn2"], apart(v, it + 1))
                for t in range(T):
                    ins = nc.vector.bn_aggr(mv2[:, t, :], stats2[:, t, :])
                ins.then_inc(s["mv2"], 1)
                v.wait_ge(s["mv2"], it + 1)
                nc.vector.tensor_copy(mv_all[:, ds(it * T, T), :], mv2[:, :, :]).then_inc(s["mv_all"], 1)
                if not last:
                    if o:
                        v.wait_ge(s["ot_ps"], (it + 1) * T)
                    v_copy(it + 1)

            v.wait_ge(s["x_loaded"], 16)
            ln_stats(v, s, 0)
            ln_apply(v, s, 0, lambda t: xn[:, t, :])
            v.wait_ge(consts, 48)
            k_copy(0)
            v_copy(0)
            steps(v, B, body)

        def attn_pool(p, s, bo):
            def body(it, last):
                ln_rstd(p, s, it)
                if bo is not None:
                    p.wait_ge(s["xn"], it + 1)
                    nc.gpsimd.tensor_tensor(x4(it), x4(it), bo.unsqueeze(1).broadcast_to([P, T, D]), ALU.add
                                            ).then_inc(s["xb"], 1)
            steps(p, B, body)

        def attn_sp(sp, s, src):
            def body(it, first, last):
                if not first:
                    sp.wait_ge(s["x_loaded"], 16 * it)
                sp.dma_start(x4(it), src[ds(it * S, S), :].rearrange("(t p) d -> p t d", p=P)
                             ).then_inc(s["x_loaded"], 16)
            steps3(sp, B, body)

        GL = Signals("gate0")

        def gate_dve(v, s):
            v.wait_ge(A["rstd"], B + 1)

            def body(i, first, last):
                for slot in range(2):
                    u = 2 * i + slot
                    if not first:
                        v.wait_ge(s[f"rows{slot}"], 16 * i)
                        v.wait_ge(s["xT_ps"], u - 1)
                    for t in range(T):
                        ins = apply_all(u, t, xg[:, slot, t, :])
                    ins.then_inc(s["xn"], 1)
                for slot in range(2):
                    u = 2 * i + slot
                    v.wait_ge(s["lg_ps"], u + 1)
                    nc.vector.tensor_tensor(lg[:, ds(u * T, T), :], bank3(4 * slot + 1, T, E0),
                                            R("bg0").rearrange("p (t e) -> p t e", t=T), ALU.add).then_inc(s["lg"], 1)
            steps3(v, B // 2, body)

        def gate_pe(pe, s):
            def body(i, first, last):
                for slot in range(2):
                    u = 2 * i + slot
                    pe.wait_ge(s["xn"], u + 1)
                    if not first:
                        pe.wait_ge(s["xT"], u - 1)
                    for t in range(T):
                        ins = nc.tensor.transpose(bank[4 * slot][:, t * P:(t + 1) * P], xg[:, slot, t, :], W("ident"))
                    ins.then_inc(s["xT_ps"], 1)
                for slot in range(2):
                    u = 2 * i + slot
                    pe.wait_ge(s["xT"], u + 1)
                    if not first:
                        pe.wait_ge(s["lg"], u - 1)
                    for t in range(T):
                        ins = nc.tensor.matmul(bank[4 * slot + 1][:, t * E0:(t + 1) * E0], xgT[:, slot, t * P:(t + 1) * P],
                                               W("g0"), start=True, stop=True)
                    ins.then_inc(s["lg_ps"], 1)
            steps3(pe, B // 2, body)

        def gate_act(act, s):
            def body(i, first, last):
                for slot in range(2):
                    u = 2 * i + slot
                    act.wait_ge(s["xT_ps"], u + 1)
                    if not first:
                        act.wait_ge(s["lg_ps"], u - 1)
                    nc.scalar.copy(xgT[:, slot, :], bank[4 * slot][:, :]).then_inc(s["xT"], 1)
            steps3(act, B // 2, body)

        def gate_sp(sp, s):
            def body(it, last):
                sp.wait_ge(A["x_out"], T * (it + 1))
                sp.dma_start(x2d[ds(it * S, S), :].rearrange("(t p) d -> p t d", p=P), x4(it)).then_inc(s["x2"], 16)
                sp.dma_start(table0[ds(it * S, S), D:2 * D].rearrange("(t p) d -> p t d", p=P), x4(it)
                             ).then_inc(s["x2"], 16)
            steps(sp, B, body)

            def rows(i, last):
                for slot in range(2):
                    u = 2 * i + slot
                    sp.wait_ge(s["xn"], u + 1)
                    sp.dma_start(table0[ds(u * S, S), 0:D].rearrange("(t p) d -> p t d", p=P), xg[:, slot, :, :]
                                 ).then_inc(s[f"rows{slot}"], 16)
            steps(sp, B // 2, rows)

        class Line:
            def __init__(self, eng, s):
                self.eng, self.s, self.n = eng, s, 0

            def __call__(self, ins):
                self.n += 1
                ins.then_inc(self.s, 1)
                self.eng.wait_ge(self.s, self.n)

        RT0 = Signals("route0")
        RT1 = Signals("route1")

        def places(v, s, then, e, pos_out):
            v.wait_ge(s["cnt_ps"], 1)
            a, b = wide[0][:, :, 0:e], wide[1][:, :, 0:e]
            then(nc.vector.tensor_copy(a, bank3(1, NT, e)))
            step = 1
            while step < NT:
                nc.vector.tensor_copy(b[:, 0:step, :], a[:, 0:step, :])
                then(nc.vector.tensor_tensor(b[:, step:, :], a[:, step:, :], a[:, 0:NT - step, :], ALU.add))
                a, b = b, a
                step *= 2
            c, d = wide[2][:, :, 0:e], wide[3][:, :, 0:e]
            nc.vector.tensor_copy(c[:, 0:1, :], bank3(0, NT, e)[:, 0:1, :])
            then(nc.vector.tensor_tensor(c[:, 1:, :], bank3(0, NT, e)[:, 1:, :], a[:, 0:NT - 1, :], ALU.add))
            then(nc.vector.tensor_tensor(d, c, oh[:, :, 0:e], ALU.mult))
            then(nc.vector.tensor_reduce(pos_out, d, AX, ALU.add))
            return a

        def slots(v, s, then, cols, n_vals):
            iota = R("iota")
            for c in range(4):
                part = slice(c * NT // 4, (c + 1) * NT // 4)
                nc.vector.tensor_tensor(at_place[:, part, :], iota.unsqueeze(1).broadcast_to([P, NT // 4, P]),
                                        bcast(one["p16"][:, part], P), ALU.is_equal).then_inc(s["a"], 1)
            w = at_place[:, 0, :]
            first = at_col[:, :, 0, 0:cols]
            hot = at_col[:, :, 1, 0:cols]
            then(nc.vector.tensor_tensor(hot, iota[:, 0:cols].unsqueeze(1).broadcast_to([P, NT, cols]),
                                         bcast(one["col"][:, :], cols), ALU.is_equal))
            nc.vector.tensor_tensor(first, hot, bcast(R("tile"), cols), ALU.mult)
            for k in range(3 if n_vals == 5 else 0):
                nc.vector.tensor_tensor(at_col[:, :, 2 + k, 0:cols], hot, bcast(gpiece[:, k, :], cols), ALU.mult)
            nc.vector.tensor_scalar(hot, hot, R("place"), None, ALU.mult).then_inc(s["b"], 1)

        def slots_pe(pe, s, cols, n_vals):
            pe.wait_ge(s["b"], 1)
            dst = bank[2][:, 0:n_vals * cols].rearrange("p (n c) -> p n c", n=n_vals)
            for t in range(NT):
                if t % (NT // 4) == 0:
                    pe.wait_ge(s["a"], t // (NT // 4) + 1)
                ins = nc.tensor.matmul(dst, at_place[:, t, :], at_col[:, t, 0:n_vals, 0:cols],
                                       start=(t == 0), stop=(t == NT - 1))
            ins.then_inc(s["ids_ps"], 1)

        def counts_pe(pe, s, e):
            pe.wait_ge(s["oh"], 1)
            nc.tensor.matmul(bank3(0, NT, e), C("tri"), oh[:, :, 0:e], start=True, stop=True)
            nc.tensor.matmul(bank3(1, NT, e), C("ones"), oh[:, :, 0:e], start=True, stop=True).then_inc(s["cnt_ps"], 1)

        def ids_out(v, s, then, cols, n_vals):
            v.wait_ge(s["ids_ps"], 1)
            src = bank[2][:, 0:n_vals * cols].rearrange("p (n c) -> p n c", n=n_vals)
            then(nc.vector.tensor_copy(vals[:, 0:n_vals, 0:cols], src))
            nc.vector.tensor_scalar(padm[:, 0:cols], vals[:, 1, 0:cols], 0.0, float(PAD), ALU.is_equal, ALU.mult)
            if n_vals == 5:
                then(nc.vector.scalar_tensor_tensor(out=gsum[:, 0:cols], in0=vals[:, 4, 0:cols], scalar=2.0 ** -12,
                                                    in1=vals[:, 3, 0:cols], op0=ALU.mult, op1=ALU.add))
                then(nc.vector.scalar_tensor_tensor(out=gslot[:, 0:cols], in0=gsum[:, 0:cols], scalar=2.0 ** -12,
                                                    in1=vals[:, 2, 0:cols], op0=ALU.mult, op1=ALU.add))
            then(nc.vector.scalar_tensor_tensor(out=idf[:, 0:cols], in0=vals[:, 0, 0:cols], scalar=float(P),
                                                in1=vals[:, 1, 0:cols], op0=ALU.mult, op1=ALU.add))
            nc.vector.scalar_tensor_tensor(out=ids_all[:, 0:cols], in0=idf[:, 0:cols], scalar=-1.0, in1=padm[:, 0:cols],
                                           op0=ALU.add, op1=ALU.add).then_inc(s["ids"], 1)

        def route0_dve(v, s):
            then = Line(v, s["line"])
            rev = R("rev0").unsqueeze(1).broadcast_to([P, NT, E0])
            v.wait_ge(GL["lg"], B)
            then(nc.vector.tensor_reduce(one["lmax"][:, :], lg[:, :, :], AX, ALU.max))
            nc.vector.tensor_tensor(wide[3][:, :, :], lg[:, :, :], bcast(one["lmax"][:, :], E0), ALU.subtract
                                    ).then_inc(s["lsh"], 1)
            then(nc.vector.tensor_tensor(wide[0][:, :, :], lg[:, :, :], bcast(one["lmax"][:, :], E0), ALU.is_equal))
            then(nc.vector.tensor_tensor(wide[1][:, :, :], wide[0][:, :, :], rev, ALU.mult))
            then(nc.vector.tensor_reduce(one["best"][:, :], wide[1][:, :, :], AX, ALU.max))
            nc.vector.tensor_tensor(oh[:, :, :], rev, bcast(one["best"][:, :], E0), ALU.is_equal).then_inc(s["oh"], 1)
            v.wait_ge(s["ex"], 1)
            then(nc.vector.tensor_reduce(one["lsum"][:, :], wide[2][:, :, :], AX, ALU.add))
            then(nc.vector.reciprocal(one["gate"][:, :], one["lsum"][:, :]))
            then(nc.vector.tensor_copy(gpiece[:, 0, :], one["gate"][:, :]))
            then(nc.vector.tensor_tensor(one["rest"][:, :], one["gate"][:, :], gpiece[:, 0, :], ALU.subtract))
            then(nc.vector.tensor_scalar(gpiece[:, 1, :], one["rest"][:, :], 4096.0, None, ALU.mult))
            then(nc.vector.scalar_tensor_tensor(out=one["rest2"][:, :], in0=one["rest"][:, :], scalar=4096.0,
                                                in1=gpiece[:, 1, :], op0=ALU.mult, op1=ALU.subtract))
            then(nc.vector.tensor_scalar(gpiece[:, 2, :], one["rest2"][:, :], 4096.0, None, ALU.mult))
            places(v, s, then, E0, one["pos"][:, :])
            then(nc.vector.tensor_scalar(one["late"][:, :], one["pos"][:, :], float(P), None, ALU.is_ge))
            then(nc.vector.scalar_tensor_tensor(out=one["p16"][:, :], in0=one["late"][:, :], scalar=-float(P),
                                                in1=one["pos"][:, :], op0=ALU.mult, op1=ALU.add))
            then(nc.vector.scalar_tensor_tensor(out=one["ef"][:, :], in0=one["best"][:, :], scalar=-2.0,
                                                in1=one["late"][:, :], op0=ALU.mult, op1=ALU.add))
            then(nc.vector.tensor_scalar(one["col"][:, :], one["ef"][:, :], 2.0 * E0, None, ALU.add))
            slots(v, s, then, 2 * E0, 5)
            ids_out(v, s, then, 2 * E0, 5)

        def route0_act(act, s):
            act.wait_ge(s["lsh"], 1)
            nc.scalar.activation(wide[2][:, :, :], wide[3][:, :, :], ACT.Exp).then_inc(s["ex"], 1)

        X0 = Signals("exp0")

        def turns(eng, n, body):
            steps3(eng, n // NX, body)

        def back(i, j, k):
            slot = (j - k) % NX
            turn = i + (j - k - slot) // NX
            return NX * turn + slot, turn, slot

        def has(i, j, k, first, last):
            return not (first and j - k < 0) and not (last and j - k >= NX)

        def expert_pool(p, s, table, dest, before, n, lag):
            def gather(at, slot):
                for t in range(2):
                    nc.gpsimd.indirect_dma_start(
                        out=rg[:, slot, t, :], out_offset=None, in_=table,
                        in_offset=bass.IndirectOffsetOnAxis(ap=at[:, t:t + 1], axis=0),
                        bounds_check=N - 1, oob_is_err=False).then_inc(s[f"g{slot}"], 16)

            def move(u, slot, free, new):
                if new is None:
                    nc.gpsimd.tensor_copy(raw[:, slot, 0, :], ids_all[:, ds(u * 2, 2)]).then_inc(s["raw"], 1)
                else:
                    far = NX + lag
                    nc.gpsimd.tensor_copy(raw[:, slot, :, :], ids_all[:, ds(u * 2, 2 * far + 2)].rearrange(
                        "p (k c) -> p k c", c=2)[:, 0:far + 1:far, :]).then_inc(s["raw"], 1)
                done = u + 1
                p.wait_ge(s["yo"], done)
                p.wait_ge(s["raw"], done)
                if new is not None and lag:
                    p.wait_ge(s["pre"], done + lag)
                    p.wait_ge(s["xT_ps"], done + lag)
                nc.gpsimd.tensor_tensor(ids[:, slot, :, :], raw[:, slot, :, :], zero_i[:, :, :], ALU.add
                                        ).then_inc(s["ids"], 1)
                p.wait_ge(ready, READY)
                p.wait_ge(s["ids"], done)
                if new is not None:
                    gather(ids[:, slot, 1, :], free)
                for t in range(2):
                    nc.gpsimd.indirect_dma_start(
                        out=dest, out_offset=bass.IndirectOffsetOnAxis(ap=ids[:, slot, 0, t:t + 1], axis=0),
                        in_=yo[:, slot, t, :], in_offset=None,
                        bounds_check=N - 1, oob_is_err=False).then_inc(s[f"s{slot}"], 16)

            def deviation(u, slot):
                p.wait_ge(s["st"], u + 1)
                nc.gpsimd.tensor_tensor(ve1[:, :], mv1[:, slot % 2, :, 1], eps[:, 0:2], ALU.add).then_inc(s["eps"], 1)
                p.wait_ge(s["eps"], u + 1)
                nc.gpsimd.tensor_tensor(rs1[:, slot % 2, :], ve1[:, :], neg_half[:, 0:2], ALU.pow).then_inc(s["rs"], 1)

            def body(i, first, last):
                for j in range(NX + (lag if last else 0)):
                    if lag and j < NX:
                        if first and j == 0:
                            p.wait_ge(s["pre"], 1)
                            p.wait_ge(s["xT_ps"], 1)
                            gather(ids_all[:, 2 * NX:2 * NX + 2], 0)
                        deviation(NX * i + j, j)
                    if has(i, j, lag, first, last):
                        u, _, slot = back(i, j, lag)
                        move(u, slot, j % NX, None if last else u + NX + lag)

            before(p)
            for slot in range(NX):
                gather(ids_all[:, 2 * slot:2 * slot + 2], slot)
            turns(p, n, body)

        def expert_sp(sp, s, pack, which, n, before):
            before(sp)

            def load(u, slot):
                sp.dma_start(wx[:, slot, :], pack[ds(which(sp, u), 1), :, :].rearrange("o p w -> (o p) w")
                             ).then_inc(s[f"w{slot}"], 16)

            def body(i, last):
                for slot in range(NX):
                    u = NX * i + slot
                    if not last:
                        sp.wait_ge(s["yb"], apart(sp, u + 1))
                        load(u + NX, slot)
            for slot in range(NX):
                load(slot, slot)
            steps(sp, n // NX, body)

        def expert_pe(pe, s, n):
            def turn(u, i, slot):
                pe.wait_ge(s[f"g{slot}"], 32 * (i + 1))
                for t in range(2):
                    ins = nc.tensor.transpose(bank[4 * (slot % 2)][:, t * P:(t + 1) * P], rg[:, slot, t, 0:D], W("ident"))
                ins.then_inc(s["xT_ps"], 1)

            def hidden(u, i, slot):
                pe.wait_ge(s["xT"], u + 1)
                pe.wait_ge(s[f"w{slot}"], 16 * (i + 1))
                for c in range(HC):
                    ins = nc.tensor.matmul(bank[4 * (slot % 2) + 1 + c // 2][:, (c % 2) * PAIR:(c % 2 + 1) * PAIR],
                                           wx[:, slot, c * P:(c + 1) * P], exT[:, slot % 2, :], start=True, stop=True)
                    if c % 2:
                        ins.then_inc(s["hb_ps" if c > 1 else "ha_ps"], 1)

            def outer(u, slot, first):
                if not first:
                    pe.wait_ge(s["yb"], u - 1)
                for t in range(2):
                    for c in range(HC):
                        if t == 0 and c % 2 == 0:
                            pe.wait_ge(s["hb" if c else "ha"], u + 1)
                        ins = nc.tensor.matmul(bank[4 * (slot % 2) + 3][:, t * D:(t + 1) * D],
                                               hT[:, slot % 2, c, t * P:(t + 1) * P],
                                               wx[:, slot, H + c * D:H + (c + 1) * D], start=(c == 0), stop=(c == HC - 1))
                ins.then_inc(s["y_ps"], 1)

            def body(i, first, last):
                for j in range(NX + 1 if last else NX):
                    if j < NX:
                        hidden(NX * i + j, i, j)
                    if has(i, j, -1, first, last):
                        turn(*back(i, j, -1))
                    if has(i, j, 1, first, last):
                        u, _, slot = back(i, j, 1)
                        outer(u, slot, first and j < 3)
            turn(0, 0, 0)
            turns(pe, n, body)

        def expert_act(act, s, n):
            def rows_copy(u, slot):
                act.wait_ge(s["xT_ps"], u + 1)
                nc.scalar.copy(exT[:, slot % 2, :], bank[4 * (slot % 2)][:, 0:PAIR]).then_inc(s["xT"], 1)

            def body(i, first, last):
                for j in range(NX):
                    u = NX * i + j
                    act.wait_ge(s["ha_ps"], u + 1)
                    for c in range(2):
                        ins = nc.scalar.activation(hT[:, j % 2, c, :], bank[4 * (j % 2) + 1][:, c * PAIR:(c + 1) * PAIR],
                                                   ACT.Relu, bias=wx[:, j, H + HC * D + c:H + HC * D + c + 1])
                    ins.then_inc(s["ha"], 1)
                    if has(i, j, -1, first, last):
                        u, _, slot = back(i, j, -1)
                        rows_copy(u, slot)
            rows_copy(0, 0)
            turns(act, n, body)

        def relu_half(v, s, u, slot):
            v.wait_ge(s["hb_ps"], u + 1)
            for c in range(2, HC):
                ins = nc.vector.tensor_scalar(hT[:, slot % 2, c, :], bank[4 * (slot % 2) + 2][:, (c - 2) * PAIR:(c - 1) * PAIR],
                                              wx[:, slot, H + HC * D + c:H + HC * D + c + 1], 0.0, ALU.add, ALU.max)
            ins.then_inc(s["hb"], 1)

        def expert_dve0(v, s, n):
            def rows(u, i, slot, first):
                v.wait_ge(s["y_ps"], u + 1)
                nc.vector.tensor_tensor(yb[:, slot % 2, :, :], bank3(4 * (slot % 2) + 3, 2, D),
                                        wx[:, slot, WP - D:WP].unsqueeze(1).broadcast_to([P, 2, D]), ALU.add
                                        ).then_inc(s["yb"], 1)
                v.wait_ge(s["yb"], u + 1)
                if not first:
                    v.wait_ge(s[f"s{slot}"], 32 * i)
                for t in range(2):
                    ins = nc.vector.scalar_tensor_tensor(out=yo[:, slot, t, :], in0=yb[:, slot % 2, t, :],
                                                         scalar=gslot[:, ds(u * 2 + t, 1)],
                                                         in1=rg[:, slot, t, D:2 * D], op0=ALU.mult, op1=ALU.add)
                ins.then_inc(s["yo"], 1)

            def body(i, first, last):
                for j in range(NX):
                    if has(i, j, -1, first, last):
                        u, _, slot = back(i, j, -1)
                        relu_half(v, s, u, slot)
                    rows(NX * i + j, i, j, first)
            relu_half(v, s, 0, 0)
            turns(v, n, body)

        def expert_dve1(v, s, n):
            def ahead(u, i, slot):
                v.wait_ge(s[f"g{slot}"], 32 * (i + 1))
                v.wait_ge(s[f"w{slot}"], 16 * (i + 1))
                nc.vector.tensor_tensor(pre[:, slot % 2, :, :], rg[:, slot, :, 0:D],
                                        wx[:, slot, WP - D:WP].unsqueeze(1).broadcast_to([P, 2, D]), ALU.add)
                nc.vector.tensor_tensor(bx[:, slot % 2, :, :], rg[:, slot, :, D:2 * D],
                                        R("b2").unsqueeze(1).broadcast_to([P, 2, D]), ALU.add).then_inc(s["pre"], 1)

            def statistics(u, i, slot):
                v.wait_ge(s["y_ps"], u + 1)
                v.wait_ge(s["pre"], u + 1)
                nc.vector.tensor_tensor(yr[:, slot % 2, :, :], bank3(4 * (slot % 2) + 3, 2, D), pre[:, slot % 2, :, :],
                                        ALU.add).then_inc(s["yb"], 1)
                v.wait_ge(s["yb"], u + 1)
                for t in range(2):
                    ins = nc.vector.bn_stats(st1[:, t, :], yr[:, slot % 2, t, :])
                ins.then_inc(s["bn"], 1)
                v.wait_ge(s["bn"], apart(v, u + 1))
                for t in range(2):
                    ins = nc.vector.bn_aggr(mv1[:, slot % 2, t, :], st1[:, t, :])
                ins.then_inc(s["st"], 1)
                v.wait_ge(s["st"], u + 1)
                for t in range(2):
                    ins = nc.vector.scalar_tensor_tensor(out=yn[:, slot % 2, t, :], in0=yr[:, slot % 2, t, :],
                                                         scalar=mv1[:, slot % 2, t, 0:1], in1=R("g2"),
                                                         op0=ALU.subtract, op1=ALU.mult)
                ins.then_inc(s["yn"], 1)

            def normalised(u, i, slot, first):
                v.wait_ge(s["rs"], u + 1)
                v.wait_ge(s["yn"], u + 1)
                if not first:
                    v.wait_ge(s[f"s{slot}"], 32 * i)
                for t in range(2):
                    ins = nc.vector.scalar_tensor_tensor(out=yo[:, slot, t, :], in0=yn[:, slot % 2, t, :],
                                                         scalar=rs1[:, slot % 2, t:t + 1], in1=bx[:, slot % 2, t, :],
                                                         op0=ALU.mult, op1=ALU.add)
                ins.then_inc(s["yo"], 1)

            def body(i, first, last):
                for j in range(NX):
                    if has(i, j, -2, first, last):
                        u, turn, slot = back(i, j, -2)
                        relu_half(v, s, u, slot)
                    normalised(NX * i + j, i, j, first)
                    if has(i, j, -1, first, last):
                        statistics(*back(i, j, -1))
                    if has(i, j, -2, first, last):
                        ahead(u, turn, slot)
            relu_half(v, s, 0, 0)
            ahead(0, 0, 0)
            relu_half(v, s, 1, 1)
            statistics(0, 0, 0)
            ahead(1, 0, 1)
            turns(v, n, body)

        LEAD = 3
        M = Signals("heads")

        def plan(first, last):
            at = [[(0, "ks", 0, 2), (2, "qs", 0, 2), (3, "V", 0, 0)],
                  [(0, "ks", 0, 3), (2, "qs", 0, 3)], [], []]
            if not first:
                at[0] += [(6, "BT", -1, 0), (8, "BT", -1, 1), (10, "BT", -1, 2), (12, "BT", -1, 3)]
                at[1] += [(10, "AT", -1, 0), (12, "WO", -1, 0)]
                at[2] += [(4, "AT", -1, 1), (6, "WO", -1, 1), (8, "AT", -1, 2), (10, "WO", -1, 2)]
                at[3] += [(5, "AT", -1, 3), (8, "WO", -1, 3)]
            if not last:
                at[1] += [(4, "T", 1, 0), (6, "Q", 1, 0), (8, "K", 1, 0)]
                at[2] += [(0, "ks", 1, 0), (2, "qs", 1, 0)]
                at[3] += [(0, "ks", 1, 1), (2, "qs", 1, 1)]
            for g in range(G - 1 if last else G):
                at[g].append((15, "q2", (g + 1) // G, (g + 1) % G))
            return [sorted(a, key=lambda z: z[0]) for a in at]

        PROLOGUE = [("T", 0, 0), ("Q", 0, 0), ("K", 0, 0), ("ks", 0, 0), ("qs", 0, 0), ("ks", 0, 1), ("qs", 0, 1)]
        EPILOGUE = [("BT", -1, t) for t in range(T)] + [(k, -1, t) for t in range(T) for k in ("AT", "WO")]
        FIRST = sum(len(a) for a in plan(True, False))
        MIDDLE = sum(len(a) for a in plan(False, False))
        START = len(PROLOGUE) + 1

        def misc_base(it, first, last):
            return START if first else it * MIDDLE + (START + FIRST - MIDDLE)

        class Misc:
            def __init__(self, do):
                self.do = do

            def sequence(self, it, first, last, step):
                base, n = misc_base(it, first, last), 0
                for slot, units in enumerate(plan(first, last)):
                    start = n
                    units = list(units)
                    for i in range(16):
                        while units and units[0][0] == i:
                            _, kind, db, k = units.pop(0)
                            self.do(kind, it + db, k, base + n)
                            n += 1
                        step(it, slot, i, base + start, first, last)

        def heads_pe(pe):
            s = M

            def do(kind, b, k, m):
                if m is None or not (type(m) is int and m == 0):
                    pe.wait_ge(s["misc_empty"], m)
                x = bank[7]
                if kind == "T":
                    pe.wait_ge(s["xn"], b + 1)
                    for t in range(T):
                        ins = nc.tensor.transpose(x[:, t * P:(t + 1) * P], xn[:, t, :], W("ident"))
                elif kind in "QK":
                    ins = nc.tensor.matmul(x, W("qh" if kind == "Q" else "kh"), xnT[:, :], start=True, stop=True)
                elif kind == "V":
                    for t in range(T):
                        ins = nc.tensor.matmul(x[:, t * D:(t + 1) * D], xnT[:, t * P:(t + 1) * P], W("vh"),
                                               start=True, stop=True)
                elif kind in ("ks", "qs"):
                    hi, lo = (khi, klo) if kind == "ks" else (qhi, qlo)
                    nc.tensor.matmul(x, C(kind[0] + "A", k), hi[:, :], start=True, stop=False)
                    ins = nc.tensor.matmul(x, C(kind[0] + "B", k), lo[:, :], start=False, stop=True)
                elif kind == "q2":
                    pe.wait_ge(s["nmax"], (b * G + k + 1) * 16)
                    for t in range(T):
                        nc.tensor.matmul(x[:, t * P:(t + 1) * P], mrow[:, k % 2, t, :], C("ident"),
                                         start=(t == 0), stop=False)
                    ins = nc.tensor.matmul(x, C("ident"), qs1[:, k, :], start=False, stop=True)
                elif kind == "BT":
                    pe.wait_ge(s["otm"], (b + 1) * G)
                    for g in range(G):
                        ins = nc.tensor.transpose(x[:, g * P:(g + 1) * P], otm[:, g, k * P:(k + 1) * P], W("ident"))
                elif kind == "AT":
                    ins = nc.tensor.transpose(x[:, 0:P], ath[:, k, :], W("ident"))
                elif kind == "WO":
                    ins = nc.tensor.matmul(x[:, 0:P], atT[:, :], W("oh"), start=True, stop=True)
                ins.then_inc(s["misc_full"], 1)

            def score(n, g, i, start=False):
                if i == 0:
                    pe.wait_ge(s["kpad"], n + 1)
                if not start:
                    pe.wait_ge(s["nmax"], n * 16 + i - 1)
                j, t = i // 4, i % 4
                nc.tensor.matmul(bank[i % 2], qs1[:, g, t * P:(t + 1) * P], kpad[:, g, j, :],
                                 start=True, stop=True).then_inc(s["s_ps"], 1)

            def turned(n, g, i, early):
                c, j = i // 4, i % 4
                if i % 2 == 0 and not (early and i < 4):
                    pe.wait_ge(s["exp"], n * 8 + i // 2 - 1)
                ins = nc.tensor.matmul(bank[2 + i % 4], kpad[:, g, j, c * P:(c + 1) * P], qs2[:, g, :],
                                       start=True, stop=True)
                if i % 2:
                    ins.then_inc(s["st_ps"], 1)

            def mix(n, g, c, early):
                pe.wait_ge(s["exp"], n * 8 + 2 * c + 2)
                if c == 0 and not early:
                    pe.wait_ge(s["otm"], n)
                for j in range(4):
                    ins = nc.tensor.matmul(bank[6][32 * j:32 * j + 32, :], vh[:, c, 4 * g + j, :],
                                           ptm[:, (2 * c + j // 2) % 4, (j % 2) * S:(j % 2 + 1) * S],
                                           start=(c == 0), stop=(c == T - 1))
                ins.then_inc(s["pv"], 1)

            def step(it, g, i, m0, first, last):
                n = it * G + g
                over, k = (i + LEAD) // 16, (i + LEAD) % 16
                if not (last and g + 1 + over >= G):
                    if k == 0:
                        at = [kind for _, kind, _, _ in plan(first, last)[g]].index("qs")
                        pe.wait_ge(s["misc_empty"], m0 + at + 1)
                    score(n + 1 + over, (g + 1 + over) % G, k)
                if i == 0:
                    pe.wait_ge(s["misc_empty"], m0)
                early = first and g == 0
                turned(n, g, i, early)
                if i == 2 and not early:
                    mix(n - 1, (g - 1) % G, 3, False)
                if i in (6, 10, 14):
                    if i == 6 and g == 0:
                        pe.wait_ge(s["misc_empty"], m0 + 3)
                    mix(n, g, (i - 6) // 4, early)

            m = 0
            for kind, b, k in PROLOGUE:
                do(kind, b, k, m)
                m += 1
            for i in range(16 + LEAD):
                if i == 16:
                    pe.wait_ge(s["misc_empty"], len(PROLOGUE))
                score(i // 16, i // 16, i % 16, i < 2)
            do("q2", 0, 0, m)
            misc = Misc(do)
            steps3(pe, B, lambda it, first, last: misc.sequence(it, first, last, step))
            mix(B * G - 1, G - 1, 3, False)
            m = misc_base(B, False, False) - MIDDLE + sum(len(a) for a in plan(False, True))
            for kind, db, k in EPILOGUE:
                do(kind, B + db, k, m)
                m += 1

        def heads_act(act):
            s = M

            def do(kind, b, k, m):
                act_kinds = {"T", "Q", "K", "ks", "qs", "q2", "AT"}
                if kind not in act_kinds:
                    return
                act.wait_ge(s["misc_full"], m + 1)
                x = bank[7]
                if kind == "T":
                    nc.scalar.copy(xnT[:, :], x).then_inc(s["misc_empty"], 1)
                elif kind == "Q":
                    nc.scalar.activation(qhi[:, :], x, ACT.Identity, bias=W("bqh")).then_inc(s["qhi"], 1)
                elif kind == "K":
                    nc.scalar.activation(khi[:, :], x, ACT.Identity, bias=W("bkh")).then_inc(s["khi"], 1)
                elif kind == "ks":
                    if not (type(b) is int and b == 0 and k == 0):
                        act.wait_ge(s["kpad"], b * G + k)
                    nc.scalar.activation(kst[:, :], x, ACT.Identity, bias=W("one24")).then_inc(s["misc_empty"], 1)
                elif kind == "qs":
                    nc.scalar.copy(qs1[:, k, :], x).then_inc(s["misc_empty"], 1)
                elif kind == "q2":
                    nc.scalar.copy(qs2[:, k, :], x).then_inc(s["misc_empty"], 1)
                elif kind == "AT":
                    nc.scalar.copy(atT[:, :], x[:, 0:P]).then_inc(s["misc_empty"], 1)

            def step(it, g, i, m0, first, last):
                n = it * G + g
                if i % 2:
                    q = i // 2
                    act.wait_ge(s["st_ps"], n * 8 + q + 1)
                    if not (first and g == 0 and q < 4):
                        act.wait_ge(s["pv"], n * 4 + q // 2 - 1)
                    nc.scalar.activation(ptm[:, q % 4, :], psum[:, (2 + 2 * (q % 2)) * S:(4 + 2 * (q % 2)) * S], ACT.Exp,
                                         scale=SCALE_H).then_inc(s["exp"], 1)
                if i == 4 and not (first and g == 0):
                    group_out(n - 1, (g - 1) % G)

            def group_out(n, g):
                act.wait_ge(s["pv"], n * 4 + 4)
                nc.scalar.copy(otm[:, g, :], bank[6]).then_inc(s["otm"], 1)

            m = 0
            for kind, b, k in PROLOGUE:
                do(kind, b, k, m)
                m += 1
            do("q2", 0, 0, m)
            misc = Misc(do)
            steps3(act, B, lambda it, first, last: misc.sequence(it, first, last, step))
            group_out(B * G - 1, G - 1)
            m = misc_base(B, False, False) - MIDDLE + sum(len(a) for a in plan(False, True))
            for kind, db, k in EPILOGUE:
                do(kind, B + db, k, m)
                m += 1

        def heads_dve(v):
            s = M

            def do(kind, b, k, m):
                if kind not in {"Q", "K", "V", "BT", "WO"}:
                    return
                x = bank[7]
                if kind in "QK":
                    hi, lo, bias, ev = (qhi, qlo, W("bqh"), "qhi") if kind == "Q" else (khi, klo, W("bkh"), "khi")
                    v.wait_ge(s[ev], b + 1)
                    nc.vector.scalar_tensor_tensor(out=lo[:, :], in0=x, scalar=bias, in1=hi[:, :], op0=ALU.add,
                                                   op1=ALU.subtract).then_inc(s["misc_empty"], 1)
                    return
                v.wait_ge(s["misc_full"], m + 1)
                if kind == "V":
                    nc.vector.tensor_tensor(vh[:, :, :, 0:DH], x.rearrange("p (t h e) -> p t h e", t=T, h=NH),
                                            R("bvh").rearrange("p (h e) -> p h e", h=NH).unsqueeze(1)
                                            .broadcast_to([P, T, NH, DH]), ALU.add).then_inc(s["misc_empty"], 1)
                elif kind == "BT":
                    x3 = x.rearrange("p (h e) -> p h e", h=NH)
                    nc.vector.reciprocal(rch[:, :], x3[:, :, DH]).then_inc(s["rch"], 1)
                    v.wait_ge(s["rch"], b * T + k + 1)
                    nc.vector.tensor_tensor(ath[:, k, :].rearrange("p (h e) -> p h e", h=NH), x3[:, :, 0:DH],
                                            bcast(rch[:, :], DH), ALU.mult).then_inc(s["misc_empty"], 1)
                elif kind == "WO":
                    nc.vector.tensor_tensor(xt(b * T + k, s_all), x[:, 0:D], xt(b * T + k, s_all), ALU.add
                                            ).then_inc(s["misc_empty"], 1)

            def row_max(n, g, i):
                v.wait_ge(s["s_ps"], n * 16 + i + 1)
                j, t = i // 4, i % 4
                nc.vector.tensor_reduce(mrow[:, g % 2, t, 32 * j + 24:32 * j + 25], bank[i % 2], AX, ALU.max, negate=True
                                        ).then_inc(s["nmax"], 1)

            def step(it, g, i, m0, first, last):
                n = it * G + g
                over, k = (i + LEAD) // 16, (i + LEAD) % 16
                if not (last and g + 1 + over >= G):
                    row_max(n + 1 + over, (g + 1 + over) % G, k)

            for kind, b, k in PROLOGUE:
                do(kind, b, k, 0)
            for i in range(16 + LEAD):
                row_max(i // 16, i // 16, i % 16)
            misc = Misc(do)
            steps3(v, B, lambda it, first, last: misc.sequence(it, first, last, step))
            m = misc_base(B, False, False) - MIDDLE + sum(len(a) for a in plan(False, True))
            for kind, db, k in EPILOGUE:
                do(kind, B + db, k, m)
                m += 1
            v.wait_ge(s["misc_empty"], m)

        def heads_pool(p):
            s = M

            def spread(b, g, m):
                p.wait_ge(s["misc_empty"], m + 1)
                nc.gpsimd.tensor_tensor(kpad[:, g, :, :], kst[:, :].unsqueeze(1).broadcast_to([P, 4, S]),
                                        c_all[:, CTOT - 4:CTOT].unsqueeze(2).broadcast_to([P, 4, S]), ALU.mult
                                        ).then_inc(s["kpad"], 1)

            def centred(b):
                nc.gpsimd.tensor_tensor(xn[:, :, :], x4(b),
                                        mv_all[:, ds(b * T, T), 0:1].broadcast_to([P, T, D]), ALU.subtract
                                        ).then_inc(s["xc"], 1)

            def normalised(b):
                p.wait_ge(s["xc"], b + 1)
                nc.gpsimd.tensor_tensor(xn[:, :, :], xn[:, :, :], bcast(rstd_all[:, ds(b * T, T)], D), ALU.mult
                                        ).then_inc(s["xn"], 1)

            def residual(b):
                p.wait_ge(s["xn"], b + 1)
                nc.gpsimd.tensor_tensor(x4(b, s_all), xn[:, :, :], R("boh").unsqueeze(1).broadcast_to([P, T, D]), ALU.add
                                        ).then_inc(s["sres"], 1)

            def do(kind, b, k, m):
                if kind == "ks":
                    spread(b, k, m)

            def step(it, g, i, m0, first, last):
                if g == 0 and not last:
                    if i == 2:
                        centred(it + 1)
                    if i == 4:
                        normalised(it + 1)
                    if i == 7:
                        residual(it + 1)
            p.wait_ge(C1["rstd"], B + 1)
            centred(0)
            normalised(0)
            residual(0)
            for m, (kind, b, k) in enumerate(PROLOGUE):
                do(kind, b, k, m)
            misc = Misc(do)
            steps3(p, B, lambda it, first, last: misc.sequence(it, first, last, step))

        F = Signals("norm1")

        def norm1_dve(v, s):
            for i in range(NT):
                ins = nc.vector.bn_stats(stats3[:, i, :], xt(i, s_all))
            ins.then_inc(s["bn"], 1)
            v.wait_ge(s["bn"], 1)
            for i in range(NT):
                ins = nc.vector.bn_aggr(mv_all[:, i, :], stats3[:, i, :])
            ins.then_inc(s["mv"], 1)
            v.wait_ge(s["rstd"], 1)
            for b in range(B):
                for t in range(T):
                    i = b * T + t
                    ins = nc.vector.tensor_scalar(xt(i, s_all), xt(i, s_all), mv_all[:, i, 0:1], rstd_all[:, i:i + 1],
                                                  ALU.subtract, ALU.mult)
                ins.then_inc(s["xn"], 1)
                v.wait_ge(s["xn"], b + 1)
                nc.vector.tensor_tensor(x4(b, s_all), x4(b, s_all), R("g1").unsqueeze(1).broadcast_to([P, T, D]), ALU.mult
                                        ).then_inc(s["scaled"], 1)
            for b in range(B):
                v.wait_ge(s["x1"], b + 1)
                nc.vector.tensor_tensor(xg[:, b % 2, :, :], x4(b, s_all), R("rw").unsqueeze(1).broadcast_to([P, T, D]),
                                        ALU.mult).then_inc(s["dot"], 1)
                v.wait_ge(s["dot"], b + 1)
                nc.vector.tensor_reduce(one["key"][:, b * T:(b + 1) * T], xg[:, b % 2, :, :], AX, ALU.add
                                        ).then_inc(s["key"], 1)
            v.wait_ge(s["key"], B)

        def norm1_pool(p, s):
            p.wait_ge(s["mv"], 1)
            nc.gpsimd.tensor_tensor(var_all[:, :], mv_all[:, :, 1], eps[:, :], ALU.add).then_inc(s["eps"], 1)
            p.wait_ge(s["eps"], 1)
            nc.gpsimd.tensor_tensor(rstd_all[:, :], var_all[:, :], neg_half[:, :], ALU.pow).then_inc(s["rstd"], 1)
            for b in range(B):
                p.wait_ge(s["scaled"], b + 1)
                nc.gpsimd.tensor_tensor(x4(b, s_all), x4(b, s_all), R("b1").unsqueeze(1).broadcast_to([P, T, D]), ALU.add
                                        ).then_inc(s["x1"], 1)

        def norm1_sp(sp, s):
            for b in range(B):
                sp.wait_ge(C1["x_out"], (b + 1) * T)
                sp.dma_start(table1[b * S:(b + 1) * S, D:2 * D].rearrange("(t p) d -> p t d", p=P), x4(b)
                             ).then_inc(s["table"], 16)
            for b in range(B):
                sp.wait_ge(s["x1"], b + 1)
                sp.dma_start(table1[b * S:(b + 1) * S, 0:D].rearrange("(t p) d -> p t d", p=P), x4(b, s_all)
                             ).then_inc(s["table"], 16)

        def route1_dve(v, s):
            then = Line(v, s["line"])
            o = {n: a[:, :] for n, a in one.items()}
            i = {n: a[:, :] for n, a in oni.items()}
            then(nc.vector.tensor_scalar(o["key"], o["key"], R("rb"), None, ALU.add))
            then(nc.vector.tensor_copy(i["key"], o["key"]))
            then(nc.vector.tensor_copy(o["keyf"], i["key"]))
            then(nc.vector.tensor_tensor(o["gt"], o["keyf"], o["key"], ALU.is_gt))
            then(nc.vector.tensor_tensor(i["floor"], o["keyf"], o["gt"], ALU.subtract))
            then(nc.vector.tensor_scalar(i["e"], i["floor"], E1 - 1, None, ALU.bitwise_and))
            then(nc.vector.tensor_copy(o["ef"], i["e"]))
            nc.vector.tensor_tensor(oh[:, :, 0:E1], R("iota")[:, 0:E1].unsqueeze(1).broadcast_to([P, NT, E1]),
                                    bcast(o["ef"], E1), ALU.is_equal).then_inc(s["oh"], 1)
            sums = places(v, s, then, E1, o["pos"])
            then(nc.vector.tensor_scalar(toti[:, :], sums[:, NT - 1, :], float(PAIR - 1), None, ALU.add))
            then(nc.vector.tensor_scalar(toti[:, :], toti[:, :], 8, None, ALU.logical_shift_right))
            then(nc.vector.tensor_copy(pairs[:, :], toti[:, :]))
            then(nc.vector.memset(starts[:, :], 0.0))
            for e in range(E1 - 1):
                then(nc.vector.tensor_tensor(starts[:, e + 1:e + 2], starts[:, e:e + 1], pairs[:, e:e + 1], ALU.add))
            for e in range(1, E1):
                ins = nc.vector.tensor_scalar(which[:, e - 1, :], R("iota")[:, 0:U1], starts[:, e:e + 1], None, ALU.is_ge)
            then(ins)
            then(nc.vector.tensor_tensor(esum[:, :], which[:, 0, :], which[:, 1, :], ALU.add))
            nc.vector.tensor_tensor(e_of[:, :], esum[:, :], which[:, 2, :], ALU.add).then_inc(s["e_of"], 1)
            then(nc.vector.tensor_copy(i["pos"], o["pos"]))
            nc.vector.tensor_scalar(i["p"], i["pos"], P - 1, None, ALU.bitwise_and)
            then(nc.vector.tensor_scalar(i["j"], i["pos"], 7, None, ALU.logical_shift_right))
            nc.vector.tensor_copy(o["p16"], i["p"])
            then(nc.vector.tensor_copy(o["jf"], i["j"]))
            then(nc.vector.tensor_tensor(wide[3][:, :, 0:E1], oh[:, :, 0:E1],
                                         starts[:, :].unsqueeze(1).broadcast_to([P, NT, E1]), ALU.mult))
            then(nc.vector.tensor_reduce(o["base"], wide[3][:, :, 0:E1], AX, ALU.add))
            then(nc.vector.scalar_tensor_tensor(out=o["col"], in0=o["base"], scalar=2.0, in1=o["jf"],
                                                op0=ALU.mult, op1=ALU.add))
            slots(v, s, then, 2 * U1, 2)
            ids_out(v, s, then, 2 * U1, 2)

        X1 = Signals("exp1")

        block = ctx.enter_context(nc.Block())

        @block.sync
        def _(sp):
            sp.dma_start(r_all[:, :], r_in).then_inc(consts, 16)
            sp.dma_start(c_all[:, :], c_in).then_inc(consts, 16)
            attn_sp(sp, A, x_in)
            gate_sp(sp, GL)
            expert_sp(sp, X0, pack0_in, lambda sp, u: u, U0, lambda sp: None)
            for slot in range(NX):
                sp.wait_ge(X0[f"s{slot}"], 32 * (U0 // NX))
            sp.wait_ge(GL["x2"], 32 * B)
            attn_sp(sp, C1, x2d)
            norm1_sp(sp, F)

            def expert_of(sp, u):
                return sp.value_load(e_of[0:1, ds(u, 1)], min_val=0, max_val=E1 - 1)
            sp.wait_ge(RT1["e_of"], 1)
            expert_sp(sp, X1, pack1_in, expert_of, U1, lambda sp: None)
            for slot in range(NX):
                sp.wait_ge(X1[f"s{slot}"], 32 * (U1 // NX))

        @block.scalar
        def _(act):
            act.dma_start(w_all[:, :], w_in).then_inc(consts, 16)
            attn_act(act, A, W("bq0"), True)
            gate_act(act, GL)
            route0_act(act, RT0)
            expert_act(act, X0, U0)
            attn_act(act, C1, None, False)
            heads_act(act)
            expert_act(act, X1, U1)

        @block.vector
        def _(v):
            nc.vector.memset(rg[:, :, :, :], 0.0).then_inc(ready, 1)
            nc.vector.memset(mrow[:, :, :, :], 0.0).then_inc(ready, 1)
            attn_dve(v, A, W("bk0"), R("bv0"), W("gauss"), True)
            gate_dve(v, GL)
            route0_dve(v, RT0)
            expert_dve0(v, X0, U0)
            attn_dve(v, C1, None, None, None, False)
            heads_dve(v)
            norm1_dve(v, F)
            route1_dve(v, RT1)
            expert_dve1(v, X1, U1)

        @block.gpsimd
        def _(p):
            nc.gpsimd.memset(neg_half[:, :], -0.5).then_inc(ready, 1)
            nc.gpsimd.memset(eps[:, :], EPS).then_inc(ready, 1)
            nc.gpsimd.memset(zero_i[:, :, :], 0).then_inc(ready, 1)
            nc.gpsimd.memset(raw[:, :, :, :], 0).then_inc(ready, 1)
            nc.gpsimd.memset(vh[:, :, :, DH + 1:], 0.0).then_inc(ready, 1)
            nc.gpsimd.memset(vh[:, :, :, DH:DH + 1], 1.0).then_inc(ready, 1)
            p.wait_ge(ready, READY)
            p.wait_ge(consts, 48)
            attn_pool(p, A, R("bo0"))
            rstd_of_all(p, A)

            def before0(p):
                p.wait_ge(RT0["ids"], 1)
                p.wait_ge(GL["x2"], 32 * B)
                for slot in range(2):
                    p.wait_ge(GL[f"rows{slot}"], 16 * (B // 2))
            expert_pool(p, X0, table0, x2d, before0, U0, 0)
            attn_pool(p, C1, None)
            rstd_of_all(p, C1)
            heads_pool(p)
            norm1_pool(p, F)

            def before1(p):
                p.wait_ge(RT1["ids"], 1)
                p.wait_ge(F["table"], 32 * B)
            expert_pool(p, X1, table1, out, before1, U1, 1)

        @block.tensor
        def _(pe):
            attn_pe(pe, A, W("q0"), W("k0"), W("v0"), W("o0"))
            gate_pe(pe, GL)
            counts_pe(pe, RT0, E0)
            slots_pe(pe, RT0, 2 * E0, 5)
            expert_pe(pe, X0, U0)
            attn_pe(pe, C1, W("q1"), W("k1"), W("v1"), None)
            heads_pe(pe)
            counts_pe(pe, RT1, E1)
            slots_pe(pe, RT1, 2 * U1, 2)
            expert_pe(pe, X1, U1)


def lay_out(x):
    import numpy as np

    f = np.float32
    w = np.zeros((P, WTOT), f)

    def put(name, a):
        w[:, WCOL[name][0]:WCOL[name][1]] = a

    put("q0", x["L0_attn_Wq"].T)
    put("k0", x["L0_attn_Wk"].T)
    put("v0", x["L0_attn_Wv"].T)
    put("o0", x["L0_attn_Wo"].T)
    put("g0", x["L0_ffn_Wg"])
    for n, name in enumerate(("q1", "k1", "v1")):
        put(name, x["L1_attn_W_qkv"][n * D:(n + 1) * D, :].T)
    put("qh", x["L1_ffn_Wq"])
    put("kh", x["L1_ffn_Wk"])
    put("vh", x["L1_ffn_Wv"])
    put("oh", x["L1_ffn_Wo"])
    put("ident", np.eye(P, dtype=f))
    place = np.arange(S, dtype=f)
    put("gauss", np.exp(f(-0.5) * ((place - f(S / 2)) / f(S / 4)) ** 2) * f(float(D) ** -0.5))
    put("bq0", x["L0_attn_bq"][:, None])
    put("bk0", x["L0_attn_bk"][:, None])
    put("bqh", x["L1_ffn_bq"][:, None])
    put("bkh", x["L1_ffn_bk"][:, None])
    one24 = np.zeros((P, 1), f)
    one24[24::32] = 1
    put("one24", one24)

    r = np.zeros((P, RTOT), f)

    def row(name, a):
        r[:, RCOL[name][0]:RCOL[name][1]] = a

    row("bv0", x["L0_attn_bv"])
    row("bo0", x["L0_attn_bo"])
    row("bg0", np.tile(x["L0_ffn_bg"], T))
    row("rev0", np.arange(E0, 0, -1, dtype=f))
    row("bvh", x["L1_ffn_bv"])
    row("boh", x["L1_ffn_bo"])
    row("g1", x["L1_ffn_ln1_g"])
    row("b1", x["L1_ffn_ln1_b"])
    row("g2", x["L1_ffn_ln2_g"])
    row("b2", x["L1_ffn_ln2_b"])
    row("rw", x["L1_ffn_router_w"][:, 0])
    row("rb", x["L1_ffn_router_b"])
    row("iota", np.arange(P, dtype=f))
    row("tile", np.arange(NT, dtype=f))
    row("place", np.arange(1, P + 1, dtype=f)[:, None])

    c = np.zeros((P, CTOT), np.float16)
    c[:, 0:D] = np.eye(P)
    c[:, D:2 * D] = np.triu(np.ones((P, P)), 1)
    c[:, 2 * D:3 * D] = 1
    for j in range(4):
        c[32 * j:32 * j + 32, CTOT - 4 + j] = 1
    for g in range(G):
        for j in range(4):
            for d in range(DH):
                i = (4 * g + j) * DH + d
                for name, pieces in (("qA", (0, 1)), ("qB", (2,)), ("kA", (0, 2)), ("kB", (1,))):
                    for piece in pieces:
                        c[i, CCOL[name] + g * P + 32 * j + piece * DH + d] = 1

    def pack(e, w1, b1, w2, b2):
        out = np.zeros((e, P, WP), f)
        out[:, :, 0:H] = w1
        out[:, :, H:H + HC * D] = w2.reshape(e, HC, P, D).transpose(0, 2, 1, 3).reshape(e, P, HC * D)
        out[:, :, H + HC * D:H + HC * D + HC] = b1.reshape(e, HC, P).transpose(0, 2, 1)
        out[:, :, WP - D:] = b2[:, None, :]
        return out

    return {
        "x": np.ascontiguousarray(x["L0_attn_x"]).reshape(N, D),
        "weights": w, "rows": r, "constants": c,
        "experts0": pack(E0, x["L0_ffn_W1"], x["L0_ffn_b1"], x["L0_ffn_W2"], x["L0_ffn_b2"]),
        "experts1": pack(E1, x["L1_ffn_W1"], x["L1_ffn_b1"], x["L1_ffn_W2"], x["L1_ffn_b2"]),
    }


def program(nc, arrays):
    args = [nc.dram_tensor(name, a.shape, mybir.dt.from_np(a.dtype), kind="ExternalInput").ap()
            for name, a in arrays.items()]
    out = nc.dram_tensor("out", (N, D), F32, kind="ExternalOutput").ap()
    build(nc, *args, out)
    return nc


def kernel(**inputs):
    import numpy as np
    import concourse.bacc as bacc
    from concourse.bass_utils import run_bass_kernel_spmd

    arrays = lay_out({name: np.asarray(a) for name, a in inputs.items()})
    nc = program(bacc.Bacc("TRN2", target_bir_lowering=False, num_devices=1), arrays)
    got = run_bass_kernel_spmd(nc, [arrays], core_ids=[0])
    return got.results[0]["out"].reshape(B, S, D)
```

```python
from contextlib import ExitStack

import concourse.bass as bass
from concourse import mybir

ALU = mybir.AluOpType
ACT = mybir.ActivationFunctionType
AX = mybir.AxisListType.X
F32 = mybir.dt.float32
F16 = mybir.dt.float16
I32 = mybir.dt.int32
ds = bass.ds

P = 128
B = 8
S = 512
D = 128
N = B * S
T = S // P
NT = N // P
H = 512
HC = H // P
E0 = 16
CAP = N // E0
E1 = 4
PAIR = 2 * P
U0 = N // PAIR
U1 = 20
NX = 4
PAD = 8192
NH = 16
DH = D // NH
G = 4
EPS = 1e-5
SCALE_H = float(DH) ** -0.5
ROW = 2 * D
WP = H + HC * D + HC + D

WCOL = {}
at = 0
for name, width in (("q0", D), ("k0", D), ("v0", D), ("o0", D), ("g0", E0), ("q1", D), ("k1", D), ("v1", D),
                    ("qh", D), ("kh", D), ("vh", D), ("oh", D), ("ident", D), ("gauss", S), ("bq0", 1), ("bk0", 1),
                    ("bv0", 1),
                    ("bqh", 1), ("bkh", 1), ("one24", 1)):
    WCOL[name] = (at, at + width)
    at += width
WTOT = at
RCOL = {}
at = 0
for name, width in (("bo0", D), ("bg0", T * E0), ("rev0", E0), ("bvh", D), ("boh", D), ("g1", D), ("b1", D),
                    ("g2", D), ("b2", D), ("rw", D), ("rb", 1), ("iota", P), ("tile", NT), ("place", 1)):
    RCOL[name] = (at, at + width)
    at += width
RTOT = at
CCOL = {"ident": 0, "tri": D, "ones": 2 * D, "qA": 3 * D, "qB": 7 * D, "kA": 11 * D, "kB": 15 * D}
CTOT = 19 * D + 4


def build(nc, x_in, w_in, r_in, c_in, pack0_in, pack1_in, out):
    table0 = nc.dram_tensor("table0", (N, ROW), F32).ap()
    x2d = nc.dram_tensor("x_after_experts0", (N, D), F32).ap()
    table1 = nc.dram_tensor("table1", (N, ROW), F32).ap()

    ctx = ExitStack()
    with ctx:
        def sb(name, shape, dt=F32):
            return ctx.enter_context(nc.sbuf_tensor(name, shape, dt))

        def sem(name):
            return ctx.enter_context(nc.semaphore(name))

        psum = ctx.enter_context(nc.psum_tensor("psum", [P, 8 * 512], F32))
        bank = [psum[:, i * 512:(i + 1) * 512] for i in range(8)]

        w_all = sb("w_all", [P, WTOT])
        r_all = sb("r_all", [P, RTOT])
        c_all = sb("c_all", [P, CTOT], F16)
        x_all = sb("x_all", [P, NT * D])
        s_all = sb("s_all", [P, NT * D])
        mv_all = sb("mv_all", [P, NT, 2])
        var_all = sb("var_all", [P, NT])
        rstd_all = sb("rstd_all", [P, NT])
        neg_half = sb("neg_half", [P, NT])
        eps = sb("eps", [P, NT])

        def W(name):
            return w_all[:, WCOL[name][0]:WCOL[name][1]]

        def R(name):
            return r_all[:, RCOL[name][0]:RCOL[name][1]]

        def C(name, n=0):
            return c_all[:, CCOL[name] + n * D:CCOL[name] + (n + 1) * D]

        def xt(i, of=x_all):
            return of[:, ds(i * D, D)]

        def x4(i, of=x_all):
            return of[:, ds(i * T * D, T * D)].rearrange("p (t d) -> p t d", t=T)

        def bank3(i, a, b):
            return bank[i][:, 0:a * b].rearrange("p (a b) -> p a b", a=a)

        def bcast(ap, n):
            return ap.unsqueeze(2).broadcast_to([P, ap.shape[1], n])

        stats = sb("stats", [P, T, 6])
        stats2 = sb("stats2", [P, T, 6])
        mv = sb("mv", [P, T, 2])
        mv2 = sb("mv2", [P, T, 2])
        var_eps = sb("var_eps", [P, T])
        var2 = sb("var2", [P, T])
        rstd2 = sb("rstd2", [P, T])
        rstd = sb("rstd", [P, T])
        xn = sb("xn", [P, T, D])
        xnT = sb("xnT", [P, S])
        qT = sb("qT", [P, S])
        kT = sb("kT", [P, S])
        vv = sb("vv", [P, T, D])
        pr_mem = sb("pr", [P, 4 * S])
        pr = pr_mem[:, 0:2 * S].rearrange("p (k n) -> p k n", k=2)
        prT = pr_mem[:, 2 * S:4 * S].rearrange("p (k n) -> p k n", k=2)
        vT = sb("vT", [P, S])
        nmax = sb("nmax", [P, T])
        rsum = sb("rsum", [P, T])
        rinv = sb("rinv", [P, T])
        xg = sb("xg", [P, 2, T, D])
        xgT = sb("xgT", [P, 2, S])
        lg = sb("lg", [P, NT, E0])
        wide = [sb(f"wide{i}", [P, NT, E0]) for i in range(4)]
        oh = sb("oh", [P, NT, E0], F16)
        one = {n: sb("r_" + n, [P, NT]) for n in
               ("lmax", "lsum", "gate", "rest", "rest2", "best", "pos", "late", "p16", "col", "key", "keyf", "gt", "floor",
                "ef", "base", "jf")}
        oni = {n: sb("ri_" + n, [P, NT], I32) for n in ("key", "floor", "e", "pos", "p", "j")}
        gpiece = sb("gpiece", [P, 3, NT], F16)
        ptm_mem = sb("ptm", [P, 4 * 2 * S])
        otm_mem = sb("otm", [P, G * S])
        ptm = ptm_mem[:, :].rearrange("p (r n) -> p r n", r=4)
        otm = otm_mem[:, :].rearrange("p (g n) -> p g n", g=G)
        at_place = otm_mem[:, :].bitcast(F16).rearrange("p (t n) -> p t n", t=NT)
        at_col = ptm_mem[:, 0:NT * 6 * U1].bitcast(F16).rearrange("p (t k n) -> p t k n", t=NT, k=6)
        vals = sb("vals", [P, 5, 2 * U1])
        padm = sb("padm", [P, 2 * U1])
        idf = sb("idf", [P, 2 * U1])
        gslot = sb("gslot", [P, 2 * U1])
        gsum = sb("gsum", [P, 2 * U1])
        toti = sb("toti", [P, E1], I32)
        pairs = sb("pairs", [P, E1])
        starts = sb("starts", [P, E1])
        which = sb("which", [P, 3, U1])
        esum = sb("esum", [P, U1])
        e_of = sb("e_of", [P, U1], I32)
        ids_all = sb("ids_all", [P, 2 * U1], I32)
        ids = sb("ids", [P, NX, 2, 2], I32)
        wx = sb("wx", [P, NX, WP])
        rg = sb("rg", [P, NX, 2, ROW])
        exT = sb("exT", [P, 2, PAIR])
        hT = pr_mem[:, :].rearrange("p (s c n) -> p s c n", s=2, c=HC)
        yb = sb("yb", [P, 2, 2, D])
        yo = sb("yo", [P, NX, 2, D])
        yr = sb("yr", [P, 2, 2, D])
        yn = sb("yn", [P, 2, 2, D])
        pre = sb("pre", [P, 2, 2, D])
        bx = sb("bx", [P, 2, 2, D])
        st1 = sb("st1", [P, 2, 6])
        mv1 = sb("mv1", [P, 2, 2, 2])
        ve1 = sb("ve1", [P, 2, 2])
        rs1 = sb("rs1", [P, 2, 2])
        qhi = sb("qhi", [P, S], F16)
        qlo = sb("qlo", [P, S], F16)
        khi = sb("khi", [P, S], F16)
        klo = sb("klo", [P, S], F16)
        kst = sb("kst", [P, S], F16)
        kpad = sb("kpad", [P, G, 4, S], F16)
        qs1 = sb("qs1", [P, G, S], F16)
        qs2 = sb("qs2", [P, G, S], F16)
        mrow = sb("mrow", [P, 2, T, P], F16)
        vh = sb("vh", [P, T, NH, 32])
        rch = sb("rch", [P, T, NH])
        ath = sb("ath", [P, T, D])
        atT = sb("atT", [P, D])

        class Signals(dict):
            def __init__(self, phase):
                self.phase = phase

            def __missing__(self, name):
                self[name] = sem(f"{self.phase}_{name}")
                return self[name]

        READY = 6
        consts = sem("consts_loaded")
        ready = sem("constants_set")

        def apart(eng, value):
            value = value if isinstance(value, int) else eng.snap(value)
            eng.wait_ge(ready, READY)
            return value

        def steps(eng, n, body):
            with eng.Fori(0, n - 1) as i:
                body(i, False)
            body(n - 1, True)

        def steps3(eng, n, body):
            body(0, True, False)
            with eng.Fori(1, n - 1) as i:
                body(i, False, False)
            body(n - 1, False, True)

        A = Signals("attn0")
        C1 = Signals("attn1")

        def ln_stats(v, s, it):
            for t in range(T):
                ins = nc.vector.bn_stats(stats[:, t, :], xt(it * T + t))
            ins.then_inc(s["bn"], 1)
            v.wait_ge(s["bn"], apart(v, it + 1))
            for t in range(T):
                ins = nc.vector.bn_aggr(mv[:, t, :], stats[:, t, :])
            ins.then_inc(s["stats"], 1)

        def normalised(p, s, b, dst, mean, var_e, r, done=None):
            nc.gpsimd.tensor_tensor(dst, x4(b), mean.broadcast_to([P, T, D]), ALU.subtract)
            nc.gpsimd.tensor_tensor(r, var_e, neg_half[:, 0:T], ALU.pow).then_inc(s["xc"], 1)
            p.wait_ge(ready, READY)
            p.wait_ge(s["xc"], b + 1 if done is None else done)
            nc.gpsimd.tensor_tensor(dst, dst, bcast(r, D), ALU.mult).then_inc(s["xn"], 1)

        def attn_sp(sp, s, src, behind=lambda: None):
            def body(it, first, last):
                if not first:
                    sp.wait_ge(s["x_loaded"], 16 * it)
                sp.dma_start(x4(it), src[ds(it * S, S), :].rearrange("(t p) d -> p t d", p=P)
                             ).then_inc(s["x_loaded"], 16)
                if first:
                    behind()
            steps3(sp, B, body)

        Z_BANK = (1, 2, 0, 2)

        def one_head_pe(pe, s, layer, out_product):
            def transposes(it, first):
                pe.wait_ge(s["xn"], it + 1)
                if not first:
                    pe.wait_ge(s["x_out"], it * T - T - 1)
                for t in range(T):
                    ins = nc.tensor.transpose(bank[0][:, t * P:(t + 1) * P], xn[:, t, :], W("ident"))
                ins.then_inc(s["xT_ps"], 1)

            def queries_keys(it, start):
                pe.wait_ge(s["xT"], it + 1)
                for n, name in enumerate("qk"):
                    if not start:
                        pe.wait_ge(s["x_out"], it * T - T + 1 + n)
                    nc.tensor.matmul(bank[1 + n][:, :], W(name + layer), xnT[:, :], start=True, stop=True
                                     ).then_inc(s[name + "_ps"], 1)

            def values(it):
                if out_product:
                    nc.tensor.matmul(bank[3][:, :], W("v" + layer), xnT[:, :], start=True, stop=True
                                     ).then_inc(s["vT_ps"], 1)
                else:
                    rows_of(xnT, W("v" + layer))

            def rows_of(turned, w):
                for t in range(T):
                    ins = nc.tensor.matmul(bank[3][:, t * D:(t + 1) * D], turned[:, t * P:(t + 1) * P], w,
                                           start=True, stop=True)
                ins.then_inc(s["v_ps"], 1)

            def scores(it, t, early=False):
                if t == 0:
                    pe.wait_ge(s["q"], it + 1)
                    pe.wait_ge(s["k"], it + 1)
                if not early:
                    pe.wait_ge(s["p"], it * T + t - 1)
                nc.tensor.matmul(bank[4 + t % 2][:, :], qT[:, t * P:(t + 1) * P], kT[:, :],
                                 start=True, stop=True).then_inc(s["s_ps"], 1)

            def turn(it, t, early):
                pe.wait_ge(s["p"], it * T + t + 1)
                if not early:
                    pe.wait_ge(s["pt"], it * T + t - 1)
                for c in range(T):
                    ins = nc.tensor.transpose(bank[6 + t % 2][:, c * P:(c + 1) * P],
                                              pr[:, t % 2, c * P:(c + 1) * P], W("ident"))
                ins.then_inc(s["pt_ps"], 1)

            def mix(it, t, early):
                pe.wait_ge(s["pt"], it * T + t + 1)
                if t == 0:
                    pe.wait_ge(s["v"], it + 1)
                if t in (1, 2) and not early:
                    pe.wait_ge(s["x_out"], it * T - (t - 1))
                if t == 3:
                    pe.wait_ge(s["x_out"], it * T + 2)
                for c in range(T):
                    ins = nc.tensor.matmul(bank[Z_BANK[t]][:, 0:D], prT[:, t % 2, c * P:(c + 1) * P], vv[:, c, :],
                                           start=(c == 0), stop=(c == T - 1))
                ins.then_inc(s["z_ps"], 1)

            def body(it, first, last):
                turn(it, 0, first)
                if out_product:
                    pe.wait_ge(s["vT"], it + 1)
                    rows_of(vT, W("o" + layer))
                scores(it, 2)
                turn(it, 1, first)
                mix(it, 0, first)
                scores(it, 3)
                if not last:
                    transposes(it + 1, first)
                turn(it, 2, False)
                mix(it, 1, first)
                turn(it, 3, False)
                if not last:
                    queries_keys(it + 1, False)
                mix(it, 2, first)
                if not last:
                    scores(it + 1, 0)
                    scores(it + 1, 1)
                mix(it, 3, False)
                if not last:
                    values(it + 1)

            transposes(0, True)
            queries_keys(0, True)
            scores(0, 0, True)
            scores(0, 1, True)
            values(0)
            steps3(pe, B, body)

        def one_head_act(act, s, bq, bv):
            def x_copy(it, start=False):
                act.wait_ge(s["xT_ps"], it + 1)
                if not start:
                    act.wait_ge(s["v_ps" if bv is None else "vT_ps"], it)
                nc.scalar.copy(xnT[:, :], bank[0][:, :]).then_inc(s["xT"], 1)

            def q_copy(it):
                act.wait_ge(s["q_ps"], it + 1)
                nc.scalar.activation(qT[:, :], bank[1][:, :], ACT.Identity, bias=bq).then_inc(s["q"], 1)

            def exp(it, t, first):
                act.wait_ge(s["nmax"], it * T + t + 1)
                if not (first and t < 2):
                    act.wait_ge(s["pt_ps"], it * T + t - 1)
                nc.scalar.activation(pr[:, t % 2, :], bank[4 + t % 2][:, :], ACT.Exp, bias=nmax[:, t:t + 1],
                                     accum_out=rsum[:, t:t + 1]).then_inc(s["p"], 1)

            def turned(it, t, first):
                act.wait_ge(s["pt_ps"], it * T + t + 1)
                if not (first and t < 2):
                    act.wait_ge(s["z_ps"], it * T + t - 1)
                nc.scalar.copy(prT[:, t % 2, :], bank[6 + t % 2][:, :]).then_inc(s["pt"], 1)

            def body(it, first, last):
                exp(it, 0, first)
                if bv is not None:
                    act.wait_ge(s["vT_ps"], it + 1)
                    nc.scalar.activation(vT[:, :], bank[3][:, :], ACT.Identity, bias=bv).then_inc(s["vT"], 1)
                exp(it, 1, first)
                turned(it, 0, first)
                act.wait_ge(s["v_ps"], it + 1)
                nc.scalar.copy(vv[:, :, :], bank3(3, T, D)).then_inc(s["v"], 1)
                exp(it, 2, first)
                turned(it, 1, first)
                exp(it, 3, first)
                if not last:
                    x_copy(it + 1)
                turned(it, 2, first)
                turned(it, 3, first)
                if not last:
                    q_copy(it + 1)

            x_copy(0, True)
            q_copy(0)
            steps3(act, B, body)

        def one_head_dve(v, s, bk, mask):
            def k_copy(it):
                v.wait_ge(s["k_ps"], it + 1)
                if mask is not None:
                    nc.vector.scalar_tensor_tensor(out=kT[:, :], in0=bank[2][:, :], scalar=bk, in1=mask,
                                                   op0=ALU.add, op1=ALU.mult).then_inc(s["k"], 1)
                else:
                    nc.vector.tensor_scalar(kT[:, :], bank[2][:, :], float(D) ** -0.5, None,
                                            ALU.mult).then_inc(s["k"], 1)

            def row_max(it, t):
                v.wait_ge(s["s_ps"], it * T + t + 1)
                nc.vector.tensor_reduce(nmax[:, t:t + 1], bank[4 + t % 2][:, :], AX, ALU.max,
                                        negate=True).then_inc(s["nmax"], 1)

            def inverses(it, half):
                v.wait_ge(s["p"], it * T + 2 * half + 2)
                part = slice(2 * half, 2 * half + 2)
                nc.vector.reciprocal(rinv[:, part], rsum[:, part]).then_inc(s["rinv"], 1)
                v.wait_ge(s["rinv"], it * 2 + half + 1)

            def final(it, t):
                v.wait_ge(s["z_ps"], it * T + t + 1)
                nc.vector.scalar_tensor_tensor(out=xt(it * T + t), in0=bank[Z_BANK[t]][:, 0:D],
                                               scalar=rinv[:, t:t + 1], in1=xt(it * T + t),
                                               op0=ALU.mult, op1=ALU.add).then_inc(s["x_out"], 1)

            def statistics(it, start=False):
                v.wait_ge(s["x_loaded"], apart(v, 16 * (it + 1)))
                if not start:
                    v.wait_ge(s["xn"], it)
                ln_stats(v, s, it)

            def new_statistics(it):
                v.wait_ge(s["x_out"], apart(v, (it + 1) * T))
                for t in range(T):
                    ins = nc.vector.bn_stats(stats2[:, t, :], xt(it * T + t))
                ins.then_inc(s["bn2"], 1)
                v.wait_ge(s["bn2"], apart(v, it + 1))
                for t in range(T):
                    ins = nc.vector.bn_aggr(mv2[:, t, :], stats2[:, t, :])
                ins.then_inc(s["mv2"], 1)
                if mask is None:
                    v.wait_ge(s["mv2"], it + 1)
                    nc.vector.tensor_copy(mv_all[:, ds(it * T, T), :], mv2[:, :, :]).then_inc(s["mv_all"], 1)

            def body(it, first, more):
                k_copy(it)
                if not first:
                    inverses(it - 1, 1)
                    final(it - 1, 2)
                row_max(it, 0)
                row_max(it, 1)
                if mask is not None:
                    v.wait_ge(s["xb"], it + 1)
                if not first:
                    final(it - 1, 3)
                if more:
                    statistics(it + 2)
                row_max(it, 2)
                if not first:
                    new_statistics(it - 1)
                row_max(it, 3)
                inverses(it, 0)
                final(it, 0)
                final(it, 1)

            statistics(0, True)
            statistics(1)
            v.wait_ge(consts, 48)
            body(0, True, True)
            with v.Fori(1, B - 2) as it:
                body(it, False, True)
            body(B - 2, False, False)
            body(B - 1, False, False)
            inverses(B - 1, 1)
            final(B - 1, 2)
            final(B - 1, 3)
            if mask is not None:
                v.wait_ge(GL["xn"], B - 1)
            new_statistics(B - 1)

        def one_head_pool(p, s, bo):
            def norm(it, first):
                p.wait_ge(s["stats"], it + 1)
                if not first:
                    p.wait_ge(s["xT_ps"], it)
                nc.gpsimd.tensor_tensor(var_eps[:, :], mv[:, :, 1], eps[:, 0:T], ALU.add).then_inc(s["eps"], 1)
                p.wait_ge(s["eps"], it + 1)
                normalised(p, s, it, xn[:, :, :], mv[:, :, 0:1], var_eps[:, :], rstd[:, :])

            def gate_rows(b):
                done = b + 1 if isinstance(b, int) else p.snap(b + 1)
                p.wait_ge(s["mv2"], done)
                nc.gpsimd.tensor_tensor(var2[:, :], mv2[:, :, 1], eps[:, 0:T], ALU.add).then_inc(s["eps2"], 1)
                p.wait_ge(s["eps2"], done)
                normalised(p, GL, b, x4(b, s_all), mv2[:, :, 0:1], var2[:, :], rstd2[:, :], done)

            def body(it, first, late):
                norm(it, first)
                if late:
                    gate_rows(it - 2)
                if bo is not None:
                    nc.gpsimd.tensor_tensor(x4(it), x4(it), bo.unsqueeze(1).broadcast_to([P, T, D]), ALU.add
                                            ).then_inc(s["xb"], 1)

            if bo is None:
                steps3(p, B, lambda it, first, last: body(it, first, False))
            else:
                body(0, True, False)
                body(1, False, False)
                with p.Fori(2, B) as it:
                    body(it, False, True)
                gate_rows(B - 2)
                gate_rows(B - 1)

        GL = Signals("gate0")

        def gate_dve(v, s):
            def body(i, first, last):
                for slot in range(2):
                    u = 2 * i + slot
                    v.wait_ge(s["xT_ps"], u + 1)
                    if not first:
                        v.wait_ge(s["lg_ps"], u - 1)
                    nc.vector.tensor_copy(xgT[:, slot, :], bank[4 * slot][:, :]).then_inc(s["xT"], 1)
                for slot in range(2):
                    u = 2 * i + slot
                    v.wait_ge(s["lg_ps"], u + 1)
                    nc.vector.tensor_tensor(lg[:, ds(u * T, T), :], bank3(4 * slot + 1, T, E0),
                                            R("bg0").rearrange("p (t e) -> p t e", t=T), ALU.add).then_inc(s["lg"], 1)
            steps3(v, B // 2, body)

        def gate_pe(pe, s):
            pe.wait_ge(A["x_out"], NT)

            def body(i, first, last):
                for slot in range(2):
                    u = 2 * i + slot
                    pe.wait_ge(s["xg"], u + 1)
                    if not first:
                        pe.wait_ge(s["xT"], u - 1)
                    for t in range(T):
                        ins = nc.tensor.transpose(bank[4 * slot][:, t * P:(t + 1) * P], xg[:, slot, t, :], W("ident"))
                    ins.then_inc(s["xT_ps"], 1)
                for slot in range(2):
                    u = 2 * i + slot
                    pe.wait_ge(s["xT"], u + 1)
                    if not first:
                        pe.wait_ge(s["lg"], u - 1)
                    for t in range(T):
                        ins = nc.tensor.matmul(bank[4 * slot + 1][:, t * E0:(t + 1) * E0], xgT[:, slot, t * P:(t + 1) * P],
                                               W("g0"), start=True, stop=True)
                    ins.then_inc(s["lg_ps"], 1)
            steps3(pe, B // 2, body)

        def gate_act(act, s):
            def body(i, first, last):
                for slot in range(2):
                    u = 2 * i + slot
                    act.wait_ge(s["xn"], u + 1)
                    if not first:
                        act.wait_ge(s["xT_ps"], u - 1)
                    nc.scalar.copy(xg[:, slot, :, :], x4(u, s_all)).then_inc(s["xg"], 1)
            steps3(act, B // 2, body)

        def gate_sp(sp, s):
            def body(it, last):
                sp.wait_ge(A["x_out"], T * (it + 1))
                sp.dma_start(x2d[ds(it * S, S), :].rearrange("(t p) d -> p t d", p=P), x4(it)).then_inc(s["x2"], 16)
                sp.dma_start(table0[ds(it * S, S), D:2 * D].rearrange("(t p) d -> p t d", p=P), x4(it)
                             ).then_inc(s["x2"], 16)
                sp.wait_ge(s["xn"], it + 1)
                sp.dma_start(table0[ds(it * S, S), 0:D].rearrange("(t p) d -> p t d", p=P), x4(it, s_all)
                             ).then_inc(s["x2"], 16)
            steps(sp, B, body)

        class Line:
            def __init__(self, eng, s):
                self.eng, self.s, self.n = eng, s, 0

            def __call__(self, ins):
                self.n += 1
                ins.then_inc(self.s, 1)
                self.eng.wait_ge(self.s, self.n)

        RT0 = Signals("route0")
        RT1 = Signals("route1")

        def places(v, s, then, e, pos_out):
            v.wait_ge(s["cnt_ps"], 1)
            a, b = wide[0][:, :, 0:e], wide[1][:, :, 0:e]
            then(nc.vector.tensor_copy(a, bank3(1, NT, e)))
            step = 1
            while step < NT:
                nc.vector.tensor_copy(b[:, 0:step, :], a[:, 0:step, :])
                then(nc.vector.tensor_tensor(b[:, step:, :], a[:, step:, :], a[:, 0:NT - step, :], ALU.add))
                a, b = b, a
                step *= 2
            c, d = wide[2][:, :, 0:e], wide[3][:, :, 0:e]
            nc.vector.tensor_copy(c[:, 0:1, :], bank3(0, NT, e)[:, 0:1, :])
            then(nc.vector.tensor_tensor(c[:, 1:, :], bank3(0, NT, e)[:, 1:, :], a[:, 0:NT - 1, :], ALU.add))
            then(nc.vector.tensor_tensor(d, c, oh[:, :, 0:e], ALU.mult))
            then(nc.vector.tensor_reduce(pos_out, d, AX, ALU.add))
            return a

        known = {}

        def carry(eng, k, cols):
            hot = at_col[:, :, 5, 0:cols]
            if k == 1:
                return eng.tensor_scalar(at_col[:, :, k, 0:cols], hot, R("place"), None, ALU.mult)
            value = R("tile") if k == 0 else gpiece[:, k - 2, :]
            return eng.tensor_tensor(at_col[:, :, k, 0:cols], hot, bcast(value, cols), ALU.mult)

        def slots_pool(p, s, cols, n_vals):
            p.wait_ge(s["line"], known[s.phase])
            for k in (2, 3) if n_vals == 5 else (0,):
                ins = carry(nc.gpsimd, k, cols)
            ins.then_inc(s["b_pool"], 1)

        def slots(v, s, then, cols, n_vals):
            iota = R("iota")
            then(nc.vector.tensor_tensor(at_col[:, :, 5, 0:cols], iota[:, 0:cols].unsqueeze(1).broadcast_to([P, NT, cols]),
                                         bcast(one["col"][:, :], cols), ALU.is_equal))
            known[s.phase] = then.n
            for k in (0, 1, 4) if n_vals == 5 else (1,):
                ins = carry(nc.vector, k, cols)
            ins.then_inc(s["b"], 1)
            for c in range(4):
                part = slice(c * NT // 4, (c + 1) * NT // 4)
                nc.vector.tensor_tensor(at_place[:, part, :], iota.unsqueeze(1).broadcast_to([P, NT // 4, P]),
                                        bcast(one["p16"][:, part], P), ALU.is_equal).then_inc(s["a"], 1)

        def slots_pe(pe, s, cols, n_vals):
            pe.wait_ge(s["b"], 1)
            pe.wait_ge(s["b_pool"], 1)
            dst = bank[2][:, 0:n_vals * cols].rearrange("p (n c) -> p n c", n=n_vals)
            for t in range(NT):
                if t % (NT // 4) == 0:
                    pe.wait_ge(s["a"], t // (NT // 4) + 1)
                ins = nc.tensor.matmul(dst, at_place[:, t, :], at_col[:, t, 0:n_vals, 0:cols],
                                       start=(t == 0), stop=(t == NT - 1))
            ins.then_inc(s["ids_ps"], 1)

        def counts_pe(pe, s, e):
            pe.wait_ge(s["oh"], 1)
            nc.tensor.matmul(bank3(0, NT, e), C("tri"), oh[:, :, 0:e], start=True, stop=True)
            nc.tensor.matmul(bank3(1, NT, e), C("ones"), oh[:, :, 0:e], start=True, stop=True).then_inc(s["cnt_ps"], 1)

        def ids_out(v, s, then, cols, n_vals):
            v.wait_ge(s["ids_ps"], 1)
            src = bank[2][:, 0:n_vals * cols].rearrange("p (n c) -> p n c", n=n_vals)
            then(nc.vector.tensor_copy(vals[:, 0:n_vals, 0:cols], src))
            nc.vector.tensor_scalar(padm[:, 0:cols], vals[:, 1, 0:cols], 0.0, float(PAD), ALU.is_equal, ALU.mult)
            if n_vals == 5:
                then(nc.vector.scalar_tensor_tensor(out=gsum[:, 0:cols], in0=vals[:, 4, 0:cols], scalar=2.0 ** -12,
                                                    in1=vals[:, 3, 0:cols], op0=ALU.mult, op1=ALU.add))
                then(nc.vector.scalar_tensor_tensor(out=gslot[:, 0:cols], in0=gsum[:, 0:cols], scalar=2.0 ** -12,
                                                    in1=vals[:, 2, 0:cols], op0=ALU.mult, op1=ALU.add))
            then(nc.vector.scalar_tensor_tensor(out=idf[:, 0:cols], in0=vals[:, 0, 0:cols], scalar=float(P),
                                                in1=vals[:, 1, 0:cols], op0=ALU.mult, op1=ALU.add))
            nc.vector.scalar_tensor_tensor(out=ids_all[:, 0:cols], in0=idf[:, 0:cols], scalar=-1.0, in1=padm[:, 0:cols],
                                           op0=ALU.add, op1=ALU.add).then_inc(s["ids"], 1)

        def route0_dve(v, s):
            then = Line(v, s["line"])
            rev = R("rev0").unsqueeze(1).broadcast_to([P, NT, E0])
            v.wait_ge(GL["lg"], B)
            then(nc.vector.tensor_reduce(one["lmax"][:, :], lg[:, :, :], AX, ALU.max))
            nc.vector.tensor_tensor(wide[3][:, :, :], lg[:, :, :], bcast(one["lmax"][:, :], E0), ALU.subtract
                                    ).then_inc(s["lsh"], 1)
            then(nc.vector.tensor_tensor(wide[0][:, :, :], lg[:, :, :], bcast(one["lmax"][:, :], E0), ALU.is_equal))
            then(nc.vector.tensor_tensor(wide[1][:, :, :], wide[0][:, :, :], rev, ALU.mult))
            then(nc.vector.tensor_reduce(one["best"][:, :], wide[1][:, :, :], AX, ALU.max))
            nc.vector.tensor_tensor(oh[:, :, :], rev, bcast(one["best"][:, :], E0), ALU.is_equal).then_inc(s["oh"], 1)
            v.wait_ge(s["ex"], 1)
            then(nc.vector.tensor_reduce(one["lsum"][:, :], wide[2][:, :, :], AX, ALU.add))
            then(nc.vector.reciprocal(one["gate"][:, :], one["lsum"][:, :]))
            then(nc.vector.tensor_copy(gpiece[:, 0, :], one["gate"][:, :]))
            then(nc.vector.tensor_tensor(one["rest"][:, :], one["gate"][:, :], gpiece[:, 0, :], ALU.subtract))
            then(nc.vector.tensor_scalar(gpiece[:, 1, :], one["rest"][:, :], 4096.0, None, ALU.mult))
            then(nc.vector.scalar_tensor_tensor(out=one["rest2"][:, :], in0=one["rest"][:, :], scalar=4096.0,
                                                in1=gpiece[:, 1, :], op0=ALU.mult, op1=ALU.subtract))
            then(nc.vector.tensor_scalar(gpiece[:, 2, :], one["rest2"][:, :], 4096.0, None, ALU.mult))
            places(v, s, then, E0, one["pos"][:, :])
            then(nc.vector.tensor_scalar(one["late"][:, :], one["pos"][:, :], float(P), None, ALU.is_ge))
            then(nc.vector.scalar_tensor_tensor(out=one["p16"][:, :], in0=one["late"][:, :], scalar=-float(P),
                                                in1=one["pos"][:, :], op0=ALU.mult, op1=ALU.add))
            then(nc.vector.scalar_tensor_tensor(out=one["ef"][:, :], in0=one["best"][:, :], scalar=-2.0,
                                                in1=one["late"][:, :], op0=ALU.mult, op1=ALU.add))
            then(nc.vector.tensor_scalar(one["col"][:, :], one["ef"][:, :], 2.0 * E0, None, ALU.add))
            slots(v, s, then, 2 * E0, 5)
            ids_out(v, s, then, 2 * E0, 5)

        def route0_act(act, s):
            act.wait_ge(s["lsh"], 1)
            nc.scalar.activation(wide[2][:, :, :], wide[3][:, :, :], ACT.Exp).then_inc(s["ex"], 1)

        X0 = Signals("exp0")

        def turns(eng, n, body):
            steps3(eng, n // NX, body)

        def back(i, j, k):
            slot = (j - k) % NX
            turn = i + (j - k - slot) // NX
            return NX * turn + slot, turn, slot

        def has(i, j, k, first, last):
            return not (first and j - k < 0) and not (last and j - k >= NX)

        def expert_pool(p, s, table, dest, before, n, lag):
            def gather(at, slot):
                for t in range(2):
                    nc.gpsimd.indirect_dma_start(
                        out=rg[:, slot, t, :], out_offset=None, in_=table,
                        in_offset=bass.IndirectOffsetOnAxis(ap=at[:, t:t + 1], axis=0),
                        bounds_check=N - 1, oob_is_err=False).then_inc(s[f"g{slot}"], 16)

            def move(u, slot, free, new):
                done = u + 1
                p.wait_ge(s["yo"], done)
                if new is not None and lag:
                    p.wait_ge(s["pre"], done + lag)
                    p.wait_ge(s["xT_ps"], done + lag)
                if new is None:
                    nc.gpsimd.tensor_copy(ids[:, slot, 0, :], ids_all[:, ds(u * 2, 2)]).then_inc(s["ids"], 1)
                else:
                    far = NX + lag
                    nc.gpsimd.tensor_copy(ids[:, slot, :, :], ids_all[:, ds(u * 2, 2 * far + 2)].rearrange(
                        "p (k c) -> p k c", c=2)[:, 0:far + 1:far, :]).then_inc(s["ids"], 1)
                p.wait_ge(ready, READY)
                p.wait_ge(s["ids"], done)
                if new is not None:
                    gather(ids[:, slot, 1, :], free)
                for t in range(2):
                    nc.gpsimd.indirect_dma_start(
                        out=dest, out_offset=bass.IndirectOffsetOnAxis(ap=ids[:, slot, 0, t:t + 1], axis=0),
                        in_=yo[:, slot, t, :], in_offset=None,
                        bounds_check=N - 1, oob_is_err=False).then_inc(s[f"s{slot}"], 16)

            def deviation(u, slot):
                p.wait_ge(s["var"], u + 1)
                nc.gpsimd.tensor_tensor(rs1[:, slot % 2, :], ve1[:, slot % 2, :], neg_half[:, 0:2], ALU.pow
                                        ).then_inc(s["rs"], 1)

            def body(i, first, last):
                for j in range(NX + (lag if last else 0)):
                    if lag and j < NX:
                        if first and j == 0:
                            p.wait_ge(s["pre"], 1)
                            p.wait_ge(s["xT_ps"], 1)
                            gather(ids_all[:, 2 * NX:2 * NX + 2], 0)
                        deviation(NX * i + j, j)
                    if has(i, j, lag, first, last):
                        u, _, slot = back(i, j, lag)
                        move(u, slot, j % NX, None if last else u + NX + lag)

            before(p)
            for slot in range(NX):
                gather(ids_all[:, 2 * slot:2 * slot + 2], slot)
            turns(p, n, body)

        def expert_sp(sp, s, pack, which, n, before):
            before(sp)

            def load(u, slot):
                sp.dma_start(wx[:, slot, :], pack[ds(which(sp, u), 1), :, :].rearrange("o p w -> (o p) w")
                             ).then_inc(s[f"w{slot}"], 16)

            def body(i, last):
                for slot in range(NX):
                    u = NX * i + slot
                    if not last:
                        sp.wait_ge(s["yb"], apart(sp, u + 1))
                        load(u + NX, slot)
            for slot in range(NX):
                load(slot, slot)
            steps(sp, n // NX, body)

        def expert_pe(pe, s, n):
            def turn(u, i, slot):
                pe.wait_ge(s[f"g{slot}"], 32 * (i + 1))
                for t in range(2):
                    ins = nc.tensor.transpose(bank[4 * (slot % 2)][:, t * P:(t + 1) * P], rg[:, slot, t, 0:D], W("ident"))
                ins.then_inc(s["xT_ps"], 1)

            def hidden(u, i, slot):
                pe.wait_ge(s["xT"], u + 1)
                pe.wait_ge(s[f"w{slot}"], 16 * (i + 1))
                for c in range(HC):
                    ins = nc.tensor.matmul(bank[4 * (slot % 2) + 1 + c // 2][:, (c % 2) * PAIR:(c % 2 + 1) * PAIR],
                                           wx[:, slot, c * P:(c + 1) * P], exT[:, slot % 2, :], start=True, stop=True)
                    if c % 2:
                        ins.then_inc(s["hb_ps" if c > 1 else "ha_ps"], 1)

            def outer(u, slot, first):
                if not first:
                    pe.wait_ge(s["yb"], u - 1)
                for t in range(2):
                    for c in range(HC):
                        if t == 0 and c % 2 == 0:
                            pe.wait_ge(s["hb" if c else "ha"], u + 1)
                        ins = nc.tensor.matmul(bank[4 * (slot % 2) + 3][:, t * D:(t + 1) * D],
                                               hT[:, slot % 2, c, t * P:(t + 1) * P],
                                               wx[:, slot, H + c * D:H + (c + 1) * D], start=(c == 0), stop=(c == HC - 1))
                ins.then_inc(s["y_ps"], 1)

            def body(i, first, last):
                for j in range(NX + 1 if last else NX):
                    if j < NX:
                        hidden(NX * i + j, i, j)
                    if has(i, j, -1, first, last):
                        turn(*back(i, j, -1))
                    if has(i, j, 1, first, last):
                        u, _, slot = back(i, j, 1)
                        outer(u, slot, first and j < 3)
            turn(0, 0, 0)
            turns(pe, n, body)

        def expert_act(act, s, n):
            def rows_copy(u, slot):
                act.wait_ge(s["xT_ps"], u + 1)
                nc.scalar.copy(exT[:, slot % 2, :], bank[4 * (slot % 2)][:, 0:PAIR]).then_inc(s["xT"], 1)

            def body(i, first, last):
                for j in range(NX):
                    u = NX * i + j
                    act.wait_ge(s["ha_ps"], u + 1)
                    for c in range(2):
                        ins = nc.scalar.activation(hT[:, j % 2, c, :], bank[4 * (j % 2) + 1][:, c * PAIR:(c + 1) * PAIR],
                                                   ACT.Relu, bias=wx[:, j, H + HC * D + c:H + HC * D + c + 1])
                    ins.then_inc(s["ha"], 1)
                    if has(i, j, -1, first, last):
                        u, _, slot = back(i, j, -1)
                        rows_copy(u, slot)
            rows_copy(0, 0)
            turns(act, n, body)

        def relu_half(v, s, u, slot):
            v.wait_ge(s["hb_ps"], u + 1)
            for c in range(2, HC):
                ins = nc.vector.tensor_scalar(hT[:, slot % 2, c, :], bank[4 * (slot % 2) + 2][:, (c - 2) * PAIR:(c - 1) * PAIR],
                                              wx[:, slot, H + HC * D + c:H + HC * D + c + 1], 0.0, ALU.add, ALU.max)
            ins.then_inc(s["hb"], 1)

        def expert_dve0(v, s, n):
            def rows(u, i, slot, first):
                v.wait_ge(s["y_ps"], u + 1)
                nc.vector.tensor_tensor(yb[:, slot % 2, :, :], bank3(4 * (slot % 2) + 3, 2, D),
                                        wx[:, slot, WP - D:WP].unsqueeze(1).broadcast_to([P, 2, D]), ALU.add
                                        ).then_inc(s["yb"], 1)
                v.wait_ge(s["yb"], u + 1)
                if not first:
                    v.wait_ge(s[f"s{slot}"], 32 * i)
                for t in range(2):
                    ins = nc.vector.scalar_tensor_tensor(out=yo[:, slot, t, :], in0=yb[:, slot % 2, t, :],
                                                         scalar=gslot[:, ds(u * 2 + t, 1)],
                                                         in1=rg[:, slot, t, D:2 * D], op0=ALU.mult, op1=ALU.add)
                ins.then_inc(s["yo"], 1)

            def body(i, first, last):
                for j in range(NX):
                    if has(i, j, -1, first, last):
                        u, _, slot = back(i, j, -1)
                        relu_half(v, s, u, slot)
                    rows(NX * i + j, i, j, first)
            relu_half(v, s, 0, 0)
            turns(v, n, body)

        def expert_dve1(v, s, n):
            def ahead(u, i, slot):
                v.wait_ge(s[f"g{slot}"], 32 * (i + 1))
                v.wait_ge(s[f"w{slot}"], 16 * (i + 1))
                nc.vector.tensor_tensor(pre[:, slot % 2, :, :], rg[:, slot, :, 0:D],
                                        wx[:, slot, WP - D:WP].unsqueeze(1).broadcast_to([P, 2, D]), ALU.add)
                nc.vector.tensor_tensor(bx[:, slot % 2, :, :], rg[:, slot, :, D:2 * D],
                                        R("b2").unsqueeze(1).broadcast_to([P, 2, D]), ALU.add).then_inc(s["pre"], 1)

            def statistics(u, i, slot):
                v.wait_ge(s["y_ps"], u + 1)
                v.wait_ge(s["pre"], u + 1)
                nc.vector.tensor_tensor(yr[:, slot % 2, :, :], bank3(4 * (slot % 2) + 3, 2, D), pre[:, slot % 2, :, :],
                                        ALU.add).then_inc(s["yb"], 1)
                v.wait_ge(s["yb"], u + 1)
                for t in range(2):
                    ins = nc.vector.bn_stats(st1[:, t, :], yr[:, slot % 2, t, :])
                ins.then_inc(s["bn"], 1)
                v.wait_ge(s["bn"], apart(v, u + 1))
                for t in range(2):
                    ins = nc.vector.bn_aggr(mv1[:, slot % 2, t, :], st1[:, t, :])
                ins.then_inc(s["st"], 1)
                v.wait_ge(s["st"], u + 1)
                nc.vector.tensor_scalar(ve1[:, slot % 2, :], mv1[:, slot % 2, :, 1], EPS, None, ALU.add
                                        ).then_inc(s["var"], 1)
                for t in range(2):
                    ins = nc.vector.scalar_tensor_tensor(out=yn[:, slot % 2, t, :], in0=yr[:, slot % 2, t, :],
                                                         scalar=mv1[:, slot % 2, t, 0:1], in1=R("g2"),
                                                         op0=ALU.subtract, op1=ALU.mult)
                ins.then_inc(s["yn"], 1)

            def normalised(u, i, slot, first):
                v.wait_ge(s["rs"], u + 1)
                v.wait_ge(s["yn"], u + 1)
                if not first:
                    v.wait_ge(s[f"s{slot}"], 32 * i)
                for t in range(2):
                    ins = nc.vector.scalar_tensor_tensor(out=yo[:, slot, t, :], in0=yn[:, slot % 2, t, :],
                                                         scalar=rs1[:, slot % 2, t:t + 1], in1=bx[:, slot % 2, t, :],
                                                         op0=ALU.mult, op1=ALU.add)
                ins.then_inc(s["yo"], 1)

            def body(i, first, last):
                for j in range(NX):
                    if has(i, j, -2, first, last):
                        u, turn, slot = back(i, j, -2)
                        relu_half(v, s, u, slot)
                    normalised(NX * i + j, i, j, first)
                    if has(i, j, -1, first, last):
                        statistics(*back(i, j, -1))
                    if has(i, j, -2, first, last):
                        ahead(u, turn, slot)
            relu_half(v, s, 0, 0)
            ahead(0, 0, 0)
            relu_half(v, s, 1, 1)
            statistics(0, 0, 0)
            ahead(1, 0, 1)
            turns(v, n, body)

        LEAD = 5
        M = Signals("heads")
        F = Signals("norm1")
        xw = xg[:, 0, :, :]
        xh = xg[:, 1, :, :]

        def plan(first, last):
            at = [[(0, "ks", 0, 2), (2, "qs", 0, 2), (4, "V", 0, 0)],
                  [(1, "ks", 0, 3), (3, "qs", 0, 3)], [], []]
            if not first:
                at[0] += [(6, "BT", -1, 0), (8, "BT", -1, 1), (10, "BT", -1, 2), (12, "BT", -1, 3)]
                at[1] += [(11, "AT", -1, 0), (12, "WO", -1, 0)]
                at[2] += [(4, "AT", -1, 1), (6, "WO", -1, 1), (8, "AT", -1, 2), (10, "WO", -1, 2)]
                at[3] += [(6, "AT", -1, 3), (9, "WO", -1, 3)]
            if not last:
                at[1] += [(5, "T", 1, 0), (7, "Q", 1, 0), (9, "K", 1, 0)]
                at[2] += [(1, "ks", 1, 0), (3, "qs", 1, 0)]
                at[3] += [(1, "ks", 1, 1), (3, "qs", 1, 1)]
            for g in range(G - 1 if last else G):
                at[g].append((13, "q2", (g + 1) // G, (g + 1) % G))
            return [sorted(a, key=lambda z: z[0]) for a in at]

        PROLOGUE = [("T", 0, 0), ("Q", 0, 0), ("K", 0, 0), ("ks", 0, 0), ("qs", 0, 0), ("ks", 0, 1), ("qs", 0, 1)]
        ENDING = [("BT", t) for t in range(T)] + [("AT", 0), ("AT", 1), ("WO", 0), ("AT", 2), ("WO", 1), ("AT", 3),
                                                  ("WO", 2), ("WO", 3)]
        FIRST = sum(len(a) for a in plan(True, False))
        MIDDLE = sum(len(a) for a in plan(False, False))
        START = len(PROLOGUE) + 1

        def misc_base(it, first, last):
            return START if first else it * MIDDLE + (START + FIRST - MIDDLE)

        class Misc:
            def __init__(self, do):
                self.do = do

            def sequence(self, it, first, last, step):
                base, n = misc_base(it, first, last), 0
                for slot, units in enumerate(plan(first, last)):
                    start = n
                    units = list(units)
                    for i in range(16):
                        while units and units[0][0] == i:
                            _, kind, db, k = units.pop(0)
                            self.do(kind, it + db, k, base + n)
                            n += 1
                        step(it, slot, i, base + start, first, last)

        def heads_pe(pe):
            s = M

            def do(kind, b, k, m, start=False):
                if not start:
                    pe.wait_ge(s["misc_empty"], m)
                x = bank[7]
                if kind == "T":
                    pe.wait_ge(s["xn"], b + 1)
                    for t in range(T):
                        ins = nc.tensor.transpose(x[:, t * P:(t + 1) * P], xh[:, t, :], W("ident"))
                elif kind in "QK":
                    ins = nc.tensor.matmul(x, W("qh" if kind == "Q" else "kh"), xnT[:, :], start=True, stop=True)
                elif kind == "V":
                    for t in range(T):
                        ins = nc.tensor.matmul(x[:, t * D:(t + 1) * D], xnT[:, t * P:(t + 1) * P], W("vh"),
                                               start=True, stop=True)
                elif kind in ("ks", "qs"):
                    hi, lo = (khi, klo) if kind == "ks" else (qhi, qlo)
                    nc.tensor.matmul(x, C(kind[0] + "A", k), hi[:, :], start=True, stop=False)
                    ins = nc.tensor.matmul(x, C(kind[0] + "B", k), lo[:, :], start=False, stop=True)
                elif kind == "q2":
                    pe.wait_ge(s["nmax"], (b * G + k + 1) * 16)
                    for t in range(T):
                        nc.tensor.matmul(x[:, t * P:(t + 1) * P], mrow[:, k % 2, t, :], C("ident"),
                                         start=(t == 0), stop=False)
                    ins = nc.tensor.matmul(x, C("ident"), qs1[:, k, :], start=False, stop=True)
                elif kind == "BT":
                    pe.wait_ge(s["otm"], (b + 1) * G)
                    for g in range(G):
                        ins = nc.tensor.transpose(x[:, g * P:(g + 1) * P], otm[:, g, k * P:(k + 1) * P], W("ident"))
                elif kind == "AT":
                    ins = nc.tensor.transpose(x[:, 0:P], ath[:, k, :], W("ident"))
                elif kind == "WO":
                    ins = nc.tensor.matmul(x[:, 0:P], atT[:, :], W("oh"), start=True, stop=True)
                ins.then_inc(s["misc_full"], 1)

            def score(n, g, i, start=False):
                if i == 0:
                    pe.wait_ge(s["kpad"], n + 1)
                if not start:
                    pe.wait_ge(s["nmax"], n * 16 + i - 1)
                j, t = i // 4, i % 4
                nc.tensor.matmul(bank[i % 2], qs1[:, g, t * P:(t + 1) * P], kpad[:, g, j, :],
                                 start=True, stop=True).then_inc(s["s_ps"], 1)

            def turned(n, g, i, early):
                c, j = i // 4, i % 4
                if i % 2 == 0 and not (early and i < 4):
                    pe.wait_ge(s["exp"], n * 8 + i // 2 - 1)
                ins = nc.tensor.matmul(bank[2 + i % 4], kpad[:, g, j, c * P:(c + 1) * P], qs2[:, g, :],
                                       start=True, stop=True)
                if i % 2:
                    ins.then_inc(s["st_ps"], 1)

            def mix(n, g, c, early):
                pe.wait_ge(s["exp"], n * 8 + 2 * c + 2)
                if c == 0 and not early:
                    pe.wait_ge(s["otm"], n)
                for j in range(4):
                    ins = nc.tensor.matmul(bank[6][32 * j:32 * j + 32, :], vh[:, c, 4 * g + j, :],
                                           ptm[:, (2 * c + j // 2) % 4, (j % 2) * S:(j % 2 + 1) * S],
                                           start=(c == 0), stop=(c == T - 1))
                ins.then_inc(s["pv"], 1)

            def step(it, g, i, m0, first, last):
                n = it * G + g
                over, k = (i + LEAD) // 16, (i + LEAD) % 16
                if not (last and g + 1 + over >= G):
                    if k == 0:
                        at = [kind for _, kind, _, _ in plan(first, last)[g]].index("qs")
                        pe.wait_ge(s["misc_empty"], m0 + at + 1)
                    score(n + 1 + over, (g + 1 + over) % G, k)
                if i == 0:
                    pe.wait_ge(s["misc_empty"], m0)
                early = first and g == 0
                turned(n, g, i, early)
                if i == 2 and not early:
                    mix(n - 1, (g - 1) % G, 3, False)
                if i in (6, 10, 14):
                    if i == 6 and g == 0:
                        pe.wait_ge(s["misc_empty"], m0 + 3)
                    mix(n, g, (i - 6) // 4, early)

            m = 0
            for kind, b, k in PROLOGUE:
                do(kind, b, k, m, m == 0)
                m += 1
            for i in range(16 + LEAD):
                if i == 16:
                    pe.wait_ge(s["misc_empty"], len(PROLOGUE))
                score(i // 16, i // 16, i % 16, i < 2)
            do("q2", 0, 0, m)
            misc = Misc(do)
            steps3(pe, B, lambda it, first, last: misc.sequence(it, first, last, step))
            mix(B * G - 1, G - 1, 3, False)
            ended = misc_base(B, False, False) - MIDDLE + sum(len(a) for a in plan(False, True))
            pe.wait_ge(s["misc_empty"], ended)
            for kind, t in ENDING:
                if kind == "BT":
                    pe.wait_ge(s["otm"], B * G)
                    for g in range(G):
                        ins = nc.tensor.transpose(bank[t][:, g * P:(g + 1) * P], otm[:, g, t * P:(t + 1) * P], W("ident"))
                elif kind == "AT":
                    pe.wait_ge(s["misc_empty"], ended + t + 1)
                    ins = nc.tensor.transpose(bank[4 + t % 2][:, 0:P], ath[:, t, :], W("ident"))
                else:
                    pe.wait_ge(s["atT"], t + 1)
                    if t >= 2:
                        pe.wait_ge(s["misc_empty"], ended + T + t - 1)
                    ins = nc.tensor.matmul(bank[6 + t % 2][:, 0:P], vT[:, t % 2 * P:(t % 2 + 1) * P], W("oh"),
                                           start=True, stop=True)
                ins.then_inc(s["misc_full"], 1)

        def heads_act(act):
            s = M

            def do(kind, b, k, m, start=False):
                act_kinds = {"T", "Q", "K", "ks", "qs", "q2", "AT"}
                if kind not in act_kinds:
                    return
                act.wait_ge(s["misc_full"], m + 1)
                x = bank[7]
                if kind == "T":
                    nc.scalar.copy(xnT[:, :], x).then_inc(s["misc_empty"], 1)
                elif kind == "Q":
                    nc.scalar.activation(qhi[:, :], x, ACT.Identity, bias=W("bqh")).then_inc(s["qhi"], 1)
                elif kind == "K":
                    nc.scalar.activation(khi[:, :], x, ACT.Identity, bias=W("bkh")).then_inc(s["khi"], 1)
                elif kind == "ks":
                    if not (start and k == 0):
                        act.wait_ge(s["kpad"], b * G + k)
                    nc.scalar.activation(kst[:, :], x, ACT.Identity, bias=W("one24")).then_inc(s["misc_empty"], 1)
                elif kind == "qs":
                    nc.scalar.copy(qs1[:, k, :], x).then_inc(s["misc_empty"], 1)
                elif kind == "q2":
                    nc.scalar.copy(qs2[:, k, :], x).then_inc(s["misc_empty"], 1)
                elif kind == "AT":
                    nc.scalar.copy(atT[:, :], x[:, 0:P]).then_inc(s["misc_empty"], 1)

            def step(it, g, i, m0, first, last):
                n = it * G + g
                if i % 2:
                    q = i // 2
                    act.wait_ge(s["st_ps"], n * 8 + q + 1)
                    if not (first and g == 0 and q < 4):
                        act.wait_ge(s["pv"], n * 4 + q // 2 - 1)
                    nc.scalar.activation(ptm[:, q % 4, :], psum[:, (2 + 2 * (q % 2)) * S:(4 + 2 * (q % 2)) * S], ACT.Exp,
                                         scale=SCALE_H).then_inc(s["exp"], 1)
                if i == 4 and not (first and g == 0):
                    group_out(n - 1, (g - 1) % G)

            def group_out(n, g):
                act.wait_ge(s["pv"], n * 4 + 4)
                nc.scalar.copy(otm[:, g, :], bank[6]).then_inc(s["otm"], 1)

            m = 0
            for kind, b, k in PROLOGUE:
                do(kind, b, k, m, True)
                m += 1
            do("q2", 0, 0, m)
            misc = Misc(do)
            steps3(act, B, lambda it, first, last: misc.sequence(it, first, last, step))
            group_out(B * G - 1, G - 1)
            ended = misc_base(B, False, False) - MIDDLE + sum(len(a) for a in plan(False, True))
            for m, (kind, t) in enumerate(ENDING):
                if kind == "AT":
                    act.wait_ge(s["misc_full"], ended + m + 1)
                    nc.scalar.copy(vT[:, t % 2 * P:(t % 2 + 1) * P], bank[4 + t % 2][:, 0:P]).then_inc(s["atT"], 1)

        def heads_dve(v):
            s = M

            def do(kind, b, k, m):
                if kind not in {"Q", "K", "V", "BT", "WO"}:
                    return
                x = bank[7]
                if kind in "QK":
                    hi, lo, bias, ev = (qhi, qlo, W("bqh"), "qhi") if kind == "Q" else (khi, klo, W("bkh"), "khi")
                    v.wait_ge(s[ev], b + 1)
                    nc.vector.scalar_tensor_tensor(out=lo[:, :], in0=x, scalar=bias, in1=hi[:, :], op0=ALU.add,
                                                   op1=ALU.subtract).then_inc(s["misc_empty"], 1)
                    return
                v.wait_ge(s["misc_full"], m + 1)
                if kind == "V":
                    nc.vector.tensor_tensor(vh[:, :, :, 0:DH], x.rearrange("p (t h e) -> p t h e", t=T, h=NH),
                                            R("bvh").rearrange("p (h e) -> p h e", h=NH).unsqueeze(1)
                                            .broadcast_to([P, T, NH, DH]), ALU.add).then_inc(s["misc_empty"], 1)
                else:
                    output_rows(kind, b, k, m, x)

            def output_rows(kind, b, k, m, x):
                if kind == "BT":
                    x3 = x.rearrange("p (h e) -> p h e", h=NH)
                    nc.vector.reciprocal(rch[:, k, :], x3[:, :, DH]).then_inc(s["rch"], 1)
                    v.wait_ge(s["rch"], b * T + k + 1)
                    nc.vector.tensor_tensor(ath[:, k, :].rearrange("p (h e) -> p h e", h=NH), x3[:, :, 0:DH],
                                            bcast(rch[:, k, :], DH), ALU.mult).then_inc(s["misc_empty"], 1)
                else:
                    if k == 0:
                        v.wait_ge(F["table"], 32 * b + 16)
                    nc.vector.tensor_tensor(xw[:, k, :], x[:, 0:D], xt(b * T + k, s_all), ALU.add
                                            ).then_inc(s["misc_empty"], 1)
                    v.wait_ge(s["misc_empty"], m + 1)
                    ins = nc.vector.bn_stats(stats2[:, k, :], xw[:, k, :])
                    if k == T - 1:
                        ins.then_inc(F["bn"], 1)
                        v.wait_ge(F["bn"], apart(v, b + 1))
                        for t in range(T):
                            ins = nc.vector.bn_aggr(mv2[:, t, :], stats2[:, t, :])
                        ins.then_inc(F["mv"], 1)

            def key_sums(b):
                v.wait_ge(F["dot"], b + 1)
                nc.vector.tensor_reduce(one["key"][:, b * T:(b + 1) * T], x4(b, s_all), AX, ALU.add)

            def row_max(n, g, i):
                v.wait_ge(s["s_ps"], n * 16 + i + 1)
                j, t = i // 4, i % 4
                nc.vector.tensor_reduce(mrow[:, g % 2, t, 32 * j + 24:32 * j + 25], bank[i % 2], AX, ALU.max, negate=True
                                        ).then_inc(s["nmax"], 1)

            def step(it, g, i, m0, first, last):
                n = it * G + g
                over, k = (i + LEAD) // 16, (i + LEAD) % 16
                if not (last and g + 1 + over >= G):
                    row_max(n + 1 + over, (g + 1 + over) % G, k)

            for kind, b, k in PROLOGUE:
                do(kind, b, k, 0)
            for i in range(16 + LEAD):
                row_max(i // 16, i // 16, i % 16)
            misc = Misc(do)
            steps3(v, B, lambda it, first, last: misc.sequence(it, first, last, step))
            for b in range(B - 1):
                key_sums(b)
            ended = misc_base(B, False, False) - MIDDLE + sum(len(a) for a in plan(False, True))
            n = 0
            for m, (kind, t) in enumerate(ENDING):
                if kind != "AT":
                    v.wait_ge(s["misc_full"], ended + m + 1)
                    output_rows(kind, B - 1, t, ended + n, bank[t] if kind == "BT" else bank[6 + t % 2])
                    n += 1
            v.wait_ge(s["misc_empty"], ended + n)

        def heads_pool(p):
            s = M

            def spread(b, g, m):
                p.wait_ge(s["misc_empty"], m + 1)
                nc.gpsimd.tensor_tensor(kpad[:, g, :, :], kst[:, :].unsqueeze(1).broadcast_to([P, 4, S]),
                                        c_all[:, CTOT - 4:CTOT].unsqueeze(2).broadcast_to([P, 4, S]), ALU.mult
                                        ).then_inc(s["kpad"], 1)

            def centred(b):
                nc.gpsimd.tensor_tensor(xh, x4(b),
                                        mv_all[:, ds(b * T, T), 0:1].broadcast_to([P, T, D]), ALU.subtract
                                        ).then_inc(s["xc"], 1)

            def normalised(b):
                p.wait_ge(s["xc"], b + 1)
                nc.gpsimd.tensor_tensor(xh, xh, bcast(rstd_all[:, ds(b * T, T)], D), ALU.mult
                                        ).then_inc(s["xn"], 1)

            def norm1(b):
                p.wait_ge(F["mv"], b + 1)
                nc.gpsimd.tensor_tensor(var2[:, :], mv2[:, :, 1], eps[:, 0:T], ALU.add).then_inc(F["eps"], 1)
                nc.gpsimd.tensor_tensor(xw, xw, mv2[:, :, 0:1].broadcast_to([P, T, D]), ALU.subtract)
                p.wait_ge(F["eps"], 2 * b + 1)
                nc.gpsimd.tensor_tensor(rstd2[:, :], var2[:, :], neg_half[:, 0:T], ALU.pow).then_inc(F["eps"], 1)
                p.wait_ge(F["eps"], 2 * b + 2)
                nc.gpsimd.tensor_tensor(xw, xw, bcast(rstd2[:, :], D), ALU.mult).then_inc(F["xn"], 1)
                p.wait_ge(F["xn"], b + 1)
                nc.gpsimd.tensor_tensor(xw, xw, R("g1").unsqueeze(1).broadcast_to([P, T, D]), ALU.mult
                                        ).then_inc(F["scaled"], 1)
                p.wait_ge(F["scaled"], b + 1)
                nc.gpsimd.tensor_tensor(xw, xw, R("b1").unsqueeze(1).broadcast_to([P, T, D]), ALU.add
                                        ).then_inc(F["x1"], 1)
                p.wait_ge(F["x1"], b + 1)
                nc.gpsimd.tensor_tensor(x4(b, s_all), xw, R("rw").unsqueeze(1).broadcast_to([P, T, D]), ALU.mult
                                        ).then_inc(F["dot"], 1)

            def residual(b):
                p.wait_ge(s["xn"], b + 1)
                nc.gpsimd.tensor_tensor(x4(b, s_all), xh, R("boh").unsqueeze(1).broadcast_to([P, T, D]), ALU.add
                                        ).then_inc(s["sres"], 1)

            def do(kind, b, k, m):
                if kind == "ks":
                    spread(b, k, m)

            def step(it, g, i, m0, first, last):
                if g == 0 and not last:
                    if i == 2:
                        centred(it + 1)
                    if i == 4:
                        normalised(it + 1)
                    if i == 7:
                        residual(it + 1)
                if g == G - 1 and i == 10 and not first:
                    norm1(it - 1)
            for k, (cols, b) in enumerate(((slice(0, T), 1), (slice(T, NT), B))):
                p.wait_ge(C1["mv_all"], b)
                nc.gpsimd.tensor_tensor(var_all[:, cols], mv_all[:, cols, 1], eps[:, cols], ALU.add
                                        ).then_inc(C1["eps"], 1)
                p.wait_ge(C1["eps"], B + k + 1)
                nc.gpsimd.tensor_tensor(rstd_all[:, cols], var_all[:, cols], neg_half[:, cols], ALU.pow
                                        ).then_inc(C1["rstd"], 1)
                p.wait_ge(C1["rstd"], k + 1)
                if k == 0:
                    centred(0)
                    normalised(0)
                    residual(0)
            for m, (kind, b, k) in enumerate(PROLOGUE):
                do(kind, b, k, m)
            misc = Misc(do)
            steps3(p, B, lambda it, first, last: misc.sequence(it, first, last, step))
            norm1(B - 1)

        def norm1_sp(sp, s):
            def residual(b):
                sp.dma_start(table1[ds(b * S, S), D:2 * D].rearrange("(t p) d -> p t d", p=P), x4(b)
                             ).then_inc(s["table"], 16)

            def rows(b, last):
                sp.wait_ge(s["x1"], b + 1)
                sp.dma_start(table1[ds(b * S, S), 0:D].rearrange("(t p) d -> p t d", p=P), xw
                             ).then_inc(s["table"], 16)
                if not last:
                    sp.wait_ge(s["dot"], b + 1)
                    residual(b + 1)
            sp.wait_ge(C1["x_out"], NT)
            residual(0)
            steps(sp, B, rows)

        def route1_dve(v, s):
            then = Line(v, s["line"])
            v.wait_ge(F["dot"], B)
            then(nc.vector.tensor_reduce(one["key"][:, (B - 1) * T:], x4(B - 1, s_all), AX, ALU.add))
            o = {n: a[:, :] for n, a in one.items()}
            i = {n: a[:, :] for n, a in oni.items()}
            then(nc.vector.tensor_scalar(o["key"], o["key"], R("rb"), None, ALU.add))
            then(nc.vector.tensor_copy(i["key"], o["key"]))
            then(nc.vector.tensor_copy(o["keyf"], i["key"]))
            then(nc.vector.tensor_tensor(o["gt"], o["keyf"], o["key"], ALU.is_gt))
            then(nc.vector.tensor_tensor(i["floor"], o["keyf"], o["gt"], ALU.subtract))
            then(nc.vector.tensor_scalar(i["e"], i["floor"], E1 - 1, None, ALU.bitwise_and))
            then(nc.vector.tensor_copy(o["ef"], i["e"]))
            nc.vector.tensor_tensor(oh[:, :, 0:E1], R("iota")[:, 0:E1].unsqueeze(1).broadcast_to([P, NT, E1]),
                                    bcast(o["ef"], E1), ALU.is_equal).then_inc(s["oh"], 1)
            sums = places(v, s, then, E1, o["pos"])
            then(nc.vector.tensor_scalar(toti[:, :], sums[:, NT - 1, :], float(PAIR - 1), None, ALU.add))
            then(nc.vector.tensor_scalar(toti[:, :], toti[:, :], 8, None, ALU.logical_shift_right))
            then(nc.vector.tensor_copy(pairs[:, :], toti[:, :]))
            then(nc.vector.memset(starts[:, :], 0.0))
            for e in range(E1 - 1):
                then(nc.vector.tensor_tensor(starts[:, e + 1:e + 2], starts[:, e:e + 1], pairs[:, e:e + 1], ALU.add))
            for e in range(1, E1):
                ins = nc.vector.tensor_scalar(which[:, e - 1, :], R("iota")[:, 0:U1], starts[:, e:e + 1], None, ALU.is_ge)
            then(ins)
            then(nc.vector.tensor_tensor(esum[:, :], which[:, 0, :], which[:, 1, :], ALU.add))
            nc.vector.tensor_tensor(e_of[:, :], esum[:, :], which[:, 2, :], ALU.add).then_inc(s["e_of"], 1)
            then(nc.vector.tensor_copy(i["pos"], o["pos"]))
            nc.vector.tensor_scalar(i["p"], i["pos"], P - 1, None, ALU.bitwise_and)
            then(nc.vector.tensor_scalar(i["j"], i["pos"], 7, None, ALU.logical_shift_right))
            nc.vector.tensor_copy(o["p16"], i["p"])
            then(nc.vector.tensor_copy(o["jf"], i["j"]))
            then(nc.vector.tensor_tensor(wide[3][:, :, 0:E1], oh[:, :, 0:E1],
                                         starts[:, :].unsqueeze(1).broadcast_to([P, NT, E1]), ALU.mult))
            then(nc.vector.tensor_reduce(o["base"], wide[3][:, :, 0:E1], AX, ALU.add))
            then(nc.vector.scalar_tensor_tensor(out=o["col"], in0=o["base"], scalar=2.0, in1=o["jf"],
                                                op0=ALU.mult, op1=ALU.add))
            slots(v, s, then, 2 * U1, 2)
            ids_out(v, s, then, 2 * U1, 2)

        X1 = Signals("exp1")

        block = ctx.enter_context(nc.Block())

        @block.sync
        def _(sp):
            def constants():
                sp.dma_start(r_all[:, :], r_in).then_inc(consts, 16)
                sp.dma_start(c_all[:, :], c_in).then_inc(consts, 16)
            attn_sp(sp, A, x_in, constants)
            gate_sp(sp, GL)
            expert_sp(sp, X0, pack0_in, lambda sp, u: u, U0, lambda sp: None)
            for slot in range(NX):
                sp.wait_ge(X0[f"s{slot}"], 32 * (U0 // NX))
            sp.wait_ge(GL["x2"], 48 * B)
            attn_sp(sp, C1, x2d)
            norm1_sp(sp, F)

            def expert_of(sp, u):
                return sp.value_load(e_of[0:1, ds(u, 1)], min_val=0, max_val=E1 - 1)
            sp.wait_ge(RT1["e_of"], 1)
            expert_sp(sp, X1, pack1_in, expert_of, U1, lambda sp: None)
            for slot in range(NX):
                sp.wait_ge(X1[f"s{slot}"], 32 * (U1 // NX))

        @block.scalar
        def _(act):
            act.dma_start(w_all[:, :], w_in).then_inc(consts, 16)
            act.wait_ge(consts, 48)
            one_head_act(act, A, W("bq0"), W("bv0"))
            gate_act(act, GL)
            route0_act(act, RT0)
            expert_act(act, X0, U0)
            one_head_act(act, C1, 0.0, None)
            heads_act(act)
            expert_act(act, X1, U1)

        @block.vector
        def _(v):
            nc.vector.memset(rg[:, :, :, :], 0.0).then_inc(ready, 1)
            nc.vector.memset(mrow[:, :, :, :], 0.0).then_inc(ready, 1)
            one_head_dve(v, A, W("bk0"), W("gauss"))
            gate_dve(v, GL)
            route0_dve(v, RT0)
            expert_dve0(v, X0, U0)
            one_head_dve(v, C1, None, None)
            heads_dve(v)
            route1_dve(v, RT1)
            expert_dve1(v, X1, U1)

        @block.gpsimd
        def _(p):
            nc.gpsimd.memset(neg_half[:, :], -0.5).then_inc(ready, 1)
            nc.gpsimd.memset(eps[:, :], EPS).then_inc(ready, 1)
            nc.gpsimd.memset(vh[:, :, :, DH + 1:], 0.0).then_inc(ready, 1)
            nc.gpsimd.memset(vh[:, :, :, DH:DH + 1], 1.0).then_inc(ready, 1)
            p.wait_ge(ready, READY)
            p.wait_ge(consts, 48)
            one_head_pool(p, A, R("bo0"))

            def before0(p):
                slots_pool(p, RT0, 2 * E0, 5)
                p.wait_ge(RT0["ids"], 1)
                p.wait_ge(GL["x2"], 48 * B)
            expert_pool(p, X0, table0, x2d, before0, U0, 0)
            one_head_pool(p, C1, None)
            heads_pool(p)

            def before1(p):
                slots_pool(p, RT1, 2 * U1, 2)
                p.wait_ge(RT1["ids"], 1)
                p.wait_ge(F["table"], 32 * B)
            expert_pool(p, X1, table1, out, before1, U1, 1)

        @block.tensor
        def _(pe):
            pe.wait_ge(consts, 48)
            one_head_pe(pe, A, "0", True)
            gate_pe(pe, GL)
            counts_pe(pe, RT0, E0)
            slots_pe(pe, RT0, 2 * E0, 5)
            expert_pe(pe, X0, U0)
            one_head_pe(pe, C1, "1", False)
            heads_pe(pe)
            counts_pe(pe, RT1, E1)
            slots_pe(pe, RT1, 2 * U1, 2)
            expert_pe(pe, X1, U1)


def lay_out(x):
    import numpy as np

    f = np.float32
    w = np.zeros((P, WTOT), f)

    def put(name, a):
        w[:, WCOL[name][0]:WCOL[name][1]] = a

    put("q0", x["L0_attn_Wq"].T)
    put("k0", x["L0_attn_Wk"].T)
    put("v0", x["L0_attn_Wv"].T)
    put("o0", x["L0_attn_Wo"].T)
    put("g0", x["L0_ffn_Wg"])
    for n, name in enumerate(("q1", "k1", "v1")):
        put(name, x["L1_attn_W_qkv"][n * D:(n + 1) * D, :].T)
    put("qh", x["L1_ffn_Wq"])
    put("kh", x["L1_ffn_Wk"])
    put("vh", x["L1_ffn_Wv"])
    put("oh", x["L1_ffn_Wo"])
    put("ident", np.eye(P, dtype=f))
    place = np.arange(S, dtype=f)
    put("gauss", np.exp(f(-0.5) * ((place - f(S / 2)) / f(S / 4)) ** 2) * f(float(D) ** -0.5))
    put("bq0", x["L0_attn_bq"][:, None])
    put("bk0", x["L0_attn_bk"][:, None])
    put("bv0", x["L0_attn_bv"][:, None])
    put("bqh", x["L1_ffn_bq"][:, None])
    put("bkh", x["L1_ffn_bk"][:, None])
    one24 = np.zeros((P, 1), f)
    one24[24::32] = 1
    put("one24", one24)

    r = np.zeros((P, RTOT), f)

    def row(name, a):
        r[:, RCOL[name][0]:RCOL[name][1]] = a

    row("bo0", x["L0_attn_bo"])
    row("bg0", np.tile(x["L0_ffn_bg"], T))
    row("rev0", np.arange(E0, 0, -1, dtype=f))
    row("bvh", x["L1_ffn_bv"])
    row("boh", x["L1_ffn_bo"])
    row("g1", x["L1_ffn_ln1_g"])
    row("b1", x["L1_ffn_ln1_b"])
    row("g2", x["L1_ffn_ln2_g"])
    row("b2", x["L1_ffn_ln2_b"])
    row("rw", x["L1_ffn_router_w"][:, 0])
    row("rb", x["L1_ffn_router_b"])
    row("iota", np.arange(P, dtype=f))
    row("tile", np.arange(NT, dtype=f))
    row("place", np.arange(1, P + 1, dtype=f)[:, None])

    c = np.zeros((P, CTOT), np.float16)
    c[:, 0:D] = np.eye(P)
    c[:, D:2 * D] = np.triu(np.ones((P, P)), 1)
    c[:, 2 * D:3 * D] = 1
    for j in range(4):
        c[32 * j:32 * j + 32, CTOT - 4 + j] = 1
    for g in range(G):
        for j in range(4):
            for d in range(DH):
                i = (4 * g + j) * DH + d
                for name, pieces in (("qA", (0, 1)), ("qB", (2,)), ("kA", (0, 2)), ("kB", (1,))):
                    for piece in pieces:
                        c[i, CCOL[name] + g * P + 32 * j + piece * DH + d] = 1

    def pack(e, w1, b1, w2, b2):
        out = np.zeros((e, P, WP), f)
        out[:, :, 0:H] = w1
        out[:, :, H:H + HC * D] = w2.reshape(e, HC, P, D).transpose(0, 2, 1, 3).reshape(e, P, HC * D)
        out[:, :, H + HC * D:H + HC * D + HC] = b1.reshape(e, HC, P).transpose(0, 2, 1)
        out[:, :, WP - D:] = b2[:, None, :]
        return out

    return {
        "x": np.ascontiguousarray(x["L0_attn_x"]).reshape(N, D),
        "weights": w, "rows": r, "constants": c,
        "experts0": pack(E0, x["L0_ffn_W1"], x["L0_ffn_b1"], x["L0_ffn_W2"], x["L0_ffn_b2"]),
        "experts1": pack(E1, x["L1_ffn_W1"], x["L1_ffn_b1"], x["L1_ffn_W2"], x["L1_ffn_b2"]),
    }


def program(nc, arrays):
    args = [nc.dram_tensor(name, a.shape, mybir.dt.from_np(a.dtype), kind="ExternalInput").ap()
            for name, a in arrays.items()]
    out = nc.dram_tensor("out", (N, D), F32, kind="ExternalOutput").ap()
    build(nc, *args, out)
    return nc


def kernel(**inputs):
    import numpy as np
    import concourse.bacc as bacc
    from concourse.bass_utils import run_bass_kernel_spmd

    arrays = lay_out({name: np.asarray(a) for name, a in inputs.items()})
    nc = program(bacc.Bacc("TRN2", target_bir_lowering=False, num_devices=1), arrays)
    got = run_bass_kernel_spmd(nc, [arrays], core_ids=[0])
    return got.results[0]["out"].reshape(B, S, D)
```
